# Optimizing a Trainium2 kernel written in Bass

```python
import numpy as np
import jax
import jax.numpy as jnp

def _softmax(x, axis=-1):
    return jax.nn.softmax(x, axis=axis)

def _gelu(x):
    return jax.nn.gelu(x, approximate=True)

def _silu(x):
    return jax.nn.silu(x)

def _sigmoid(x):
    return jax.nn.sigmoid(x)

def _layernorm(x, axis=-1, eps=1e-05):
    m = jnp.mean(x, axis=axis, keepdims=True)
    v = jnp.var(x, axis=axis, keepdims=True)
    return (x - m) / jnp.sqrt(v + eps)

def _scatter_add(tgt, idx, src, axis=0):
    return tgt.at[idx].add(src)

def _segment_sum(src, seg, n):
    return jax.ops.segment_sum(src, seg, n)
kernel_name = 'mk_seq_preln_d2_jaxref_r8_c5882c'

def setup_inputs(seed: int=0):
    np.random.seed(seed)
    _w = jnp.asarray

    def _L0_attn_setup():
        import jax, jax.numpy as jnp
        import numpy as np
        H = 16
        LN_EPS = 1e-05
        key = jax.random.key(seed)
        ks = jax.random.split(key, 10)
        B, N, D = (2, 256, 128)
        s = 1.0 / np.sqrt(D).astype(np.float32)
        x = jax.random.normal(ks[0], (B, N, D), jnp.float32)
        Wq = jax.random.normal(ks[1], (D, D), jnp.float32) * s
        Wk = jax.random.normal(ks[2], (D, D), jnp.float32) * s
        Wv = jax.random.normal(ks[3], (D, D), jnp.float32) * s
        Wo = jax.random.normal(ks[4], (D, D), jnp.float32) * s
        bq = jnp.zeros((D,), jnp.float32)
        bk = jnp.zeros((D,), jnp.float32)
        bv = jnp.zeros((D,), jnp.float32)
        bo = jnp.zeros((D,), jnp.float32)
        beta = jnp.ones((H,), jnp.float32)
        t = jnp.ones((H,), jnp.float32)
        ln_w = jnp.ones((D,), jnp.float32)
        ln_b = jnp.zeros((D,), jnp.float32)
        return {'x': x, 'Wq': Wq, 'bq': bq, 'Wk': Wk, 'bk': bk, 'Wv': Wv, 'bv': bv, 'Wo': Wo, 'bo': bo, 'beta': beta, 't': t, 'ln_w': ln_w, 'ln_b': ln_b}
    _L0_attn_in = _L0_attn_setup()

    def _L0_ffn_setup():
        import jax, jax.numpy as jnp
        import numpy as np
        THRESHOLD = 0.1
        key = jax.random.key(seed)
        k1, k2, k3 = jax.random.split(key, 3)
        B, S, D, E = (4, 512, 128, 8)
        inputs = jax.random.normal(k1, (B, S, D), dtype=jnp.float32)
        gate_w = jax.random.normal(k2, (D, E), dtype=jnp.float32) * 0.02
        gate_b = jnp.zeros((E,), dtype=jnp.float32)
        expert_w = jax.random.normal(k3, (E, D, D), dtype=jnp.float32) * 0.02
        expert_b = jnp.zeros((E, D), dtype=jnp.float32)
        return {'inputs': inputs, 'gate_w': gate_w, 'gate_b': gate_b, 'expert_w': expert_w, 'expert_b': expert_b}
    _L0_ffn_in = _L0_ffn_setup()

    def _L1_attn_setup():
        import jax, jax.numpy as jnp
        import numpy as np
        import math
        E = 128
        H = 64
        B = 4
        S = 256
        key = jax.random.key(seed)
        ks = jax.random.split(key, 9)
        x = jax.random.normal(ks[0], (B, S, E), dtype=jnp.float32)

        def he(k, fan_in, shape):
            return jax.random.normal(k, shape, dtype=jnp.float32) * jnp.sqrt(2.0 / fan_in)
        wq = he(ks[1], E, (E, H))
        bq = jnp.zeros((H,), jnp.float32)
        wk = he(ks[2], E, (E, H))
        bk = jnp.zeros((H,), jnp.float32)
        wv = he(ks[3], E, (E, H))
        bv = jnp.zeros((H,), jnp.float32)
        wo = he(ks[4], H, (H, E))
        bo = jnp.zeros((E,), jnp.float32)
        return {'x': x, 'wq': wq, 'bq': bq, 'wk': wk, 'bk': bk, 'wv': wv, 'bv': bv, 'wo': wo, 'bo': bo}
    _L1_attn_in = _L1_attn_setup()

    def _L1_ffn_setup():
        import jax, jax.numpy as jnp
        import numpy as np
        D_MODEL = 128
        DEPTH = 8
        M = 2 ** DEPTH
        N_INTERNAL = M - 1
        B, T = (8, 512)

        def _leaf_probs(gate):
            BT = gate.shape[0]
            lp = jnp.ones((BT, M), dtype=gate.dtype)
            for level in range(DEPTH):
                n = 2 ** level
                half = M // (2 * n)
                g = gate[:, n - 1:2 * n - 1]
                f = jnp.stack([1.0 - g, g], axis=-1)
                f = jnp.broadcast_to(f[..., None], (BT, n, 2, half))
                lp = lp * f.reshape(BT, M)
            return lp
        key = jax.random.key(seed)
        ks = jax.random.split(key, 7)
        x = jax.random.normal(ks[0], (B, T, D_MODEL), dtype=jnp.float32)
        Wq = jax.random.normal(ks[1], (D_MODEL, D_MODEL), dtype=jnp.float32) * 0.02
        routers = jax.random.normal(ks[2], (N_INTERNAL, D_MODEL), dtype=jnp.float32) * 0.02
        leaf_keys = jax.random.normal(ks[3], (M, D_MODEL), dtype=jnp.float32) * 0.02
        leaf_values = jax.random.normal(ks[4], (M, D_MODEL), dtype=jnp.float32) * 0.02
        Wout_w = jax.random.normal(ks[5], (D_MODEL, D_MODEL), dtype=jnp.float32) * 0.02
        Wout_b = jax.random.normal(ks[6], (D_MODEL,), dtype=jnp.float32) * 0.02
        return {'x': x, 'Wq': Wq, 'routers': routers, 'leaf_keys': leaf_keys, 'leaf_values': leaf_values, 'Wout_w': Wout_w, 'Wout_b': Wout_b}
    _L1_ffn_in = _L1_ffn_setup()
    _d = {'L0_attn_x': _L0_attn_in['x'], 'L0_attn_Wq': _L0_attn_in['Wq'], 'L0_attn_bq': _L0_attn_in['bq'], 'L0_attn_Wk': _L0_attn_in['Wk'], 'L0_attn_bk': _L0_attn_in['bk'], 'L0_attn_Wv': _L0_attn_in['Wv'], 'L0_attn_bv': _L0_attn_in['bv'], 'L0_attn_Wo': _L0_attn_in['Wo'], 'L0_attn_bo': _L0_attn_in['bo'], 'L0_attn_beta': _L0_attn_in['beta'], 'L0_attn_t': _L0_attn_in['t'], 'L0_attn_ln_w': _L0_attn_in['ln_w'], 'L0_attn_ln_b': _L0_attn_in['ln_b'], 'L0_ffn_gate_w': _L0_ffn_in['gate_w'], 'L0_ffn_gate_b': _L0_ffn_in['gate_b'], 'L0_ffn_expert_w': _L0_ffn_in['expert_w'], 'L0_ffn_expert_b': _L0_ffn_in['expert_b'], 'L1_attn_wq': _L1_attn_in['wq'], 'L1_attn_bq': _L1_attn_in['bq'], 'L1_attn_wk': _L1_attn_in['wk'], 'L1_attn_bk': _L1_attn_in['bk'], 'L1_attn_wv': _L1_attn_in['wv'], 'L1_attn_bv': _L1_attn_in['bv'], 'L1_attn_wo': _L1_attn_in['wo'], 'L1_attn_bo': _L1_attn_in['bo'], 'L1_ffn_Wq': _L1_ffn_in['Wq'], 'L1_ffn_routers': _L1_ffn_in['routers'], 'L1_ffn_leaf_keys': _L1_ffn_in['leaf_keys'], 'L1_ffn_leaf_values': _L1_ffn_in['leaf_values'], 'L1_ffn_Wout_w': _L1_ffn_in['Wout_w'], 'L1_ffn_Wout_b': _L1_ffn_in['Wout_b']}
    _x0 = _d['L0_attn_x']
    _d['L0_attn_x'] = jax.random.normal(jax.random.fold_in(jax.random.key(seed), 1), (4, 1024, 128), dtype=_x0.dtype)
    del _x0
    return _d

def reference(L0_attn_x, L0_attn_Wq, L0_attn_bq, L0_attn_Wk, L0_attn_bk, L0_attn_Wv, L0_attn_bv, L0_attn_Wo, L0_attn_bo, L0_attn_beta, L0_attn_t, L0_attn_ln_w, L0_attn_ln_b, L0_ffn_gate_w, L0_ffn_gate_b, L0_ffn_expert_w, L0_ffn_expert_b, L1_attn_wq, L1_attn_bq, L1_attn_wk, L1_attn_bk, L1_attn_wv, L1_attn_bv, L1_attn_wo, L1_attn_bo, L1_ffn_Wq, L1_ffn_routers, L1_ffn_leaf_keys, L1_ffn_leaf_values, L1_ffn_Wout_w, L1_ffn_Wout_b):

    def _L0_attn_ref(x, Wq, bq, Wk, bk, Wv, bv, Wo, bo, beta, t, ln_w, ln_b):
        import jax, jax.numpy as jnp
        import numpy as np
        H = 16
        LN_EPS = 1e-05
        B, N, D = x.shape
        dh = D // H

        def proj(W, b):
            return (x @ W.T + b).reshape(B, N, H, dh).transpose(0, 2, 1, 3)
        Q, K, V = (proj(Wq, bq), proj(Wk, bk), proj(Wv, bv))
        S = jnp.einsum('bhnd,bhmd->bhnm', Q, K) / dh ** 0.5
        W_tau = jax.nn.softmax(S, axis=-1)
        b_ = beta.reshape(1, H, 1, 1)
        t_ = t.reshape(1, H, 1, 1)
        W_sigma = 1.0 / ((1.0 + jnp.abs(S) / b_) ** 2 + t_ ** 2)
        W_sigma = W_sigma / W_sigma.sum(axis=-1, keepdims=True)
        tau = jnp.einsum('bhnm,bhmd->bhnd', W_tau, V).transpose(0, 2, 1, 3).reshape(B, N, D)
        sigma = jnp.einsum('bhnm,bhmd->bhnd', W_sigma, V).transpose(0, 2, 1, 3).reshape(B, N, D)
        f = 0.5 * tau + 0.5 * sigma
        y = f @ Wo.T + bo
        mu = y.mean(axis=-1, keepdims=True)
        var = jnp.mean((y - mu) ** 2, axis=-1, keepdims=True)
        out = x + ln_w * (y - mu) * jax.lax.rsqrt(var + LN_EPS) + ln_b
        return out

    def _L0_ffn_ref(inputs, gate_w, gate_b, expert_w, expert_b):
        import jax, jax.numpy as jnp
        import numpy as np
        THRESHOLD = 0.1
        d = inputs.shape[-1]
        x = inputs.reshape(-1, d)
        gate_logits = jax.nn.softmax(x @ gate_w + gate_b, axis=-1)
        selected = (gate_logits >= THRESHOLD).astype(x.dtype)
        weights = gate_logits * selected
        wsum = jnp.sum(weights, axis=-1, keepdims=True)
        weights = weights / jnp.where(wsum == 0, jnp.ones_like(wsum), wsum)
        E = expert_w.shape[0]
        out = jnp.zeros((x.shape[0], expert_w.shape[-1]), dtype=x.dtype)
        for e in range(E):
            out = out + weights[:, e:e + 1] * (x @ expert_w[e] + expert_b[e])
        return out.reshape(*inputs.shape[:-1], out.shape[-1])

    def _L1_attn_ref(x, wq, bq, wk, bk, wv, bv, wo, bo):
        import jax, jax.numpy as jnp
        import numpy as np
        import math
        E = 128
        H = 64
        B = 4
        S = 256
        q = x @ wq + bq
        k = x @ wk + bk
        v = x @ wv + bv
        scale = 1.0 / math.sqrt(H)
        w = jnp.einsum('bqh,bkh->bqk', q, k) * scale
        seq = x.shape[1]
        mask = jnp.triu(jnp.ones((1, seq, seq), dtype=w.dtype), 1) * -100000000000.0
        w = w + mask
        w = jax.nn.softmax(w, axis=-1)
        z = jnp.einsum('bqk,bkh->bqh', w, v)
        z = z @ wo + bo
        return z

    def _L1_ffn_ref(x, Wq, routers, leaf_keys, leaf_values, Wout_w, Wout_b):
        import jax, jax.numpy as jnp
        import numpy as np
        D_MODEL = 128
        DEPTH = 8
        M = 2 ** DEPTH
        N_INTERNAL = M - 1
        B, T = (8, 512)

        def _leaf_probs(gate):
            BT = gate.shape[0]
            lp = jnp.ones((BT, M), dtype=gate.dtype)
            for level in range(DEPTH):
                n = 2 ** level
                half = M // (2 * n)
                g = gate[:, n - 1:2 * n - 1]
                f = jnp.stack([1.0 - g, g], axis=-1)
                f = jnp.broadcast_to(f[..., None], (BT, n, 2, half))
                lp = lp * f.reshape(BT, M)
            return lp
        Bv, Tv, d = x.shape
        q = jnp.einsum('btd,ed->bte', x, Wq)
        q_flat = q.reshape(Bv * Tv, d)
        gate = jax.nn.sigmoid(q_flat @ routers.T)
        leaf_prob = _leaf_probs(gate)
        ret = (leaf_prob @ leaf_values).reshape(Bv, Tv, d)
        return jnp.einsum('btd,ed->bte', ret, Wout_w) + Wout_b
    x = L0_attn_x
    x = x + _L0_attn_ref(_layernorm(x, axis=-1), L0_attn_Wq, L0_attn_bq, L0_attn_Wk, L0_attn_bk, L0_attn_Wv, L0_attn_bv, L0_attn_Wo, L0_attn_bo, L0_attn_beta, L0_attn_t, L0_attn_ln_w, L0_attn_ln_b)
    x = x + _L0_ffn_ref(_layernorm(x, axis=-1), L0_ffn_gate_w, L0_ffn_gate_b, L0_ffn_expert_w, L0_ffn_expert_b)
    x = x + _L1_attn_ref(_layernorm(x, axis=-1), L1_attn_wq, L1_attn_bq, L1_attn_wk, L1_attn_bk, L1_attn_wv, L1_attn_bv, L1_attn_wo, L1_attn_bo)
    x = x + _L1_ffn_ref(_layernorm(x, axis=-1), L1_ffn_Wq, L1_ffn_routers, L1_ffn_leaf_keys, L1_ffn_leaf_values, L1_ffn_Wout_w, L1_ffn_Wout_b)
    return x

_drawn_inputs = setup_inputs


def setup_inputs(seed=0):
    import zlib

    import numpy as np

    out = dict(_drawn_inputs(seed))
    spreads = {'L0_attn_bq': (0.0, 0.492),
     'L0_attn_bk': (0.0, 0.8),
     'L0_attn_bv': (0.0, 0.1),
     'L0_attn_bo': (0.0, 0.1),
     'L0_attn_beta': (1.0, 0.6),
     'L0_attn_t': (1.0, 0.6),
     'L0_attn_ln_w': (1.0, 0.2),
     'L0_attn_ln_b': (0.0, 0.1),
     'L0_ffn_gate_b': (0.0, 0.573),
     'L0_ffn_expert_b': (0.0, 0.386),
     'L1_attn_bq': (0.0, 0.449),
     'L1_attn_bk': (0.0, 0.8),
     'L1_attn_bv': (0.0, 0.1),
     'L1_attn_bo': (0.0, 0.1)}
    factors = {'L1_ffn_Wq': 8.0,
     'L1_ffn_routers': 8.0,
     'L1_ffn_leaf_values': 8.0,
     'L1_ffn_Wout_w': 8.0,
     'L1_ffn_Wout_b': 6.573}
    for name, (base, spread) in spreads.items():
        noise = np.random.default_rng([zlib.crc32(name.encode()), seed]).standard_normal(out[name].shape)
        drawn = base * np.exp(spread * noise) if base else spread * noise
        out[name] = jnp.asarray(drawn.astype(out[name].dtype))
    for name, factor in factors.items():
        out[name] = (out[name] * factor).astype(out[name].dtype)
    return out
```

```python
from contextlib import ExitStack

import concourse.bass as bass
from concourse import mybir

F32 = mybir.dt.float32
BF16 = mybir.dt.bfloat16
I32 = mybir.dt.int32
ALU = mybir.AluOpType
ACT = mybir.ActivationFunctionType
AX = mybir.AxisListType

P = 128
B, N, D = 4, 1024, 128
TB = N // P
NT = B * TB
H, DH = 16, 8
NH = B * H
HALF = 512
EPS = 1e-5
SIGN_OFF = 0x7FFFFFFF

E = 8
THRESHOLD = 0.1
DA = 64
DEPTH = 8
LEAVES = 2 ** DEPTH
NODES = LEAVES - 1
MASKED = -100000000000.0

PARTS = 3
TERMS = PARTS * PARTS * DH
MROW = 96
SIGMA_ROWS = 96
SLOTS = 3
TAU_RING = 8
MAG_RING = 3
VEC_COLS = 224
CHUNK = 2
SIG_RING = 8
CHUNK_LAG = 3
PV_LAG = 7
MAX_UNITS = [[0, 1], [2], [3], [4, 5], [6], [7], [], []]
MT_STEP, FT_STEP = 6, 7
COLS = DH + 1
PAIRS = [(kind, half) for kind in range(2) for half in range(2)]


def build(nc, a, out):
    with ExitStack() as ctx:
        def sb(name, shape, dt=F32):
            return ctx.enter_context(nc.sbuf_tensor(name, shape, dt))

        def dram(name, shape, dt):
            return nc.dram_tensor(name, shape, dt, kind="Internal").ap()

        w = {}
        w["ident"] = sb("ident", [P, P])
        w["x"] = sb("x_res", [P, NT, D])
        w["wt"] = sb("wt", [P, 4, D])
        w["bq"] = sb("bq_col", [P, 1])
        w["bk"] = sb("bk_col", [P, 1])
        w["bv"] = sb("bv_rows", [P, D])
        w["eps"] = sb("eps", [P, 1])
        w["shape"] = sb("kernel_shape", [P, NH, 2])
        w["v"] = sb("v_heads", [P, NH, TB, COLS])
        w["f"] = sb("f_heads", [P, NH, TB, DH])
        w["bo"] = sb("bo_rows", [P, D])
        w["ln_w"] = sb("ln_w_rows", [P, D])
        w["ln_b"] = sb("ln_b_rows", [P, D])
        w["gate"] = sb("gate", [P, E])
        w["gate_b"] = sb("gate_b_rows", [P, E])
        w["experts"] = sb("experts", [P, E, D])
        w["expert_b"] = sb("expert_b", [E, D])
        w["qkv1"] = sb("qkv1", [P, 3, DA])
        w["b1"] = sb("b1_cols", [DA, 2])
        w["bv1"] = sb("bv1_rows", [P, DA])
        w["wo1"] = sb("wo1", [DA, D])
        w["bo1"] = sb("bo1_rows", [P, D])
        w["causal"] = sb("causal", [P, P])
        w["router"] = sb("router", [P, NODES])
        w["leaf"] = sb("leaf", [P, 2, D])
        w["bout"] = sb("bout_rows", [P, D])
        w["q_parts"] = dram("q_parts", [NH, PARTS, DH, N], BF16)
        w["k_parts"] = dram("k_parts", [NH, PARTS, DH, N], BF16)

        for engine in ("dve", "pool", "sp", "pe"):
            w[f"{engine}_passed"] = ctx.enter_context(nc.semaphore(f"{engine}_passed"))

        load_weights(nc, a, w)
        project_heads(nc, a, w)
        attend_heads(nc, a, w)
        mix_experts(nc, w)
        attend_causal(nc, w)
        descend_tree(nc, w, out)


def alone(eng, passed):
    eng.sem_inc(passed, 1)


def load_weights(nc, a, w):
    with ExitStack() as ctx:
        raw = ctx.enter_context(nc.sbuf_tensor("raw_w", [P, 4, D], F32))
        tree = ctx.enter_context(nc.sbuf_tensor("raw_tree", [P, 6, D], F32))
        tree_t = ctx.enter_context(nc.sbuf_tensor("tree_t", [P, 5, D], F32))
        turned_tree = ctx.enter_context(nc.psum_tensor("turned_tree", [P, 2, 4, D], F32))
        made = ctx.enter_context(nc.psum_tensor("made", [P, 2, 512], F32))
        tree_ready = ctx.enter_context(nc.semaphore("tree_ready"))
        made_ready = ctx.enter_context(nc.semaphore("made_ready"))
        loaded2 = ctx.enter_context(nc.semaphore("loaded2"))
        bt = ctx.enter_context(nc.sbuf_tensor("beta_t", [P, 4, H], F32))
        turned = ctx.enter_context(nc.psum_tensor("turned_w", [P, 4, D], F32))
        loaded = ctx.enter_context(nc.semaphore("loaded"))
        ident_ready = ctx.enter_context(nc.semaphore("ident_ready"))
        turned_ready = ctx.enter_context(nc.semaphore("turned_ready"))
        shape_step = ctx.enter_context(nc.semaphore("shape_step"))
        const_ready = ctx.enter_context(nc.semaphore("const_ready"))
        n_loads = 9 + B
        n_loads2 = 22
        block = ctx.enter_context(nc.Block())

        @block.sync
        def _(sp):
            for i, name in enumerate(("Wq", "Wk", "Wv", "Wo")):
                sp.dma_start(raw[:, i, :], a[f"L0_attn_{name}"]).then_inc(loaded, 16)
            for key in ("bq", "bk"):
                sp.dma_start(w[key][:, :], a[f"L0_attn_{key}"].rearrange("(p o) -> p o", o=1)).then_inc(loaded, 16)
            sp.dma_start(w["bv"][:, :], a["L0_attn_bv"].partition_broadcast(P)).then_inc(loaded, 16)
            sp.dma_start(bt[:, 0, :], a["L0_attn_beta"].partition_broadcast(P)).then_inc(loaded, 16)
            sp.dma_start(bt[:, 1, :], a["L0_attn_t"].partition_broadcast(P)).then_inc(loaded, 16)
            for b in range(B):
                sp.dma_start(w["x"][:, b * TB:(b + 1) * TB, :],
                             a["L0_attn_x"][b].rearrange("(t p) d -> p t d", p=P)).then_inc(loaded, 16)

        @block.scalar
        def _(act):
            def rows_of(name):
                return a[name].partition_broadcast(P)

            def column(name):
                return a[name].rearrange("(p o) -> p o", o=1)

            routers, leaves = a["L1_ffn_routers"], a["L1_ffn_leaf_values"]
            for dst, src in (
                (tree[:, 0, :], routers[0:P, :]), (tree[0:NODES - P, 1, :], routers[P:NODES, :]),
                (tree[:, 2, :], leaves[0:P, :]), (tree[:, 3, :], leaves[P:LEAVES, :]),
                (tree[:, 4, :], a["L1_ffn_Wout_w"]), (tree[:, 5, :], a["L1_ffn_Wq"]),
                (w["bo"][:, :], rows_of("L0_attn_bo")), (w["ln_w"][:, :], rows_of("L0_attn_ln_w")),
                (w["ln_b"][:, :], rows_of("L0_attn_ln_b")), (w["gate"][:, :], a["L0_ffn_gate_w"]),
                (w["gate_b"][:, :], rows_of("L0_ffn_gate_b")),
                (w["experts"][:, :, :], a["L0_ffn_expert_w"].rearrange("e i o -> i e o")),
                (w["expert_b"][:, :], a["L0_ffn_expert_b"]),
                (w["qkv1"][:, 0, :], a["L1_attn_wq"]), (w["qkv1"][:, 1, :], a["L1_attn_wk"]),
                (w["qkv1"][:, 2, :], a["L1_attn_wv"]),
                (w["b1"][:, 0:1], column("L1_attn_bq")), (w["b1"][:, 1:2], column("L1_attn_bk")),
                (w["bv1"][:, :], rows_of("L1_attn_bv")), (w["wo1"][:, :], a["L1_attn_wo"]),
                (w["bo1"][:, :], rows_of("L1_attn_bo")), (w["bout"][:, :], rows_of("L1_ffn_Wout_b")),
            ):
                act.dma_start(dst, src).then_inc(loaded2, 16)

        @block.gpsimd
        def _(pool):
            pool.memset(w["ident"][:, :], 0.0).then_inc(const_ready, 1)
            pool.wait_ge(const_ready, 1)
            pool.affine_select(out=w["ident"][:, :], in_=w["ident"][:, :], compare_op=ALU.not_equal, fill=1.0,
                               base=0, pattern=[[-1, P]], channel_multiplier=1).then_inc(ident_ready, 1)
            pool.memset(w["eps"][:, :], EPS)
            pool.memset(w["causal"][:, :], 0.0).then_inc(const_ready, 1)
            pool.wait_ge(const_ready, 2)
            pool.affine_select(out=w["causal"][:, :], in_=w["causal"][:, :], compare_op=ALU.is_ge,
                               fill=MASKED * float(DA) ** 0.5, base=0, pattern=[[-1, P]], channel_multiplier=1)\
                .then_inc(const_ready, 1)
            pool.memset(w["v"][:, :, :, DH:COLS], 2.0)

        @block.tensor
        def _(pe):
            pe.wait_ge(ident_ready, 1)
            pe.wait_ge(loaded, 16 * n_loads)
            for i in range(4):
                pe.transpose(turned[:, i, :], raw[:, i, :], w["ident"][:, :]).then_inc(turned_ready, 1)
            pe.wait_ge(loaded2, 16 * n_loads2)
            for i in range(5):
                rows = NODES - P if i == 1 else P
                pe.transpose(turned_tree[:, i // 4, i % 4, 0:rows], tree[0:rows, i, :], w["ident"][0:rows, 0:rows])\
                  .then_inc(turned_ready, 1)
            pe.wait_ge(tree_ready, 2)
            pe.matmul(made[:, 0, 0:NODES], tree[:, 5, :],
                      tree_t[:, 0:2, :].rearrange("p i d -> p (i d)")[:, 0:NODES], start=True, stop=True)\
              .then_inc(made_ready, 1)
            for i in range(2):
                pe.matmul(made[:, 1, i * D:(i + 1) * D], tree_t[:, 2 + i, :], tree_t[:, 4, :], start=True, stop=True)\
                  .then_inc(made_ready, 1)

        @block.vector
        def _(dve):
            dve.wait_ge(loaded, 16 * n_loads)
            dve.tensor_scalar(bt[:, 0, :], bt[:, 0, :], float(DH) ** 0.5, None, ALU.mult).then_inc(shape_step, 1)
            dve.wait_ge(shape_step, 1)
            dve.tensor_tensor(bt[:, 1, :], bt[:, 0, :], bt[:, 1, :], ALU.mult).then_inc(shape_step, 1)
            dve.wait_ge(shape_step, 2)
            dve.tensor_tensor(bt[:, 2, :], bt[:, 0, :], bt[:, 0, :], ALU.mult).then_inc(shape_step, 1)
            dve.tensor_tensor(bt[:, 3, :], bt[:, 1, :], bt[:, 1, :], ALU.mult).then_inc(shape_step, 1)
            dve.wait_ge(shape_step, 4)
            for b in range(B):
                dve.tensor_scalar(w["shape"][:, b * H:(b + 1) * H, 0], bt[:, 0, :], 2.0, None, ALU.mult)
                dve.tensor_tensor(w["shape"][:, b * H:(b + 1) * H, 1], bt[:, 2, :], bt[:, 3, :], ALU.add)
            dve.wait_ge(turned_ready, 4)
            dve.tensor_copy(w["wt"][:, :, :], turned[:, :, :])
            dve.wait_ge(turned_ready, 9)
            dve.tensor_copy(tree_t[:, 0:4, :].rearrange("p i d -> p (i d)")[:, 0:NODES],
                            turned_tree[:, 0, :, :].rearrange("p i d -> p (i d)")[:, 0:NODES])
            dve.tensor_copy(tree_t[:, 2:4, :], turned_tree[:, 0, 2:4, :]).then_inc(tree_ready, 1)
            dve.tensor_copy(tree_t[:, 4, :], turned_tree[:, 1, 0, :]).then_inc(tree_ready, 1)
            dve.wait_ge(made_ready, 3)
            dve.tensor_copy(w["router"][:, :], made[:, 0, 0:NODES])
            dve.tensor_copy(w["leaf"][:, :, :].rearrange("p i d -> p (i d)"), made[:, 1, 0:2 * D])


def project_heads(nc, a, w):
    with ExitStack() as ctx:
        def sb(name, shape, dt=F32):
            return ctx.enter_context(nc.sbuf_tensor(name, shape, dt))

        def sem(name):
            return ctx.enter_context(nc.semaphore(name))

        stats = sb("stats", [P, TB, 6])
        mv = sb("mean_var", [P, TB, 2])
        rstd = sb("rstd", [P, TB])
        lnv = sb("ln_var", [P, TB])
        h = sb("h", [P, TB, D])
        ht = sb("h_turned", [P, N])
        qk = sb("qk", [P, 2, N])
        rest = sb("rest", [P, 2, N])
        parts = sb("parts", [P, 2, PARTS, N], BF16)
        pt = ctx.enter_context(nc.psum_tensor("ps_turn", [P, 2, HALF], F32))
        pq = ctx.enter_context(nc.psum_tensor("ps_qk", [P, 2, 2, HALF], F32))
        pv = ctx.enter_context(nc.psum_tensor("ps_v", [P, 2, HALF], F32))
        stats_ready = sem("stats_ready")
        mv_ready = sem("mv_ready")
        ln_ready = sem("ln_ready")
        rstd_ready = sem("rstd_ready")
        h_ready = sem("h_ready")
        turned = sem("turned")
        ht_ready = sem("ht_ready")
        proj_ready = sem("proj_ready")
        qk_ready = sem("qk_ready")
        split_step = sem("split_step")
        v_ready = sem("v_ready")
        v_done = sem("v_done")
        stored = sem("stored")
        x_done = sem("x_done")
        n_stores = 2 * PARTS
        block = ctx.enter_context(nc.Block())

        @block.vector
        def _(dve):
            with dve.Fori(0, B) as b:
                for t in range(TB):
                    dve.bn_stats(stats[:, t, :], w["x"][:, bass.ds(b * TB + t, 1), :].rearrange("p o d -> p (o d)"))\
                       .then_inc(stats_ready, 1)
                dve.wait_ge(ln_ready, b)
                dve.wait_ge(h_ready, b * TB)
                dve.wait_ge(stats_ready, b * TB + TB)
                alone(dve, w["dve_passed"])
                for t in range(TB):
                    dve.bn_aggr(mv[:, t, :], stats[:, t, :]).then_inc(mv_ready, 1)
                dve.wait_ge(mv_ready, b * TB + TB)
                dve.wait_ge(rstd_ready, b + 1)
                dve.wait_ge(turned, b * TB)
                dve.wait_ge(x_done, b)
                for t in range(TB):
                    dve.tensor_scalar(h[:, t, :], w["x"][:, bass.ds(b * TB + t, 1), :].rearrange("p o d -> p (o d)"),
                                      mv[:, t, 0:1], rstd[:, t:t + 1], ALU.subtract, ALU.mult).then_inc(h_ready, 1)
                for g in range(2):
                    dve.wait_ge(v_ready, b * TB + (g + 1) * 4)
                    dst = w["v"][:, bass.ds(b * H, H), 4 * g:4 * g + 4, 0:DH].rearrange("p h t d -> p t h d")
                    dve.tensor_tensor(dst, pv[:, g, :].rearrange("p (t h d) -> p t h d", t=4, h=H),
                                      w["bv"][:, :].rearrange("p (h d) -> p h d", h=H).unsqueeze(1)
                                      .to_broadcast([P, 4, H, DH]), ALU.add).then_inc(v_done, 1)
                dve.wait_ge(stored, b * (16 * n_stores))
                for s in range(2):
                    dve.wait_ge(qk_ready, b * 4 + (2 * s + 2))
                    dve.tensor_copy(parts[:, s, 0, :], qk[:, s, :]).then_inc(split_step, 1)
                    dve.wait_ge(split_step, b * 10 + (5 * s + 1))
                    dve.tensor_tensor(rest[:, s, :], qk[:, s, :], parts[:, s, 0, :], ALU.subtract).then_inc(split_step, 1)
                    dve.wait_ge(split_step, b * 10 + (5 * s + 2))
                    dve.tensor_copy(parts[:, s, 1, :], rest[:, s, :]).then_inc(split_step, 1)
                    dve.wait_ge(split_step, b * 10 + (5 * s + 3))
                    dve.tensor_tensor(parts[:, s, 2, :], rest[:, s, :], parts[:, s, 1, :], ALU.subtract)\
                       .then_inc(split_step, 2)

        @block.scalar
        def _(act):
            act.preload_act_table_set("natural_log_exp_and_others")
            with act.Fori(0, B) as b:
                act.wait_ge(mv_ready, b * TB + TB)
                act.activation(lnv[:, :], mv[:, :, 1], ACT.Ln, bias=w["eps"][:, 0:1]).then_inc(ln_ready, 1)
                act.wait_ge(ln_ready, b + 1)
                act.wait_ge(h_ready, b * TB)
                act.activation(rstd[:, :], lnv[:, :], ACT.Exp, scale=-0.5).then_inc(rstd_ready, 1)
                act.wait_ge(proj_ready, b * 4)
                act.wait_ge(v_ready, b * TB)
                for g in range(2):
                    act.wait_ge(turned, b * TB + 4 * (g + 1))
                    act.activation(ht[:, g * HALF:(g + 1) * HALF], pt[:, g, :], ACT.Copy).then_inc(ht_ready, 1)
                act.wait_ge(split_step, b * 10)
                for s in range(2):
                    for g in range(2):
                        act.wait_ge(proj_ready, b * 4 + (2 * s + g + 1))
                        act.activation(qk[:, s, g * HALF:(g + 1) * HALF], pq[:, s, g, :], ACT.Identity,
                                       bias=w["bq" if s == 0 else "bk"][:, 0:1]).then_inc(qk_ready, 1)

        @block.tensor
        def _(pe):
            with pe.Fori(0, B) as b:
                pe.wait_ge(ht_ready, b * 2)
                for t in range(TB):
                    pe.wait_ge(h_ready, b * TB + (t + 1))
                    pe.transpose(pt[:, t // 4, (t % 4) * P:(t % 4 + 1) * P], h[:, t, :], w["ident"][:, :])\
                      .then_inc(turned, 1)
                pe.wait_ge(ht_ready, b * 2 + 2)
                pe.wait_ge(qk_ready, b * 4)
                for s in range(2):
                    for g in range(2):
                        pe.matmul(pq[:, s, g, :], w["wt"][:, s, :], ht[:, g * HALF:(g + 1) * HALF],
                                  start=True, stop=True).then_inc(proj_ready, 1)
                pe.wait_ge(v_done, b * 2)
                for t in range(TB):
                    pe.matmul(pv[:, t // 4, (t % 4) * P:(t % 4 + 1) * P], ht[:, t * P:(t + 1) * P], w["wt"][:, 2, :],
                              start=True, stop=True).then_inc(v_ready, 1)

        @block.gpsimd
        def _(pool):
            with pool.Fori(0, B) as b:
                pool.wait_ge(h_ready, b * TB + TB)
                xs = w["x"][:, bass.ds(b * TB, TB), :].rearrange("p t d -> p (t d)")
                pool.tensor_tensor(xs, xs, h[:, :, :].rearrange("p t d -> p (t d)"), ALU.add).then_inc(x_done, 1)

        @block.sync
        def _(sp):
            with sp.Fori(0, B) as b:
                for s, scratch in enumerate((w["q_parts"], w["k_parts"])):
                    sp.wait_ge(split_step, b * 10 + 5 * (s + 1))
                    for i in range(PARTS):
                        sp.dma_start(scratch[bass.ds(b * H, H), i], parts[:, s, i, :]).then_inc(stored, 16)
            sp.wait_ge(stored, 16 * n_stores * B)


def attend_heads(nc, a, w):
    with ExitStack() as ctx:
        def sb(name, shape, dt=F32):
            return ctx.enter_context(nc.sbuf_tensor(name, shape, dt))

        def ps(name, shape, dt=F32):
            return ctx.enter_context(nc.psum_tensor(name, shape, dt))

        def sem(name):
            return ctx.enter_context(nc.semaphore(name))

        qop = sb("q_operand", [P, SLOTS, N], BF16)
        kop = sb("k_operand", [P, SLOTS, N], BF16)
        vop = sb("v_operand", [P, SLOTS, TB, COLS])
        shape = sb("shape_operand", [P, SLOTS, 2])
        tau = sb("tau_weights", [P, TAU_RING, N])
        mag = sb("magnitudes", [P, MAG_RING, N])
        grown = sb("grown", [P, N - VEC_COLS])
        sig = sb("sigma_weights", [P, SIG_RING, N])
        halfmax = sb("half_max", [P, TB, 2])
        rowmax = sb("row_max", [P, TB])
        mrow = sb("max_rows", [TB, 2, P], BF16)
        sums = sb("sums", [P, HALF])
        rden = sb("rden", [P, 4, 4])
        scaled = sb("scaled", [P, 4, 4, DH])

        ps_tau = ps("ps_tau", [P, 2, 2, HALF])
        ps_sig = ps("ps_sig", [P, 2, HALF])
        ps_misc = ps("ps_misc", [P, HALF])
        ps_acc = ps("ps_acc", [P, HALF])

        idle_rows_ready = sem("idle_rows_ready")
        ops_loaded = [sem(f"ops_loaded{slot}") for slot in range(SLOTS)]
        head_copied = sem("head_copied")
        tau_ready, tau_done = sem("tau_scores_ready"), sem("tau_weights_ready")
        sig_ready, mag_ready = sem("sig_scores_ready"), sem("magnitudes_ready")
        grown_ready = sem("grown_ready")
        sqv_ready, sqp_ready = sem("vector_squares_ready"), sem("pool_squares_ready")
        ln_done, sig_done = sem("logs_ready"), sem("sigma_weights_ready")
        misc_ready, misc_done = sem("misc_ready"), sem("misc_read")
        max_ready, mrow_ready, mrow_loaded = sem("max_ready"), sem("mrow_ready"), sem("mrow_loaded")
        pv_done, sums_ready = sem("pv_done"), sem("sums_ready")
        norm_step = sem("norm_step")

        MAXIMA = 2 * TB + 1
        LOADED = 16 * (PARTS + 1)

        def misc_before(n, first):
            return MAXIMA if first else n * (MAXIMA + 1) + (MAXIMA - 1)

        def wait(eng, signal, value):
            if not isinstance(value, int) or value > 0:
                eng.wait_ge(signal, value)

        def heads(eng, head):
            for n in (0, 1):
                head(n, n % SLOTS, n // SLOTS, n == 0, False)
            with eng.Fori(0, (NH - 4) // SLOTS) as i:
                for k in range(2, 2 + SLOTS):
                    head(i * SLOTS + k, k % SLOTS, i + k // SLOTS, False, False)
            for n in (NH - 2, NH - 1):
                head(n, n % SLOTS, n // SLOTS, False, n == NH - 1)

        block = ctx.enter_context(nc.Block())

        @block.sync
        def _(sp):
            def load(n, slot):
                for i in range(PARTS):
                    sp.dma_start(qop[i * PARTS * DH:(i + 1) * PARTS * DH, slot, :],
                                 w["q_parts"][bass.ds(n, 1), i].to_broadcast([PARTS, DH, N]))\
                      .then_inc(ops_loaded[slot], 16)
                sp.dma_start(kop[0:TERMS, slot, :],
                             w["k_parts"][bass.ds(n, 1)].rearrange("o j d t -> (o j d) t").unsqueeze(0)
                             .to_broadcast([PARTS, PARTS * DH, N])).then_inc(ops_loaded[slot], 16)

            def rows(n, slot, misc_uses):
                sp.wait_ge(mrow_ready, n + 1)
                sp.dma_start(qop[MROW:MROW + 1, slot, :], mrow[:, 0, :]).then_inc(mrow_loaded, 16)
                sp.wait_ge(misc_done, misc_uses)
                sp.dma_start(qop[MROW + 1:MROW + 2, slot, :], mrow[:, 1, :]).then_inc(mrow_loaded, 16)

            def head(n, slot, turn, first, last):
                if isinstance(n, int) and n + 2 >= NH:
                    pass
                else:
                    wait(sp, sig_ready, n * (2 * TB))
                    alone(sp, w["sp_passed"])
                    wait(sp, tau_ready, n * TB)
                    alone(sp, w["sp_passed"])
                    load(n + 2, (slot + 2) % SLOTS)
                if not last:
                    rows(n + 1, (slot + 1) % SLOTS, misc_before(n, first) + MAXIMA)

            sp.wait_ge(idle_rows_ready, 3)
            load(0, 0)
            load(1, 1)
            rows(0, 0, MAXIMA)
            heads(sp, head)

        @block.tensor
        def _(pe):
            def score_halves(n, slot, u, before):
                for half in range(2):
                    wait(pe, misc_done, before + half)
                    pe.matmul(ps_misc[:, :], qop[0:SIGMA_ROWS, slot, u * P:(u + 1) * P],
                              kop[0:SIGMA_ROWS, slot, half * HALF:(half + 1) * HALF],
                              start=True, stop=True).then_inc(misc_ready, 1)

            def turn_maxima(n, before):
                pe.wait_ge(max_ready, n + 1)
                wait(pe, misc_done, before)
                pe.transpose(ps_misc[0:TB, 0:P], rowmax[:, :], w["ident"][:, :]).then_inc(misc_ready, 1)

            def turn_sums(n, before):
                pe.wait_ge(sums_ready, n + 1)
                wait(pe, misc_done, before)
                for t in range(4):
                    mm = pe.transpose(ps_misc[:, t * P:(t + 1) * P], sums[:, t * P:(t + 1) * P], w["ident"][:, :])
                mm.then_inc(misc_ready, 1)

            def weigh(n, slot, j, first):
                g = n * TB + j
                if j == 0:
                    wait(pe, sums_ready, n)
                    pe.wait_ge(head_copied, n * 2 + 1)
                pe.wait_ge(tau_done, g + 1)
                pe.wait_ge(sig_done, n * (TB // CHUNK) + (j // CHUNK + 1))
                for q, (kind, half) in enumerate(PAIRS):
                    at = (slot * TB + j)
                    weights = tau[:, at % TAU_RING] if kind == 0 else sig[:, at % SIG_RING]
                    mm = pe.matmul(ps_acc[32 * q:32 * q + COLS, :], vop[:, slot, j, :],
                                   weights[:, half * HALF:(half + 1) * HALF],
                                   start=(j == 0), stop=(j == TB - 1))
                mm.then_inc(pv_done, 1)

            def head(n, slot, turn, first, last):
                before = misc_before(n, first)
                used = 0
                for j in range(TB):
                    g = n * TB + j
                    keys = slice(j * P, (j + 1) * P)

                    def sigma_scores(half):
                        wait(pe, mag_ready, n * (2 * TB) + (2 * j - 1 + half))
                        pe.matmul(ps_sig[:, half, :], kop[0:SIGMA_ROWS, slot, keys],
                                  qop[0:SIGMA_ROWS, slot, half * HALF:(half + 1) * HALF],
                                  start=True, stop=True).then_inc(sig_ready, 1)

                    sigma_scores(0)
                    if j == 0:
                        pe.wait_ge(mrow_loaded, n * 32 + 32)
                    wait(pe, tau_done, n * TB + (j - 1))
                    for half in range(2):
                        mm = pe.matmul(ps_tau[:, j % 2, half, :], kop[:, slot, keys],
                                       qop[:, slot, half * HALF:(half + 1) * HALF], start=True, stop=True)
                    mm.then_inc(tau_ready, 1)
                    sigma_scores(1)
                    if not last:
                        if j == 0:
                            nxt = (slot + 1) % SLOTS
                            pe.wait_ge(ops_loaded[nxt], (turn + int(nxt == 0)) * LOADED + LOADED)
                        for u in MAX_UNITS[j]:
                            score_halves(n + 1, (slot + 1) % SLOTS, u, before + used)
                            used += 2
                        if j == MT_STEP:
                            turn_maxima(n + 1, before + used)
                            used += 1
                    if j == FT_STEP and not first:
                        turn_sums(n - 1, before + used)
                        used += 1
                    if j == TB - 1:
                        weigh(n, slot, 0, first)
                    elif not first:
                        weigh(n - 1, (slot - 1) % SLOTS, j + 1, first)

            pe.wait_ge(ops_loaded[0], LOADED)
            for u in range(TB):
                score_halves(0, 0, u, 2 * u)
            turn_maxima(0, 2 * TB)
            heads(pe, head)
            for j in range(1, TB):
                weigh(NH - 1, (NH - 1) % SLOTS, j, False)
            turn_sums(NH - 1, misc_before(NH - 1, False) + 1)

        @block.vector
        def _(dve):
            def half_maxima(u, before):
                for half in range(2):
                    dve.wait_ge(misc_ready, before + (half + 1))
                    dve.tensor_reduce(halfmax[:, u, half:half + 1], ps_misc[:, :], AX.X, ALU.max).then_inc(misc_done, 1)

            def maxima(n, before):
                dve.wait_ge(misc_done, before)
                dve.tensor_reduce(rowmax[:, :], halfmax[:, :, :], AX.X, ALU.max).then_inc(max_ready, 1)

            def split_maxima(n, before):
                dve.wait_ge(misc_ready, before + 1)
                wait(dve, mrow_loaded, n * 32)
                dve.tensor_scalar(mrow[:, 0, :], ps_misc[0:TB, 0:P], -1.0, None, ALU.mult).then_inc(mrow_ready, 1)
                dve.wait_ge(mrow_ready, n + 1)
                dve.scalar_tensor_tensor(out=mrow[:, 1, :], in0=ps_misc[0:TB, 0:P], scalar=-1.0, in1=mrow[:, 0, :],
                                         op0=ALU.mult, op1=ALU.subtract).then_inc(misc_done, 1)

            def take_sums(n):
                dve.wait_ge(pv_done, n * TB + TB)
                dve.tensor_copy(sums[:, :], ps_acc[:, :]).then_inc(sums_ready, 1)

            def normalise(n, before):
                m = ps_misc[:, :].rearrange("p (t g r) -> p t g r", t=4, g=4)
                dve.wait_ge(misc_ready, before)
                wait(dve, norm_step, n * 2)
                dve.reciprocal(rden[:, :, :], m[:, :, :, DH]).then_inc(norm_step, 1)
                dve.wait_ge(norm_step, n * 2 + 1)
                dve.tensor_tensor(scaled[:, :, :, :], m[:, :, :, 0:DH],
                                  rden[:, :, :].unsqueeze(3).to_broadcast([P, 4, 4, DH]), ALU.mult)\
                   .then_inc(misc_done, 1)
                dve.wait_ge(misc_done, before)
                s = scaled[:, :, :, :].rearrange("p t (k f) d -> p k f t d", k=2)
                dve.tensor_tensor(w["f"][:, bass.ds(n, 1), :, :].rearrange("p o (f t) d -> p (o f) t d", f=2),
                                  s[:, 0], s[:, 1], ALU.add).then_inc(norm_step, 1)

            def head(n, slot, turn, first, last):
                before = misc_before(n, first)
                used = 0
                dve.wait_ge(head_copied, n * 2 + 2)
                for j in range(TB):
                    at = slot * TB + j

                    def magnitude(half):
                        dve.wait_ge(sig_ready, n * (2 * TB) + (2 * j + half + 1))
                        if half == 0:
                            wait(dve, sqv_ready, n * TB + (j - MAG_RING + 1))
                            wait(dve, sqp_ready, n * TB + (j - MAG_RING + 1))
                        dve.tensor_scalar(mag[:, at % MAG_RING, half * HALF:(half + 1) * HALF].bitcast(I32),
                                          ps_sig[:, half, :].bitcast(I32), SIGN_OFF, None, ALU.bitwise_and)\
                           .then_inc(mag_ready, 1)

                    magnitude(0)
                    if j == 0 and not first and not (isinstance(n, int) and n == 1):
                        normalise(n - 2, before)
                    if j == FT_STEP and not first:
                        take_sums(n - 1)
                    magnitude(1)
                    if not last:
                        for u in MAX_UNITS[j]:
                            half_maxima(u, before + used)
                            used += 2
                            if u == TB - 1:
                                maxima(n + 1, before + used)
                    dve.wait_ge(mag_ready, n * (2 * TB) + (2 * j + 1))
                    wait(dve, pv_done, n * TB + (j - SIG_RING + 1))
                    u = mag[:, at % MAG_RING, 0:VEC_COLS]
                    dve.scalar_tensor_tensor(out=sig[:, at % SIG_RING, 0:VEC_COLS], in0=u, scalar=shape[:, slot, 0:1],
                                             in1=u, op0=ALU.add, op1=ALU.mult).then_inc(sqv_ready, 1)
                    if not last:
                        if j == MT_STEP:
                            split_maxima(n + 1, before + used)
                            used += 1

            dve.memset(ps_acc[:, :], 0.0)
            for u in range(TB):
                half_maxima(u, 2 * u)
            maxima(0, 2 * TB)
            split_maxima(0, 2 * TB)
            heads(dve, head)
            normalise(NH - 2, misc_before(NH - 1, False) + 1)
            take_sums(NH - 1)
            normalise(NH - 1, misc_before(NH - 1, False) + 2)

        @block.scalar
        def _(act):
            def chunk(n, slot, c):
                at = (slot * TB + c * CHUNK) % SIG_RING
                tile = sig[:, at:at + CHUNK, :]
                act.wait_ge(sqv_ready, n * TB + (c * CHUNK + CHUNK))
                act.wait_ge(sqp_ready, n * TB + (c * CHUNK + CHUNK))
                act.activation(tile, tile, ACT.Ln, bias=shape[:, slot, 1:2]).then_inc(ln_done, 1)
                act.wait_ge(ln_done, n * (TB // CHUNK) + (c + 1))
                act.activation(tile, tile, ACT.Exp, scale=-1.0).then_inc(sig_done, 1)

            def head(n, slot, turn, first, last):
                for j in range(TB):
                    at = slot * TB + j
                    act.wait_ge(tau_ready, n * TB + (j + 1))
                    wait(act, pv_done, n * TB + (j - TAU_RING + 1))
                    act.activation(tau[:, at % TAU_RING, :], ps_tau[:, j % 2, :, :].rearrange("p h q -> p (h q)"),
                                   ACT.Exp, scale=float(DH) ** -0.5).then_inc(tau_done, 1)
                    if j == 1 and not first:
                        chunk(n - 1, (slot - 1) % SLOTS, 3)
                    elif j % 2 == 1 and j > 1:
                        chunk(n, slot, (j - CHUNK_LAG) // CHUNK)

            act.preload_act_table_set("natural_log_exp_and_others")
            heads(act, head)
            chunk(NH - 1, (NH - 1) % SLOTS, 3)

        @block.gpsimd
        def _(pool):
            def copy_head(n, slot):
                pool.tensor_copy(vop[:, slot, :, :], w["v"][:, bass.ds(n, 1), :, :].rearrange("p o t c -> p (o t) c"))\
                    .then_inc(head_copied, 1)
                pool.tensor_copy(shape[:, slot, :], w["shape"][:, bass.ds(n, 1), :].rearrange("p o c -> p (o c)"))\
                    .then_inc(head_copied, 1)

            def head(n, slot, turn, first, last):
                for j in range(TB):
                    at = slot * TB + j
                    if j == 2 and not last:
                        if not first:
                            wait(pool, pv_done, (n - 1) * TB)
                        copy_head(n + 1, (slot + 1) % SLOTS)
                    pool.wait_ge(mag_ready, n * (2 * TB) + (2 * j + 2))
                    wait(pool, pv_done, n * TB + (j - SIG_RING + 1))
                    u = mag[:, at % MAG_RING, VEC_COLS:N]
                    wait(pool, sqp_ready, n * TB + j)
                    alone(pool, w["pool_passed"])
                    pool.tensor_scalar(grown[:, :], u, 1.0, shape[:, slot, 0:1], ALU.mult, ALU.add)\
                        .then_inc(grown_ready, 1)
                    pool.wait_ge(grown_ready, n * TB + (j + 1))
                    pool.tensor_tensor(sig[:, at % SIG_RING, VEC_COLS:N], u, grown[:, :], ALU.mult)\
                        .then_inc(sqp_ready, 1)

            pool.memset(qop[:, :, :], 0.0).then_inc(idle_rows_ready, 1)
            pool.memset(kop[:, :, :], 0.0).then_inc(idle_rows_ready, 1)
            pool.wait_ge(idle_rows_ready, 2)
            pool.memset(kop[MROW:MROW + 2, :, :], 1.0).then_inc(idle_rows_ready, 1)
            pool.wait_ge(idle_rows_ready, 3)
            copy_head(0, 0)
            heads(pool, head)


def take_stats(dve, tile_of, stats, mv, stats_ready, mv_ready, before, passed):
    for t in range(TB):
        dve.bn_stats(stats[:, t, :], tile_of(t)).then_inc(stats_ready, 1)
    dve.wait_ge(stats_ready, before + TB)
    alone(dve, passed)
    for t in range(TB):
        dve.bn_aggr(mv[:, t, :], stats[:, t, :]).then_inc(mv_ready, 1)


def take_rstd(act, w, mv, lnv, rstd, mv_ready, ln_ready, rstd_ready, turn):
    act.wait_ge(mv_ready, turn * TB + TB)
    act.activation(lnv[:, :], mv[:, :, 1], ACT.Ln, bias=w["eps"][:, 0:1]).then_inc(ln_ready, 1)
    act.wait_ge(ln_ready, turn + 1)
    act.activation(rstd[:, :], lnv[:, :], ACT.Exp, scale=-0.5).then_inc(rstd_ready, 1)


def four(rows):
    return rows[:, :].unsqueeze(1).to_broadcast([P, 4, rows.shape[-1]])


def mix_experts(nc, w):
    with ExitStack() as ctx:
        def sb(name, shape, dt=F32):
            return ctx.enter_context(nc.sbuf_tensor(name, shape, dt))

        def sem(name):
            return ctx.enter_context(nc.semaphore(name))

        f = sb("f_tile", [P, TB, H, DH])
        turned_sb = sb("turned_sb", [P, 2, N])
        y = sb("y", [P, TB, D])
        yn = sb("y_normed", [P, TB, D])
        z = sb("z", [P, TB, D])
        stats = sb("stats_m", [P, 2, TB, 6])
        mv = sb("mv_m", [P, 2, TB, 2])
        lnv = sb("lnv_m", [P, 2, TB])
        rstd = sb("rstd_m", [P, 2, TB])
        lg = sb("gate_logits", [P, TB, E])
        top = sb("gate_max", [P, TB])
        prob = sb("gate_prob", [P, TB, E])
        total = sb("gate_sum", [P, 2, TB])
        inv = sb("gate_inverse", [P, 2, TB])
        kept = sb("gate_kept", [P, TB, E])
        guard = sb("gate_guard", [P, TB])
        weight = sb("gate_weight", [P, TB, E])
        weight_t = sb("gate_weight_t", [E, N])
        ps_t = ctx.enter_context(nc.psum_tensor("ps_mt", [P, 2, HALF], F32))
        ps_y = ctx.enter_context(nc.psum_tensor("ps_my", [P, 2, HALF], F32))
        ps_e = ctx.enter_context(nc.psum_tensor("ps_me", [P, 2, 2, HALF], F32))

        f_copied = sem("f_copied")
        turned, turned_read = sem("m_turned"), sem("m_turned_read")
        y_ready, y_biased = sem("y_ready"), sem("y_biased")
        stats_ready, mv_ready = [sem(f"m_stats{i}") for i in range(2)], [sem(f"m_mv{i}") for i in range(2)]
        ln_ready, rstd_ready = [sem(f"m_ln{i}") for i in range(2)], [sem(f"m_rstd{i}") for i in range(2)]
        yn_ready, x_biased, x_ready, z_ready = sem("yn_ready"), sem("x_biased"), sem("m_x_ready"), sem("m_z_ready")
        gate_ready, gate_step, exp_ready = sem("gate_ready"), sem("gate_step"), sem("gate_exp")
        bias_ready, e_ready, e_step = sem("expert_bias_ready"), sem("e_ready"), sem("e_step")
        GATE = 11
        block = ctx.enter_context(nc.Block())

        def xt(b, t):
            return w["x"][:, bass.ds(b * TB + t, 1), :].rearrange("p o d -> p (o d)")

        @block.scalar
        def _(act):
            act.preload_act_table_set("natural_log_exp_and_others")
            with act.Fori(0, B) as b:
                act.wait_ge(turned, b * 3 * TB)
                act.activation(f[:, :, :, :].rearrange("p t h d -> p h t d"), w["f"][:, bass.ds(b * H, H), :, :], ACT.Copy).then_inc(f_copied, 1)
                for use in range(2):
                    if use == 1:
                        take_rstd(act, w, mv[:, 0], lnv[:, 0], rstd[:, 0], mv_ready[0], ln_ready[0], rstd_ready[0], b)
                        take_rstd(act, w, mv[:, 1], lnv[:, 1], rstd[:, 1], mv_ready[1], ln_ready[1], rstd_ready[1], b)
                    for g in range(2):
                        act.wait_ge(turned, b * 3 * TB + (use * TB + 4 * (g + 1)))
                        act.wait_ge(y_ready if use == 0 else e_ready, b * (TB if use == 0 else 2 * TB))
                        act.activation(turned_sb[:, use, g * HALF:(g + 1) * HALF], ps_t[:, g, :], ACT.Copy)\
                           .then_inc(turned_read, 1)
                act.wait_ge(gate_step, b * GATE + 3)
                act.activation(prob[:, :, :], lg[:, :, :], ACT.Exp).then_inc(exp_ready, 1)
                act.wait_ge(bias_ready, b * TB)
                for g in range(2):
                    act.wait_ge(turned, b * 3 * TB + (2 * TB + 4 * (g + 1)))
                    act.activation(weight_t[:, g * HALF:(g + 1) * HALF], ps_t[0:E, g, :], ACT.Copy)\
                       .then_inc(turned_read, 1)

        @block.tensor
        def _(pe):
            with pe.Fori(0, B) as b:
                pe.wait_ge(f_copied, b + 1)
                pe.wait_ge(turned_read, b * 6)
                for t in range(TB):
                    pe.transpose(ps_t[:, t // 4, (t % 4) * P:(t % 4 + 1) * P], f[:, t].rearrange("p h d -> p (h d)"),
                                 w["ident"][:, :]).then_inc(turned, 1)
                pe.wait_ge(turned_read, b * 6 + 2)
                pe.wait_ge(e_step, b * (TB * E + 2))
                for t in range(TB):
                    pe.matmul(ps_y[:, t // 4, (t % 4) * P:(t % 4 + 1) * P], turned_sb[:, 0, t * P:(t + 1) * P],
                              w["wt"][:, 3, :], start=True, stop=True).then_inc(y_ready, 1)
                for t in range(TB):
                    pe.wait_ge(z_ready, b * TB + (t + 1))
                    pe.transpose(ps_t[:, t // 4, (t % 4) * P:(t % 4 + 1) * P], z[:, t, :], w["ident"][:, :])\
                      .then_inc(turned, 1)
                pe.wait_ge(turned_read, b * 6 + 4)
                pe.wait_ge(y_biased, b * 2 + 2)
                for t in range(TB):
                    pe.matmul(ps_y[:, 0, t * E:(t + 1) * E], turned_sb[:, 1, t * P:(t + 1) * P], w["gate"][:, :],
                              start=True, stop=True).then_inc(gate_ready, 1)

                def experts(t):
                    pe.wait_ge(e_step, b * (TB * E + 2) + max(0, 2 + (t - 1) * E) if t > 1
                               else b * (TB * E + 2))
                    for half in range(2):
                        pe.matmul(ps_e[:, t % 2, half, :], turned_sb[:, 1, t * P:(t + 1) * P],
                                  w["experts"][:, 4 * half:4 * half + 4, :], start=True, stop=True).then_inc(e_ready, 1)

                experts(0)
                experts(1)
                pe.wait_ge(gate_step, b * GATE + GATE)
                for t in range(TB):
                    pe.transpose(ps_t[0:E, t // 4, (t % 4) * P:(t % 4 + 1) * P], weight[:, t, :], w["ident"][:, :])\
                      .then_inc(turned, 1)
                pe.wait_ge(turned_read, b * 6 + 6)
                for t in range(TB):
                    pe.matmul(ps_y[:, t // 4, (t % 4) * P:(t % 4 + 1) * P], weight_t[:, t * P:(t + 1) * P],
                              w["expert_b"][:, :], start=True, stop=True).then_inc(bias_ready, 1)
                for t in range(2, TB):
                    experts(t)

        @block.gpsimd
        def _(pool):
            with pool.Fori(0, B) as b:
                for g in range(2):
                    xs = w["x"][:, bass.ds(b * TB + 4 * g, 4), :]
                    pool.tensor_tensor(xs, xs, four(w["ln_b"]), ALU.add).then_inc(x_biased, 1)

        @block.vector
        def _(dve):
            with dve.Fori(0, B) as b:
                dve.wait_ge(yn_ready, b * (TB + 1))
                for g in range(2):
                    dve.wait_ge(y_ready, b * TB + 4 * (g + 1))
                    dve.tensor_tensor(y[:, 4 * g:4 * g + 4, :], ps_y[:, g, :].rearrange("p (t d) -> p t d", t=4),
                                      four(w["bo"]), ALU.add).then_inc(y_biased, 1)
                dve.wait_ge(y_biased, b * 2 + 2)
                take_stats(dve, lambda t: y[:, t, :], stats[:, 0], mv[:, 0], stats_ready[0], mv_ready[0], b * TB, w["dve_passed"])
                dve.wait_ge(mv_ready[0], b * TB + TB)
                dve.wait_ge(rstd_ready[0], b + 1)
                for t in range(TB):
                    dve.tensor_scalar(yn[:, t, :], y[:, t, :], mv[:, 0, t, 0:1], rstd[:, 0, t:t + 1],
                                      ALU.subtract, ALU.mult).then_inc(yn_ready, 1)
                dve.wait_ge(yn_ready, b * (TB + 1) + TB)
                for g in range(2):
                    ins = dve.tensor_tensor(yn[:, 4 * g:4 * g + 4, :], yn[:, 4 * g:4 * g + 4, :], four(w["ln_w"]), ALU.mult)
                ins.then_inc(yn_ready, 1)
                dve.wait_ge(yn_ready, b * (TB + 1) + (TB + 1))
                dve.wait_ge(x_biased, b * 2 + 2)
                xs = w["x"][:, bass.ds(b * TB, TB), :].rearrange("p t d -> p (t d)")
                dve.tensor_tensor(xs, xs, yn[:, :, :].rearrange("p t d -> p (t d)"), ALU.add).then_inc(x_ready, 1)
                dve.wait_ge(x_ready, b + 1)
                alone(dve, w["dve_passed"])
                take_stats(dve, lambda t: xt(b, t), stats[:, 1], mv[:, 1], stats_ready[1], mv_ready[1], b * TB, w["dve_passed"])
                dve.wait_ge(mv_ready[1], b * TB + TB)
                dve.wait_ge(rstd_ready[1], b + 1)
                for t in range(TB):
                    dve.tensor_scalar(z[:, t, :], xt(b, t), mv[:, 1, t, 0:1], rstd[:, 1, t:t + 1],
                                      ALU.subtract, ALU.mult).then_inc(z_ready, 1)
                step = [0]

                def then(ins):
                    ins.then_inc(gate_step, 1)
                    step[0] += 1
                    dve.wait_ge(gate_step, b * GATE + step[0])

                def each(v):
                    return v.unsqueeze(2).to_broadcast([P, TB, E])

                dve.wait_ge(gate_ready, b * TB + TB)
                then(dve.tensor_tensor(lg[:, :, :], ps_y[:, 0, 0:TB * E].rearrange("p (t e) -> p t e", t=TB),
                                       w["gate_b"][:, :].unsqueeze(1).to_broadcast([P, TB, E]), ALU.add))
                then(dve.tensor_reduce(top[:, :], lg[:, :, :], AX.X, ALU.max))
                then(dve.tensor_tensor(lg[:, :, :], lg[:, :, :], each(top[:, :]), ALU.subtract))
                dve.wait_ge(exp_ready, b + 1)
                then(dve.tensor_reduce(total[:, 0, :], prob[:, :, :], AX.X, ALU.add))
                then(dve.reciprocal(inv[:, 0, :], total[:, 0, :]))
                then(dve.tensor_tensor(prob[:, :, :], prob[:, :, :], each(inv[:, 0, :]), ALU.mult))
                then(dve.scalar_tensor_tensor(out=kept[:, :, :], in0=prob[:, :, :], scalar=THRESHOLD, in1=prob[:, :, :],
                                              op0=ALU.is_ge, op1=ALU.mult))
                then(dve.tensor_reduce(total[:, 1, :], kept[:, :, :], AX.X, ALU.add))
                then(dve.scalar_tensor_tensor(out=guard[:, :], in0=total[:, 1, :], scalar=0.0, in1=total[:, 1, :],
                                              op0=ALU.is_equal, op1=ALU.add))
                then(dve.reciprocal(inv[:, 1, :], guard[:, :]))
                then(dve.tensor_tensor(weight[:, :, :], kept[:, :, :], each(inv[:, 1, :]), ALU.mult))
                assert step[0] == GATE
                for g in range(2):
                    dve.wait_ge(bias_ready, b * TB + 4 * (g + 1))
                    xs = w["x"][:, bass.ds(b * TB + 4 * g, 4), :]
                    dve.tensor_tensor(xs, xs, ps_y[:, g, :].rearrange("p (t d) -> p t d", t=4), ALU.add)\
                       .then_inc(e_step, 1)
                for t in range(TB):
                    for e in range(E):
                        dve.wait_ge(e_step, b * (TB * E + 2) + (2 + t * E + e))
                        if e % 4 == 0:
                            dve.wait_ge(e_ready, b * 2 * TB + (2 * t + e // 4 + 1))
                        dve.scalar_tensor_tensor(out=xt(b, t), in0=ps_e[:, t % 2, e // 4, (e % 4) * D:(e % 4 + 1) * D],
                                                 scalar=weight[:, t, e:e + 1], in1=xt(b, t),
                                                 op0=ALU.mult, op1=ALU.add).then_inc(e_step, 1)


def attend_causal(nc, w):
    with ExitStack() as ctx:
        def sb(name, shape, dt=F32):
            return ctx.enter_context(nc.sbuf_tensor(name, shape, dt))

        def ps(name, shape, dt=F32):
            return ctx.enter_context(nc.psum_tensor(name, shape, dt))

        def sem(name):
            return ctx.enter_context(nc.semaphore(name))

        stats, mv = sb("stats_c", [P, TB, 6]), sb("mv_c", [P, TB, 2])
        lnv, rstd = sb("lnv_c", [P, TB]), sb("rstd_c", [P, TB])
        z = sb("z_c", [P, TB, D])
        zt = sb("z_turned", [P, N])
        qk = sb("qk_c", [DA, 2, N])
        v = sb("v_c", [P, TB, DA])
        top, shift = sb("top_c", [P, TB]), sb("shift_c", [P, TB])
        prob = sb("prob_c", [P, 2, N])
        total, inv = sb("total_c", [P, TB]), sb("inverse_c", [P, TB])
        prob_t = sb("prob_t", [P, 2, N])
        mixed = sb("mixed", [P, 2, DA])
        mixed_t = sb("mixed_t", [DA, 2, P])
        ps_s = ps("ps_cs", [P, 2, 2, HALF])
        ps_t = ps("ps_ct", [P, 2, HALF])
        ps_o = ps("ps_co", [P, HALF])
        ps_x = ps("ps_cx", [P, HALF])

        stats_ready, mv_ready, ln_ready, rstd_ready = sem("c_stats"), sem("c_mv"), sem("c_ln"), sem("c_rstd")
        z_ready, turned, zt_ready = sem("c_z"), sem("c_turned"), sem("c_zt")
        proj_ready, qk_ready, v_ready, v_done = sem("c_proj"), sem("c_qk"), sem("c_v"), sem("c_v_done")
        s_ready, masked, max_step = sem("c_scores"), sem("c_masked"), sem("c_max")
        exp_ready, p_turned, p_copied = sem("c_exp"), sem("c_p_turned"), sem("c_p_copied")
        o_ready, inv_ready, mixed_ready = sem("c_out"), sem("c_inverse"), sem("c_mixed")
        m_turned, m_copied, add_ready, x_done = sem("c_m_turned"), sem("c_m_copied"), sem("c_add"), sem("c_x_done")
        x_biased = sem("c_x_biased")
        block = ctx.enter_context(nc.Block())

        def xt(b, t):
            return w["x"][:, bass.ds(b * TB + t, 1), :].rearrange("p o d -> p (o d)")

        @block.vector
        def _(dve):
            with dve.Fori(0, B) as b:
                take_stats(dve, lambda t: xt(b, t), stats, mv, stats_ready, mv_ready, b * TB, w["dve_passed"])
                dve.wait_ge(mv_ready, b * TB + TB)
                dve.wait_ge(rstd_ready, b + 1)
                for t in range(TB):
                    dve.tensor_scalar(z[:, t, :], xt(b, t), mv[:, t, 0:1], rstd[:, t:t + 1],
                                      ALU.subtract, ALU.mult).then_inc(z_ready, 1)
                dve.wait_ge(v_ready, b * TB + TB)
                dve.tensor_tensor(v[:, :, :], ps_x[:, :].rearrange("p (t d) -> p t d", t=TB),
                                  w["bv1"][:, :].unsqueeze(1).to_broadcast([P, TB, DA]), ALU.add).then_inc(v_done, 1)

                def weigh(i):
                    dve.wait_ge(exp_ready, b * TB + (i + 1))
                    dve.reciprocal(inv[:, i:i + 1], total[:, i:i + 1]).then_inc(inv_ready, 1)
                    dve.wait_ge(inv_ready, b * TB + (i + 1))
                    dve.wait_ge(o_ready, b * TB + (i + 1))
                    dve.tensor_scalar(mixed[:, i % 2, :], ps_o[:, 0:DA], inv[:, i:i + 1], None, ALU.mult)\
                       .then_inc(mixed_ready, 1)

                def add(i):
                    dve.wait_ge(x_biased, b * 2 + (1 if i < 4 else 2))
                    dve.wait_ge(add_ready, b * TB + (i + 1))
                    dve.tensor_tensor(xt(b, i), xt(b, i), ps_x[:, 0:D], ALU.add).then_inc(x_done, 1)

                def turned_half(i, g):
                    n = min(4, i + 1 - 4 * g)
                    dve.wait_ge(p_turned, b * 12 + (sum(1 + (k >= 4) for k in range(i)) + (g + 1)))
                    dve.tensor_copy(prob_t[:, i % 2, g * HALF:g * HALF + n * P], ps_t[:, g, 0:n * P]).then_inc(p_copied, 1)

                for i in range(TB):
                    dve.wait_ge(s_ready, b * TB + (i + 1))
                    diagonal = ps_s[:, i % 2, i // 4, (i % 4) * P:(i % 4 + 1) * P]
                    dve.tensor_tensor(diagonal, diagonal, w["causal"][:, :], ALU.add).then_inc(masked, 1)
                    dve.wait_ge(masked, b * TB + (i + 1))
                    dve.tensor_reduce(top[:, i:i + 1],
                                      ps_s[:, i % 2, :, :].rearrange("p f k -> p (f k)")[:, 0:(i + 1) * P],
                                      AX.X, ALU.max).then_inc(max_step, 1)
                    dve.wait_ge(max_step, b * 2 * TB + (2 * i + 1))
                    dve.tensor_scalar(shift[:, i:i + 1], top[:, i:i + 1], -float(DA) ** -0.5, None, ALU.mult)\
                       .then_inc(max_step, 1)
                    if i >= 1:
                        for g in range(1 + (i - 1) // 4):
                            turned_half(i - 1, g)
                        weigh(i - 1)
                    if i >= 2:
                        add(i - 2)
                for g in range(2):
                    turned_half(TB - 1, g)
                weigh(TB - 1)
                add(TB - 2)
                add(TB - 1)
                dve.wait_ge(x_done, b * TB + TB)

        @block.scalar
        def _(act):
            act.preload_act_table_set("natural_log_exp_and_others")
            with act.Fori(0, B) as b:
                take_rstd(act, w, mv, lnv, rstd, mv_ready, ln_ready, rstd_ready, b)
                for g in range(2):
                    act.wait_ge(turned, b * TB + 4 * (g + 1))
                    act.activation(zt[:, g * HALF:(g + 1) * HALF], ps_t[:, g, :], ACT.Copy).then_inc(zt_ready, 1)
                for s in range(2):
                    for g in range(2):
                        act.wait_ge(proj_ready, b * 4 + (2 * s + g + 1))
                        act.activation(qk[:, s, g * HALF:(g + 1) * HALF], ps_s[0:DA, s, g, :], ACT.Identity,
                                       bias=w["b1"][:, s:s + 1]).then_inc(qk_ready, 1)

                def mixed_half(i):
                    act.wait_ge(m_turned, b * TB + (i + 1))
                    act.activation(mixed_t[:, i % 2, :], ps_o[0:DA, P:2 * P], ACT.Copy).then_inc(m_copied, 1)

                for i in range(TB):
                    act.wait_ge(max_step, b * 2 * TB + (2 * i + 2))
                    act.activation(prob[:, i % 2, 0:(i + 1) * P],
                                   ps_s[:, i % 2, :, :].rearrange("p f k -> p (f k)")[:, 0:(i + 1) * P], ACT.Exp,
                                   bias=shift[:, i:i + 1], scale=float(DA) ** -0.5, accum_out=total[:, i:i + 1])\
                       .then_inc(exp_ready, 1)
                    if i >= 2:
                        mixed_half(i - 2)
                mixed_half(TB - 2)
                mixed_half(TB - 1)

        @block.gpsimd
        def _(pool):
            with pool.Fori(0, B) as b:
                pool.wait_ge(z_ready, b * TB + TB)
                for g in range(2):
                    xs = w["x"][:, bass.ds(b * TB + 4 * g, 4), :]
                    pool.tensor_tensor(xs, xs, four(w["bo1"]), ALU.add).then_inc(x_biased, 1)

        @block.tensor
        def _(pe):
            with pe.Fori(0, B) as b:
                for t in range(TB):
                    pe.wait_ge(z_ready, b * TB + (t + 1))
                    if t == 0:
                        pe.wait_ge(p_copied, b * 12)
                    pe.transpose(ps_t[:, t // 4, (t % 4) * P:(t % 4 + 1) * P], z[:, t, :], w["ident"][:, :])\
                      .then_inc(turned, 1)
                pe.wait_ge(zt_ready, b * 2 + 2)
                pe.wait_ge(exp_ready, b * TB)
                for s in range(2):
                    for g in range(2):
                        pe.matmul(ps_s[0:DA, s, g, :], w["qkv1"][:, s, :], zt[:, g * HALF:(g + 1) * HALF],
                                  start=True, stop=True).then_inc(proj_ready, 1)
                pe.wait_ge(x_done, b * TB)
                for t in range(TB):
                    pe.matmul(ps_x[:, t * DA:(t + 1) * DA], zt[:, t * P:(t + 1) * P], w["qkv1"][:, 2, :],
                              start=True, stop=True).then_inc(v_ready, 1)

                def scores(i):
                    if i == 0:
                        pe.wait_ge(qk_ready, b * 4 + 4)
                    else:
                        pe.wait_ge(exp_ready, b * TB + (i - 1))
                    for g in range(1 + i // 4):
                        n = min(4, i + 1 - 4 * g) * P
                        mm = pe.matmul(ps_s[:, i % 2, g, 0:n], qk[:, 0, i * P:(i + 1) * P],
                                       qk[:, 1, g * HALF:g * HALF + n], start=True, stop=True)
                    mm.then_inc(s_ready, 1)

                def turn_weights(i):
                    pe.wait_ge(exp_ready, b * TB + (i + 1))
                    for g in range(1 + i // 4):
                        pe.wait_ge(p_copied, b * 12 + sum(1 + (k >= 4) for k in range(i)))
                        for k in range(4 * g, min(4 * g + 4, i + 1)):
                            mm = pe.transpose(ps_t[:, g, (k % 4) * P:(k % 4 + 1) * P], prob[:, i % 2, k * P:(k + 1) * P],
                                              w["ident"][:, :])
                        mm.then_inc(p_turned, 1)

                def weigh(i):
                    pe.wait_ge(p_copied, b * 12 + sum(1 + (k >= 4) for k in range(i + 1)))
                    if i == 0:
                        pe.wait_ge(v_done, b + 1)
                    pe.wait_ge(mixed_ready, b * TB + i)
                    pe.wait_ge(m_copied, b * TB + i)
                    for k in range(i + 1):
                        mm = pe.matmul(ps_o[:, 0:DA], prob_t[:, i % 2, k * P:(k + 1) * P], v[:, k, :],
                                       start=(k == 0), stop=(k == i))
                    mm.then_inc(o_ready, 1)

                def turn_mixed(i):
                    pe.wait_ge(mixed_ready, b * TB + (i + 1))
                    pe.wait_ge(m_copied, b * TB + i)
                    alone(pe, w["pe_passed"])
                    pe.transpose(ps_o[0:DA, P:2 * P], mixed[:, i % 2, :], w["ident"][:, :]).then_inc(m_turned, 1)

                def project(i):
                    pe.wait_ge(m_copied, b * TB + (i + 1))
                    pe.wait_ge(x_done, b * TB + i)
                    pe.matmul(ps_x[:, 0:D], mixed_t[:, i % 2, :], w["wo1"][:, :], start=True, stop=True)\
                      .then_inc(add_ready, 1)

                scores(0)
                for i in range(TB):
                    if i + 1 < TB:
                        scores(i + 1)
                    turn_weights(i)
                    if i >= 1:
                        turn_mixed(i - 1)
                    weigh(i)
                    if i >= 1:
                        project(i - 1)
                turn_mixed(TB - 1)
                project(TB - 1)


def descend_tree(nc, w, out):
    with ExitStack() as ctx:
        def sb(name, shape, dt=F32):
            return ctx.enter_context(nc.sbuf_tensor(name, shape, dt))

        def ps(name, shape, dt=F32):
            return ctx.enter_context(nc.psum_tensor(name, shape, dt))

        def sem(name):
            return ctx.enter_context(nc.semaphore(name))

        stats, mv = sb("stats_d", [P, TB, 6]), sb("mv_d", [P, TB, 2])
        lnv, rstd = sb("lnv_d", [P, TB]), sb("rstd_d", [P, TB])
        z = sb("z_d", [P, TB, D])
        zt = sb("zt_d", [P, N])
        right = sb("right", [P, TB, LEAVES])
        reach = [sb(f"reach{i}", [P, TB, LEAVES]) for i in range(2)]
        reach_t = sb("reach_t", [P, TB, 2, P])
        ps_t = ps("ps_dt", [P, 2, HALF])
        ps_g = ps("ps_dg", [P, 4, HALF])
        ps_x = ps("ps_dx", [P, 2, HALF])
        stats_ready, mv_ready, ln_ready, rstd_ready = sem("d_stats"), sem("d_mv"), sem("d_ln"), sem("d_rstd")
        z_ready, turned, zt_ready = sem("d_z"), sem("d_turned"), sem("d_zt")
        logit_ready, right_ready, level = sem("d_logit"), sem("d_right"), sem("d_level")
        leaf_turned, leaf_copied = sem("d_leaf_turned"), sem("d_leaf_copied")
        add_ready, x_biased, x_done, stored = sem("d_add"), sem("d_x_biased"), sem("d_x_done"), sem("d_stored")
        block = ctx.enter_context(nc.Block())

        def xt(b, t):
            return w["x"][:, bass.ds(b * TB + t, 1), :].rearrange("p o d -> p (o d)")

        LEVELS = 2 * DEPTH

        @block.vector
        def _(dve):
            with dve.Fori(0, B) as b:
                take_stats(dve, lambda t: xt(b, t), stats, mv, stats_ready, mv_ready, b * TB, w["dve_passed"])
                dve.wait_ge(mv_ready, b * TB + TB)
                dve.wait_ge(rstd_ready, b + 1)
                for t in range(TB):
                    dve.tensor_scalar(z[:, t, :], xt(b, t), mv[:, t, 0:1], rstd[:, t:t + 1],
                                      ALU.subtract, ALU.mult).then_inc(z_ready, 1)
                dve.wait_ge(right_ready, b * 4 + 4)
                dve.wait_ge(leaf_turned, b * 4)
                for d in range(DEPTH):
                    n = 2 ** d
                    new = reach[d % 2][:, :, 0:2 * n].rearrange("p t (n s) -> p t n s", s=2)
                    g = right[:, :, n - 1:2 * n - 1]
                    if d == 0:
                        dve.tensor_copy(new[:, :, :, 1], g).then_inc(level, 1)
                        dve.tensor_scalar(new[:, :, :, 0], g, -1.0, 1.0, ALU.mult, ALU.add).then_inc(level, 1)
                    else:
                        old = reach[(d - 1) % 2][:, :, 0:n]
                        dve.wait_ge(level, b * LEVELS + 2 * d)
                        dve.tensor_tensor(new[:, :, :, 1], old, g, ALU.mult).then_inc(level, 1)
                        dve.wait_ge(level, b * LEVELS + (2 * d + 1))
                        dve.tensor_tensor(new[:, :, :, 0], old, new[:, :, :, 1], ALU.subtract).then_inc(level, 1)
                for g in range(2):
                    dve.wait_ge(x_biased, b * 2 + (g + 1))
                    dve.wait_ge(add_ready, b * TB + 4 * (g + 1))
                    xs = w["x"][:, bass.ds(b * TB + 4 * g, 4), :]
                    dve.tensor_tensor(xs, xs, ps_x[:, g, :].rearrange("p (t d) -> p t d", t=4), ALU.add)\
                       .then_inc(x_done, 1)

        @block.scalar
        def _(act):
            with act.Fori(0, B) as b:
                take_rstd(act, w, mv, lnv, rstd, mv_ready, ln_ready, rstd_ready, b)
                for g in range(2):
                    act.wait_ge(turned, b * TB + 4 * (g + 1))
                    act.activation(zt[:, g * HALF:(g + 1) * HALF], ps_t[:, g, :], ACT.Copy).then_inc(zt_ready, 1)
                act.wait_ge(level, b * LEVELS)
                for g in range(4):
                    act.wait_ge(logit_ready, b * TB + 2 * (g + 1))
                    act.activation(right[:, 2 * g:2 * g + 2, 0:NODES],
                                   ps_g[:, g, :].rearrange("p (t n) -> p t n", t=2)[:, :, 0:NODES], ACT.Sigmoid)\
                       .then_inc(right_ready, 1)
                for g in range(4):
                    act.wait_ge(leaf_turned, b * 4 + (g + 1))
                    act.activation(reach_t[:, 2 * g:2 * g + 2, :, :].rearrange("p t i d -> p (t i d)"), ps_g[:, g, :],
                                   ACT.Copy).then_inc(leaf_copied, 1)

        @block.gpsimd
        def _(pool):
            with pool.Fori(0, B) as b:
                pool.wait_ge(z_ready, b * TB + TB)
                for g in range(2):
                    xs = w["x"][:, bass.ds(b * TB + 4 * g, 4), :]
                    pool.tensor_tensor(xs, xs, four(w["bout"]), ALU.add).then_inc(x_biased, 1)

        @block.tensor
        def _(pe):
            with pe.Fori(0, B) as b:
                for t in range(TB):
                    pe.wait_ge(z_ready, b * TB + (t + 1))
                    pe.transpose(ps_t[:, t // 4, (t % 4) * P:(t % 4 + 1) * P], z[:, t, :], w["ident"][:, :])\
                      .then_inc(turned, 1)
                pe.wait_ge(zt_ready, b * 2 + 2)
                pe.wait_ge(leaf_copied, b * 4)
                for t in range(TB):
                    at = (t % 2) * LEAVES
                    pe.matmul(ps_g[:, t // 2, at:at + NODES], zt[:, t * P:(t + 1) * P], w["router"][:, :],
                              start=True, stop=True).then_inc(logit_ready, 1)
                pe.wait_ge(level, b * LEVELS + LEVELS)
                leaves = reach[(DEPTH - 1) % 2]
                for g in range(4):
                    for t in range(2 * g, 2 * g + 2):
                        for i in range(2):
                            at = (t % 2) * LEAVES + i * P
                            mm = pe.transpose(ps_g[:, g, at:at + P], leaves[:, t, i * P:(i + 1) * P], w["ident"][:, :])
                    mm.then_inc(leaf_turned, 1)
                pe.wait_ge(x_done, b * 2)
                for t in range(TB):
                    pe.wait_ge(leaf_copied, b * 4 + (t // 2 + 1))
                    for i in range(2):
                        mm = pe.matmul(ps_x[:, t // 4, (t % 4) * P:(t % 4 + 1) * P], reach_t[:, t, i, :],
                                       w["leaf"][:, i, :], start=(i == 0), stop=(i == 1))
                    mm.then_inc(add_ready, 1)

        @block.sync
        def _(sp):
            with sp.Fori(0, B) as b:
                sp.wait_ge(x_done, b * 2 + 2)
                sp.dma_start(out[bass.ds(b, 1)].rearrange("o (t p) d -> p (o t) d", p=P),
                             w["x"][:, bass.ds(b * TB, TB), :]).then_inc(stored, 16)
            sp.wait_ge(stored, 16 * B)


_INS = ["L0_attn_x"] + [f"L0_attn_{n}" for n in ("Wq", "bq", "Wk", "bk", "Wv", "bv", "Wo", "bo", "beta", "t", "ln_w", "ln_b")]\
    + [f"L0_ffn_{n}" for n in ("gate_w", "gate_b", "expert_w", "expert_b")]\
    + [f"L1_attn_{n}" for n in ("wq", "bq", "wk", "bk", "wv", "bv", "wo", "bo")]\
    + [f"L1_ffn_{n}" for n in ("Wq", "routers", "leaf_keys", "leaf_values", "Wout_w", "Wout_b")]


def kernel(**inputs):
    import numpy as np
    import concourse.bacc as bacc
    from concourse.bass_utils import run_bass_kernel_spmd

    nc = bacc.Bacc("TRN2", target_bir_lowering=False, num_devices=1)
    arrays, drams = {}, {}
    for name in _INS:
        x = np.ascontiguousarray(inputs[name])
        arrays[f"in_{name}"] = x
        drams[name] = nc.dram_tensor(f"in_{name}", x.shape, mybir.dt.from_np(x.dtype), kind="ExternalInput").ap()
    out = nc.dram_tensor("out", (B, N, D), F32, kind="ExternalOutput").ap()
    build(nc, drams, out)
    result = run_bass_kernel_spmd(nc, [arrays], core_ids=[0])
    return result.results[0]["out"]
```

```python
from contextlib import ExitStack

import concourse.bass as bass
from concourse import mybir

F32 = mybir.dt.float32
BF16 = mybir.dt.bfloat16
I32 = mybir.dt.int32
ALU = mybir.AluOpType
ACT = mybir.ActivationFunctionType
AX = mybir.AxisListType

P = 128
B, N, D = 4, 1024, 128
TB = N // P
NT = B * TB
H, DH = 16, 8
NH = B * H
HALF = 512
EPS = 1e-5
SIGN_OFF = 0x7FFFFFFF

E = 8
THRESHOLD = 0.1
DA = 64
DEPTH = 8
LEAVES = 2 ** DEPTH
NODES = LEAVES - 1
MASKED = -100000000000.0

PARTS = 3
TERMS = PARTS * PARTS * DH
MROW = 96
SIGMA_ROWS = 96
SLOTS = 3
TAU_SHIFT = 4
TAU_RING = 6
MAG_RING = 4
VEC_COLS = 176
GROWN_RING = 3
CHUNK = 2
SIG_RING = 12
CHUNK_LAG = 5
PV_LAG = 7
MT_STEP, FT_STEP = 1, 3
SUMS_STEP = 7
LOOPS = (NH - 1) // SLOTS - 1
COLS = DH + 1
PAIRS = [(kind, half) for kind in range(2) for half in range(2)]


def build(nc, a, out):
    with ExitStack() as ctx:
        def sb(name, shape, dt=F32):
            return ctx.enter_context(nc.sbuf_tensor(name, shape, dt))

        def dram(name, shape, dt):
            return nc.dram_tensor(name, shape, dt, kind="Internal").ap()

        w = {}
        w["ident"] = sb("ident", [P, P])
        w["x"] = sb("x_res", [P, NT, D])
        w["wt"] = sb("wt", [P, 4, D])
        w["bq"] = sb("bq_col", [P, 1])
        w["bk"] = sb("bk_col", [P, 1])
        w["bv"] = sb("bv_rows", [P, D])
        w["eps"] = sb("eps", [P, 1])
        w["shape"] = sb("kernel_shape", [P, NH, 2])
        w["v"] = sb("v_heads", [P, NH, TB, COLS])
        w["f"] = sb("f_heads", [P, NH, TB, DH])
        w["bo"] = sb("bo_rows", [P, D])
        w["ln_w"] = sb("ln_w_rows", [P, D])
        w["ln_b"] = sb("ln_b_rows", [P, D])
        w["gate"] = sb("gate", [P, E])
        w["gate_b"] = sb("gate_b_rows", [P, E])
        w["experts"] = sb("experts", [P, E, D])
        w["expert_b"] = sb("expert_b", [E, D])
        w["qkv1"] = sb("qkv1", [P, 3, DA])
        w["b1"] = sb("b1_cols", [DA, 2])
        w["bv1"] = sb("bv1_rows", [P, DA])
        w["wo1"] = sb("wo1", [DA, D])
        w["bo1"] = sb("bo1_rows", [P, D])
        w["causal"] = sb("causal", [P, P])
        w["router"] = sb("router", [P, NODES])
        w["leaf"] = sb("leaf", [P, 2, D])
        w["bout"] = sb("bout_rows", [P, D])
        w["q_parts"] = dram("q_parts", [NH, PARTS, DH, N], BF16)
        w["k_parts"] = dram("k_parts", [NH, PARTS, DH, N], BF16)

        for engine in ("dve", "pool", "sp", "pe"):
            w[f"{engine}_passed"] = ctx.enter_context(nc.semaphore(f"{engine}_passed"))

        load_weights(nc, a, w)
        project_heads(nc, a, w)
        attend_heads(nc, a, w)
        mix_experts(nc, w)
        attend_causal(nc, w)
        descend_tree(nc, w, out)


def alone(eng, passed):
    eng.sem_inc(passed, 1)


def load_weights(nc, a, w):
    with ExitStack() as ctx:
        raw = ctx.enter_context(nc.sbuf_tensor("raw_w", [P, 4, D], F32))
        tree = ctx.enter_context(nc.sbuf_tensor("raw_tree", [P, 6, D], F32))
        tree_t = ctx.enter_context(nc.sbuf_tensor("tree_t", [P, 5, D], F32))
        turned_tree = ctx.enter_context(nc.psum_tensor("turned_tree", [P, 2, 4, D], F32))
        made = ctx.enter_context(nc.psum_tensor("made", [P, 2, 512], F32))
        tree_ready = ctx.enter_context(nc.semaphore("tree_ready"))
        made_ready = ctx.enter_context(nc.semaphore("made_ready"))
        loaded2 = ctx.enter_context(nc.semaphore("loaded2"))
        bt = ctx.enter_context(nc.sbuf_tensor("beta_t", [P, 4, H], F32))
        turned = ctx.enter_context(nc.psum_tensor("turned_w", [P, 4, D], F32))
        loaded = ctx.enter_context(nc.semaphore("loaded"))
        ident_ready = ctx.enter_context(nc.semaphore("ident_ready"))
        turned_ready = ctx.enter_context(nc.semaphore("turned_ready"))
        shape_step = ctx.enter_context(nc.semaphore("shape_step"))
        const_ready = ctx.enter_context(nc.semaphore("const_ready"))
        n_loads = 9 + B
        n_loads2 = 22
        block = ctx.enter_context(nc.Block())

        @block.sync
        def _(sp):
            for i, name in enumerate(("Wq", "Wk", "Wv", "Wo")):
                sp.dma_start(raw[:, i, :], a[f"L0_attn_{name}"]).then_inc(loaded, 16)
            for key in ("bq", "bk"):
                sp.dma_start(w[key][:, :], a[f"L0_attn_{key}"].rearrange("(p o) -> p o", o=1)).then_inc(loaded, 16)
            sp.dma_start(w["bv"][:, :], a["L0_attn_bv"].partition_broadcast(P)).then_inc(loaded, 16)
            sp.dma_start(bt[:, 0, :], a["L0_attn_beta"].partition_broadcast(P)).then_inc(loaded, 16)
            sp.dma_start(bt[:, 1, :], a["L0_attn_t"].partition_broadcast(P)).then_inc(loaded, 16)
            for b in range(B):
                sp.dma_start(w["x"][:, b * TB:(b + 1) * TB, :],
                             a["L0_attn_x"][b].rearrange("(t p) d -> p t d", p=P)).then_inc(loaded, 16)

        @block.scalar
        def _(act):
            def rows_of(name):
                return a[name].partition_broadcast(P)

            def column(name):
                return a[name].rearrange("(p o) -> p o", o=1)

            routers, leaves = a["L1_ffn_routers"], a["L1_ffn_leaf_values"]
            for dst, src in (
                (tree[:, 0, :], routers[0:P, :]), (tree[0:NODES - P, 1, :], routers[P:NODES, :]),
                (tree[:, 2, :], leaves[0:P, :]), (tree[:, 3, :], leaves[P:LEAVES, :]),
                (tree[:, 4, :], a["L1_ffn_Wout_w"]), (tree[:, 5, :], a["L1_ffn_Wq"]),
                (w["bo"][:, :], rows_of("L0_attn_bo")), (w["ln_w"][:, :], rows_of("L0_attn_ln_w")),
                (w["ln_b"][:, :], rows_of("L0_attn_ln_b")), (w["gate"][:, :], a["L0_ffn_gate_w"]),
                (w["gate_b"][:, :], rows_of("L0_ffn_gate_b")),
                (w["experts"][:, :, :], a["L0_ffn_expert_w"].rearrange("e i o -> i e o")),
                (w["expert_b"][:, :], a["L0_ffn_expert_b"]),
                (w["qkv1"][:, 0, :], a["L1_attn_wq"]), (w["qkv1"][:, 1, :], a["L1_attn_wk"]),
                (w["qkv1"][:, 2, :], a["L1_attn_wv"]),
                (w["b1"][:, 0:1], column("L1_attn_bq")), (w["b1"][:, 1:2], column("L1_attn_bk")),
                (w["bv1"][:, :], rows_of("L1_attn_bv")), (w["wo1"][:, :], a["L1_attn_wo"]),
                (w["bo1"][:, :], rows_of("L1_attn_bo")), (w["bout"][:, :], rows_of("L1_ffn_Wout_b")),
            ):
                act.dma_start(dst, src).then_inc(loaded2, 16)

        @block.gpsimd
        def _(pool):
            pool.memset(w["ident"][:, :], 0.0).then_inc(const_ready, 1)
            pool.wait_ge(const_ready, 1)
            pool.affine_select(out=w["ident"][:, :], in_=w["ident"][:, :], compare_op=ALU.not_equal, fill=1.0,
                               base=0, pattern=[[-1, P]], channel_multiplier=1).then_inc(ident_ready, 1)
            pool.memset(w["eps"][:, :], EPS)
            pool.memset(w["causal"][:, :], 0.0).then_inc(const_ready, 1)
            pool.wait_ge(const_ready, 2)
            pool.affine_select(out=w["causal"][:, :], in_=w["causal"][:, :], compare_op=ALU.is_ge,
                               fill=MASKED * float(DA) ** 0.5, base=0, pattern=[[-1, P]], channel_multiplier=1)\
                .then_inc(const_ready, 1)
            pool.memset(w["v"][:, :, :, DH:COLS], 2.0)

        @block.tensor
        def _(pe):
            pe.wait_ge(ident_ready, 1)
            pe.wait_ge(loaded, 16 * n_loads)
            for i in range(4):
                pe.transpose(turned[:, i, :], raw[:, i, :], w["ident"][:, :]).then_inc(turned_ready, 1)
            pe.wait_ge(loaded2, 16 * n_loads2)
            for i in range(5):
                rows = NODES - P if i == 1 else P
                pe.transpose(turned_tree[:, i // 4, i % 4, 0:rows], tree[0:rows, i, :], w["ident"][0:rows, 0:rows])\
                  .then_inc(turned_ready, 1)
            pe.wait_ge(tree_ready, 2)
            pe.matmul(made[:, 0, 0:NODES], tree[:, 5, :],
                      tree_t[:, 0:2, :].rearrange("p i d -> p (i d)")[:, 0:NODES], start=True, stop=True)\
              .then_inc(made_ready, 1)
            for i in range(2):
                pe.matmul(made[:, 1, i * D:(i + 1) * D], tree_t[:, 2 + i, :], tree_t[:, 4, :], start=True, stop=True)\
                  .then_inc(made_ready, 1)

        @block.vector
        def _(dve):
            dve.wait_ge(loaded, 16 * n_loads)
            dve.tensor_scalar(bt[:, 0, :], bt[:, 0, :], float(DH) ** 0.5, None, ALU.mult).then_inc(shape_step, 1)
            dve.wait_ge(shape_step, 1)
            dve.tensor_tensor(bt[:, 1, :], bt[:, 0, :], bt[:, 1, :], ALU.mult).then_inc(shape_step, 1)
            dve.wait_ge(shape_step, 2)
            dve.tensor_tensor(bt[:, 2, :], bt[:, 0, :], bt[:, 0, :], ALU.mult).then_inc(shape_step, 1)
            dve.tensor_tensor(bt[:, 3, :], bt[:, 1, :], bt[:, 1, :], ALU.mult).then_inc(shape_step, 1)
            dve.wait_ge(shape_step, 4)
            for b in range(B):
                dve.tensor_scalar(w["shape"][:, b * H:(b + 1) * H, 0], bt[:, 0, :], 2.0, None, ALU.mult)
                dve.tensor_tensor(w["shape"][:, b * H:(b + 1) * H, 1], bt[:, 2, :], bt[:, 3, :], ALU.add)
            dve.wait_ge(turned_ready, 4)
            dve.tensor_copy(w["wt"][:, :, :], turned[:, :, :])
            dve.wait_ge(turned_ready, 9)
            dve.tensor_copy(tree_t[:, 0:4, :].rearrange("p i d -> p (i d)")[:, 0:NODES],
                            turned_tree[:, 0, :, :].rearrange("p i d -> p (i d)")[:, 0:NODES])
            dve.tensor_copy(tree_t[:, 2:4, :], turned_tree[:, 0, 2:4, :]).then_inc(tree_ready, 1)
            dve.tensor_copy(tree_t[:, 4, :], turned_tree[:, 1, 0, :]).then_inc(tree_ready, 1)
            dve.wait_ge(made_ready, 3)
            dve.tensor_copy(w["router"][:, :], made[:, 0, 0:NODES])
            dve.tensor_copy(w["leaf"][:, :, :].rearrange("p i d -> p (i d)"), made[:, 1, 0:2 * D])


def project_heads(nc, a, w):
    with ExitStack() as ctx:
        def sb(name, shape, dt=F32):
            return ctx.enter_context(nc.sbuf_tensor(name, shape, dt))

        def sem(name):
            return ctx.enter_context(nc.semaphore(name))

        stats = sb("stats", [P, TB, 6])
        mv = sb("mean_var", [P, TB, 2])
        rstd = sb("rstd", [P, TB])
        lnv = sb("ln_var", [P, TB])
        h = sb("h", [P, TB, D])
        ht = sb("h_turned", [P, N])
        qk = sb("qk", [P, 2, N])
        rest = sb("rest", [P, 2, N])
        parts = sb("parts", [P, 2, PARTS, N], BF16)
        pt = ctx.enter_context(nc.psum_tensor("ps_turn", [P, 2, HALF], F32))
        pq = ctx.enter_context(nc.psum_tensor("ps_qk", [P, 2, 2, HALF], F32))
        pv = ctx.enter_context(nc.psum_tensor("ps_v", [P, 2, HALF], F32))
        stats_ready = sem("stats_ready")
        mv_ready = sem("mv_ready")
        ln_ready = sem("ln_ready")
        rstd_ready = sem("rstd_ready")
        h_ready = sem("h_ready")
        turned = sem("turned")
        ht_ready = sem("ht_ready")
        proj_ready = sem("proj_ready")
        qk_ready = sem("qk_ready")
        split_step = sem("split_step")
        v_ready = sem("v_ready")
        v_done = sem("v_done")
        stored = sem("stored")
        x_done = sem("x_done")
        n_stores = 2 * PARTS
        block = ctx.enter_context(nc.Block())

        @block.vector
        def _(dve):
            with dve.Fori(0, B) as b:
                for t in range(TB):
                    dve.bn_stats(stats[:, t, :], w["x"][:, bass.ds(b * TB + t, 1), :].rearrange("p o d -> p (o d)"))\
                       .then_inc(stats_ready, 1)
                dve.wait_ge(ln_ready, b)
                dve.wait_ge(h_ready, b * TB)
                dve.wait_ge(stats_ready, b * TB + TB)
                alone(dve, w["dve_passed"])
                for t in range(TB):
                    dve.bn_aggr(mv[:, t, :], stats[:, t, :]).then_inc(mv_ready, 1)
                dve.wait_ge(mv_ready, b * TB + TB)
                dve.wait_ge(rstd_ready, b + 1)
                dve.wait_ge(turned, b * TB)
                dve.wait_ge(x_done, b)
                for t in range(TB):
                    dve.tensor_scalar(h[:, t, :], w["x"][:, bass.ds(b * TB + t, 1), :].rearrange("p o d -> p (o d)"),
                                      mv[:, t, 0:1], rstd[:, t:t + 1], ALU.subtract, ALU.mult).then_inc(h_ready, 1)
                for g in range(2):
                    dve.wait_ge(v_ready, b * TB + (g + 1) * 4)
                    dst = w["v"][:, bass.ds(b * H, H), 4 * g:4 * g + 4, 0:DH].rearrange("p h t d -> p t h d")
                    dve.tensor_tensor(dst, pv[:, g, :].rearrange("p (t h d) -> p t h d", t=4, h=H),
                                      w["bv"][:, :].rearrange("p (h d) -> p h d", h=H).unsqueeze(1)
                                      .to_broadcast([P, 4, H, DH]), ALU.add).then_inc(v_done, 1)
                dve.wait_ge(stored, b * (16 * n_stores))
                for s in range(2):
                    dve.wait_ge(qk_ready, b * 4 + (2 * s + 2))
                    dve.tensor_copy(parts[:, s, 0, :], qk[:, s, :]).then_inc(split_step, 1)
                    dve.wait_ge(split_step, b * 10 + (5 * s + 1))
                    dve.tensor_tensor(rest[:, s, :], qk[:, s, :], parts[:, s, 0, :], ALU.subtract).then_inc(split_step, 1)
                    dve.wait_ge(split_step, b * 10 + (5 * s + 2))
                    dve.tensor_copy(parts[:, s, 1, :], rest[:, s, :]).then_inc(split_step, 1)
                    dve.wait_ge(split_step, b * 10 + (5 * s + 3))
                    dve.tensor_tensor(parts[:, s, 2, :], rest[:, s, :], parts[:, s, 1, :], ALU.subtract)\
                       .then_inc(split_step, 2)

        @block.scalar
        def _(act):
            act.preload_act_table_set("natural_log_exp_and_others")
            with act.Fori(0, B) as b:
                act.wait_ge(mv_ready, b * TB + TB)
                act.activation(lnv[:, :], mv[:, :, 1], ACT.Ln, bias=w["eps"][:, 0:1]).then_inc(ln_ready, 1)
                act.wait_ge(ln_ready, b + 1)
                act.wait_ge(h_ready, b * TB)
                act.activation(rstd[:, :], lnv[:, :], ACT.Exp, scale=-0.5).then_inc(rstd_ready, 1)
                act.wait_ge(proj_ready, b * 4)
                act.wait_ge(v_ready, b * TB)
                for g in range(2):
                    act.wait_ge(turned, b * TB + 4 * (g + 1))
                    act.activation(ht[:, g * HALF:(g + 1) * HALF], pt[:, g, :], ACT.Copy).then_inc(ht_ready, 1)
                act.wait_ge(split_step, b * 10)
                for s in range(2):
                    for g in range(2):
                        act.wait_ge(proj_ready, b * 4 + (2 * s + g + 1))
                        act.activation(qk[:, s, g * HALF:(g + 1) * HALF], pq[:, s, g, :], ACT.Identity,
                                       bias=w["bq" if s == 0 else "bk"][:, 0:1]).then_inc(qk_ready, 1)

        @block.tensor
        def _(pe):
            with pe.Fori(0, B) as b:
                pe.wait_ge(ht_ready, b * 2)
                for t in range(TB):
                    pe.wait_ge(h_ready, b * TB + (t + 1))
                    pe.transpose(pt[:, t // 4, (t % 4) * P:(t % 4 + 1) * P], h[:, t, :], w["ident"][:, :])\
                      .then_inc(turned, 1)
                pe.wait_ge(ht_ready, b * 2 + 2)
                pe.wait_ge(qk_ready, b * 4)
                for s in range(2):
                    for g in range(2):
                        pe.matmul(pq[:, s, g, :], w["wt"][:, s, :], ht[:, g * HALF:(g + 1) * HALF],
                                  start=True, stop=True).then_inc(proj_ready, 1)
                pe.wait_ge(v_done, b * 2)
                for t in range(TB):
                    pe.matmul(pv[:, t // 4, (t % 4) * P:(t % 4 + 1) * P], ht[:, t * P:(t + 1) * P], w["wt"][:, 2, :],
                              start=True, stop=True).then_inc(v_ready, 1)

        @block.gpsimd
        def _(pool):
            with pool.Fori(0, B) as b:
                pool.wait_ge(h_ready, b * TB + TB)
                xs = w["x"][:, bass.ds(b * TB, TB), :].rearrange("p t d -> p (t d)")
                pool.tensor_tensor(xs, xs, h[:, :, :].rearrange("p t d -> p (t d)"), ALU.add).then_inc(x_done, 1)

        @block.sync
        def _(sp):
            with sp.Fori(0, B) as b:
                for s, scratch in enumerate((w["q_parts"], w["k_parts"])):
                    sp.wait_ge(split_step, b * 10 + 5 * (s + 1))
                    for i in range(PARTS):
                        sp.dma_start(scratch[bass.ds(b * H, H), i], parts[:, s, i, :]).then_inc(stored, 16)
            sp.wait_ge(stored, 16 * n_stores * B)


def attend_heads(nc, a, w):
    with ExitStack() as ctx:
        def sb(name, shape, dt=F32):
            return ctx.enter_context(nc.sbuf_tensor(name, shape, dt))

        def ps(name, shape, dt=F32):
            return ctx.enter_context(nc.psum_tensor(name, shape, dt))

        def sem(name):
            return ctx.enter_context(nc.semaphore(name))

        qop = sb("q_operand", [P, SLOTS, N], BF16)
        kop = sb("k_operand", [P, SLOTS, N], BF16)
        vop = sb("v_operand", [P, SLOTS, TB, COLS])
        shape = sb("shape_operand", [P, SLOTS, 2])
        tau = sb("tau_weights", [P, TAU_RING, N])
        mag = sb("magnitudes", [P, MAG_RING, N])
        run = sb("running_max", [P, SLOTS, N])
        grown = sb("grown", [P, GROWN_RING, N - VEC_COLS])
        sig = sb("sigma_weights", [P, SIG_RING, N])
        rowmax = sb("row_max", [P, TB])
        mrow = sb("max_rows", [TB, 2, P], BF16)
        sums = sb("sums", [P, HALF])
        rden = sb("rden", [P, 4, 4])
        quotient = sb("quotient", [P, 4, 2, DH])

        ps_tau = ps("ps_tau", [P, 2, 2, HALF])
        ps_sig = ps("ps_sig", [P, 2, HALF])
        ps_misc = ps("ps_misc", [P, HALF])
        ps_acc = ps("ps_acc", [P, HALF])

        idle_rows_ready = sem("idle_rows_ready")
        ops_loaded = [sem(f"ops_loaded{slot}") for slot in range(SLOTS)]
        head_copied = sem("head_copied")
        tau_ready, tau_done = sem("tau_scores_ready"), sem("tau_weights_ready")
        sig_ready, mag_ready, run_ready = sem("sig_scores_ready"), sem("magnitudes_ready"), sem("running_max_ready")
        grown_ready = sem("grown_ready")
        sqv_ready, sqp_ready = sem("vector_squares_ready"), sem("pool_squares_ready")
        ln_done, sig_done = sem("logs_ready"), sem("sigma_weights_ready")
        misc_ready, misc_done = sem("misc_ready"), sem("misc_read")
        mrow_ready, mrow_loaded = sem("mrow_ready"), sem("mrow_loaded")
        pv_done, sums_ready = sem("pv_done"), sem("sums_ready")
        acc_set, norm_step = sem("acc_set"), sem("norm_step")

        LOADED = 16 * (PARTS + 1)

        def misc_before(s):
            return 0 if isinstance(s, int) and s <= 1 else s * 4 - 5

        def known(value):
            return isinstance(value, int)

        def wait(eng, signal, value):
            if not known(value) or value > 0:
                eng.wait_ge(signal, value)

        def stages(eng, stage):
            for s in range(SLOTS):
                stage(s, s, 0)
            with eng.Fori(0, LOOPS) as i:
                for k in range(SLOTS, 2 * SLOTS):
                    stage(i * SLOTS + k, k % SLOTS, i + k // SLOTS)
            for s in range((LOOPS + 1) * SLOTS, NH + 2):
                stage(s, s % SLOTS, s // SLOTS)

        def at(s, low, high):
            return not known(s) or low <= s <= high

        def tau_tile(s, slot, j):
            back = 1 if j >= TAU_SHIFT else 2
            if not at(s, back, NH - 1 + back):
                return None
            tile = (j - TAU_SHIFT) % TB
            return s - back, (slot - back) % SLOTS, tile, s * TB + (tile - back * TB)

        block = ctx.enter_context(nc.Block())

        @block.sync
        def _(sp):
            def load(n, slot):
                for i in range(PARTS):
                    sp.dma_start(qop[i * PARTS * DH:(i + 1) * PARTS * DH, slot, :],
                                 w["q_parts"][bass.ds(n, 1), i].to_broadcast([PARTS, DH, N]))\
                      .then_inc(ops_loaded[slot], 16)
                sp.dma_start(kop[0:TERMS, slot, :],
                             w["k_parts"][bass.ds(n, 1)].rearrange("o j d t -> (o j d) t").unsqueeze(0)
                             .to_broadcast([PARTS, PARTS * DH, N])).then_inc(ops_loaded[slot], 16)

            def rows(n, slot, misc_uses):
                wait(sp, mrow_ready, n + 1)
                sp.dma_start(qop[MROW:MROW + 1, slot, :], mrow[:, 0, :]).then_inc(mrow_loaded, 16)
                wait(sp, misc_done, misc_uses)
                sp.dma_start(qop[MROW + 1:MROW + 2, slot, :], mrow[:, 1, :]).then_inc(mrow_loaded, 16)

            def stage(s, slot, turn):
                if at(s, 1, NH):
                    rows(s - 1, (slot - 1) % SLOTS, misc_before(s) + 3)
                if at(s, 2, NH - 2):
                    wait(sp, tau_ready, s * TB - TB)
                    alone(sp, w["sp_passed"])
                    load(s + 1, (slot + 1) % SLOTS)

            sp.wait_ge(idle_rows_ready, 3)
            for n in range(SLOTS):
                load(n, n)
            stages(sp, stage)

        @block.tensor
        def _(pe):
            def turn_running(slot, half, before):
                wait(pe, misc_done, before)
                for t in range(4):
                    q = half * HALF + t * P
                    mm = pe.transpose(ps_misc[:, t * P:(t + 1) * P], run[:, slot, q:q + P], w["ident"][:, :])
                mm.then_inc(misc_ready, 1)

            def turn_maxima(before):
                pe.wait_ge(misc_done, before)
                pe.transpose(ps_misc[0:TB, 0:P], rowmax[:, :], w["ident"][:, :]).then_inc(misc_ready, 1)

            def turn_sums(v, before):
                pe.wait_ge(sums_ready, v + 1)
                pe.wait_ge(misc_done, before)
                for t in range(4):
                    mm = pe.transpose(ps_misc[:, t * P:(t + 1) * P], sums[:, t * P:(t + 1) * P], w["ident"][:, :])
                mm.then_inc(misc_ready, 1)

            def weigh(v, slot, j):
                if j == 0:
                    wait(pe, sums_ready, v)
                    if at(v, 0, NH - 1):
                        pe.wait_ge(head_copied, v * 2 + 2)
                kinds = []
                if at(v, 1, NH):
                    pe.wait_ge(tau_done, v * TB + (j - TB + 1))
                    kinds.append(0)
                if at(v, 0, NH - 1):
                    pe.wait_ge(sig_done, v * (TB // CHUNK) + (j // CHUNK + 1))
                    kinds.append(1)
                for q, (kind, half) in enumerate(PAIRS):
                    if kind in kinds:
                        tile = slot * TB + j
                        weights = tau[:, (tile - TB) % TAU_RING] if kind == 0 else sig[:, tile % SIG_RING]
                        mm = pe.matmul(ps_acc[32 * q:32 * q + COLS, :], vop[:, (slot - 1 + kind) % SLOTS, j, :],
                                       weights[:, half * HALF:(half + 1) * HALF],
                                       start=(j == 0), stop=(j == TB - 1))
                mm.then_inc(pv_done, 1)

            def stage(s, slot, turn):
                before = misc_before(s)
                for j in range(TB):
                    keys = slice(j * P, (j + 1) * P)

                    def sigma_scores(half):
                        wait(pe, run_ready, s * (2 * TB) + (2 * j - 1 + half))
                        pe.matmul(ps_sig[:, half, :], kop[0:SIGMA_ROWS, slot, keys],
                                  qop[0:SIGMA_ROWS, slot, half * HALF:(half + 1) * HALF],
                                  start=True, stop=True).then_inc(sig_ready, 1)

                    if at(s, 0, NH - 1):
                        if j == 0:
                            pe.wait_ge(ops_loaded[slot], turn * LOADED + LOADED)
                        sigma_scores(0)
                    elif j == 0 and at(s, NH, NH):
                        pe.wait_ge(run_ready, 2 * TB * NH)
                    if j == 0 and at(s, 1, NH):
                        turn_running((slot - 1) % SLOTS, 0, before)
                    if tile := tau_tile(s, slot, j):
                        head, head_slot, of, g = tile
                        if of == 0:
                            pe.wait_ge(mrow_loaded, head * 32 + 32)
                        wait(pe, tau_done, g - 1)
                        for half in range(2):
                            mm = pe.matmul(ps_tau[:, of % 2, half, :], kop[:, head_slot, of * P:(of + 1) * P],
                                           qop[:, head_slot, half * HALF:(half + 1) * HALF], start=True, stop=True)
                        mm.then_inc(tau_ready, 1)
                    if at(s, 0, NH - 1):
                        sigma_scores(1)
                    if j < PV_LAG:
                        if at(s, 1, NH + 1):
                            weigh(s - 1, (slot - 1) % SLOTS, j - PV_LAG + TB)
                    elif at(s, 0, NH):
                        weigh(s, slot, j - PV_LAG)
                    if at(s, 1, NH):
                        if j == 0:
                            turn_running((slot - 1) % SLOTS, 1, before + 1)
                        if j == MT_STEP:
                            turn_maxima(before + 2)
                    if j == FT_STEP and at(s, 2, NH + 1):
                        turn_sums(s - 2, before + (3 if at(s, 0, NH) else 0))

            stages(pe, stage)
            turn_sums(NH, misc_before(NH + 1) + 1)

        @block.vector
        def _(dve):
            def half_maxima(half, before):
                dve.wait_ge(misc_ready, before + 1)
                dve.tensor_reduce(rowmax[:, 4 * half:4 * half + 4],
                                  ps_misc[:, :].rearrange("p (t k) -> p t k", t=4), AX.X, ALU.max).then_inc(misc_done, 1)

            def first_part(n, before):
                dve.wait_ge(misc_ready, before + 1)
                wait(dve, mrow_loaded, n * 32)
                dve.tensor_scalar(mrow[:, 0, :], ps_misc[0:TB, 0:P], -1.0, None, ALU.mult).then_inc(mrow_ready, 1)

            def second_part(n):
                dve.wait_ge(mrow_ready, n + 1)
                dve.scalar_tensor_tensor(out=mrow[:, 1, :], in0=ps_misc[0:TB, 0:P], scalar=-1.0, in1=mrow[:, 0, :],
                                         op0=ALU.mult, op1=ALU.subtract).then_inc(misc_done, 1)

            turned = ps_misc[:, :].rearrange("p (t g r) -> p t g r", t=4, g=4)

            def result(n):
                return w["f"][:, bass.ds(n, 1), :, :].rearrange("p o (f t) d -> p t (o f) d", f=2)

            def over(g):
                return rden[:, :, g:g + 2].unsqueeze(3).to_broadcast([P, 4, 2, DH])

            def invert(v, before):
                dve.wait_ge(misc_ready, before + 1)
                wait(dve, norm_step, v * 2)
                dve.reciprocal(rden[:, :, :], turned[:, :, :, DH]).then_inc(norm_step, 1)

            def divide(v):
                dve.wait_ge(norm_step, v * 2 + 1)
                if at(v, 0, NH - 1):
                    dve.tensor_tensor(result(v), turned[:, :, 2:4, 0:DH], over(2), ALU.mult)
                dve.tensor_tensor(quotient[:, :, :, :], turned[:, :, 0:2, 0:DH] if at(v, 1, NH)
                                  else turned[:, :, 2:4, 0:DH], over(0) if at(v, 1, NH) else over(2),
                                  ALU.mult).then_inc(misc_done, 1)

            def complete(v, before):
                dve.wait_ge(misc_done, before + 1)
                if at(v, 1, NH):
                    dve.tensor_tensor(result(v - 1), result(v - 1), quotient[:, :, :, :], ALU.add).then_inc(norm_step, 1)
                else:
                    dve.tensor_copy(result(v), quotient[:, :, :, :]).then_inc(norm_step, 1)

            def stage(s, slot, turn):
                before = misc_before(s)
                if at(s, 0, NH - 1):
                    dve.wait_ge(head_copied, s * 2 + 1)
                for j in range(TB):
                    tile = slot * TB + j

                    def magnitude(half):
                        dve.wait_ge(sig_ready, s * (2 * TB) + (2 * j + half + 1))
                        if half == 0:
                            wait(dve, sqv_ready, s * TB + (j - MAG_RING + 1))
                            wait(dve, sqp_ready, s * TB + (j - MAG_RING + 1))
                        cols = slice(half * HALF, (half + 1) * HALF)
                        dve.tensor_scalar(mag[:, tile % MAG_RING, cols].bitcast(I32),
                                          ps_sig[:, half, :].bitcast(I32), SIGN_OFF, None, ALU.bitwise_and)\
                           .then_inc(mag_ready, 1)
                        if j == 0:
                            dve.tensor_copy(run[:, slot, cols], ps_sig[:, half, :]).then_inc(run_ready, 1)
                        else:
                            dve.wait_ge(run_ready, s * (2 * TB) + (2 * j - 1 + half))
                            dve.tensor_tensor(run[:, slot, cols], ps_sig[:, half, :], run[:, slot, cols], ALU.max)\
                               .then_inc(run_ready, 1)

                    if at(s, 0, NH - 1):
                        magnitude(0)
                    if j == 0 and at(s, 1, NH):
                        half_maxima(0, before)
                    if j == MT_STEP + 1 and at(s, 1, NH):
                        first_part(s - 1, before + 2)
                    sums_use = before + (3 if at(s, 0, NH) else 0)
                    if j == FT_STEP + 1 and at(s, 2, NH + 1):
                        invert(s - 2, sums_use)
                    if j == FT_STEP + 2 and at(s, 2, NH + 1):
                        complete(s - 2, sums_use)
                    if at(s, 0, NH - 1):
                        magnitude(1)
                    if at(s, 1, NH):
                        if j == 0:
                            half_maxima(1, before + 1)
                        if j == MT_STEP + 1:
                            second_part(s - 1)
                    if j == FT_STEP + 1 and at(s, 2, NH + 1):
                        divide(s - 2)
                    if at(s, 0, NH - 1):
                        dve.wait_ge(mag_ready, s * (2 * TB) + (2 * j + 1))
                        wait(dve, pv_done, s * TB + (j - SIG_RING + 1))
                        u = mag[:, tile % MAG_RING, 0:VEC_COLS]
                        dve.scalar_tensor_tensor(out=sig[:, tile % SIG_RING, 0:VEC_COLS], in0=u,
                                                 scalar=shape[:, slot, 0:1], in1=u, op0=ALU.add, op1=ALU.mult)\
                           .then_inc(sqv_ready, 1)

            dve.memset(ps_acc[:, :], 0.0).then_inc(acc_set, 1)
            stages(dve, stage)
            invert(NH, misc_before(NH + 1) + 1)
            divide(NH)
            complete(NH, misc_before(NH + 1) + 1)

        @block.scalar
        def _(act):
            def chunk(n, slot, c):
                first = (slot * TB + c * CHUNK) % SIG_RING
                tile = sig[:, first:first + CHUNK, :]
                act.wait_ge(sqv_ready, n * TB + (c * CHUNK + CHUNK))
                act.wait_ge(sqp_ready, n * TB + (c * CHUNK + CHUNK))
                act.activation(tile, tile, ACT.Ln, bias=shape[:, slot, 1:2]).then_inc(ln_done, 1)
                act.wait_ge(ln_done, n * (TB // CHUNK) + (c + 1))
                act.activation(tile, tile, ACT.Exp, scale=-1.0).then_inc(sig_done, 1)

            def take_sums(v):
                act.wait_ge(pv_done, v * TB + TB)
                act.activation(sums[:, :], ps_acc[:, :], ACT.Copy).then_inc(sums_ready, 1)

            def stage(s, slot, turn):
                for j in range(TB):
                    if j == SUMS_STEP and at(s, 1, NH + 1):
                        wait(act, misc_done, misc_before(s) if at(s, 2, NH + 1) else 0)
                        take_sums(s - 1)
                    if tile := tau_tile(s, slot, j):
                        head, head_slot, of, g = tile
                        act.wait_ge(tau_ready, g + 1)
                        wait(act, pv_done, g + (TB - TAU_RING + 1))
                        act.activation(tau[:, (head_slot * TB + of) % TAU_RING, :],
                                       ps_tau[:, of % 2, :, :].rearrange("p h q -> p (h q)"),
                                       ACT.Exp, scale=float(DH) ** -0.5).then_inc(tau_done, 1)
                    if j % CHUNK == 1:
                        c = (j - CHUNK_LAG) // CHUNK
                        if c >= 0:
                            if at(s, 0, NH - 1):
                                chunk(s, slot, c)
                        elif at(s, 1, NH):
                            chunk(s - 1, (slot - 1) % SLOTS, c + TB // CHUNK)

            act.preload_act_table_set("natural_log_exp_and_others")
            act.wait_ge(acc_set, 1)
            stages(act, stage)

        @block.gpsimd
        def _(pool):
            def copy_shape(n, slot):
                pool.tensor_copy(shape[:, slot, :], w["shape"][:, bass.ds(n, 1), :].rearrange("p o c -> p (o c)"))\
                    .then_inc(head_copied, 1)

            def grow(s, slot, j):
                pool.wait_ge(mag_ready, s * (2 * TB) + (2 * j + 2))
                wait(pool, sqp_ready, s * TB + (j - GROWN_RING + 1))
                alone(pool, w["pool_passed"])
                tile = slot * TB + j
                u = mag[:, tile % MAG_RING, VEC_COLS:N]
                pool.tensor_scalar(grown[:, tile % GROWN_RING, :], u, 1.0, shape[:, slot, 0:1], ALU.mult, ALU.add)\
                    .then_inc(grown_ready, 1)

            def stage(s, slot, turn):
                if not at(s, 0, NH - 1):
                    return
                for j in range(TB):
                    tile = slot * TB + j
                    if j == 2:
                        if at(s, 2, NH):
                            wait(pool, pv_done, s * TB - TB)
                            alone(pool, w["pool_passed"])
                        pool.tensor_copy(vop[:, slot, :, :], w["v"][:, bass.ds(s, 1), :, :]
                                         .rearrange("p o t c -> p (o t) c")).then_inc(head_copied, 1)
                        if at(s, 0, NH - 2):
                            copy_shape(s + 1, (slot + 1) % SLOTS)
                    if j + 1 < TB:
                        grow(s, slot, j + 1)
                    elif at(s, 0, NH - 2):
                        pool.wait_ge(head_copied, s * 2 + 3)
                        grow(s + 1, (slot + 1) % SLOTS, 0)
                    wait(pool, pv_done, s * TB + (j - SIG_RING + 1))
                    pool.wait_ge(grown_ready, s * TB + (j + 1))
                    u = mag[:, tile % MAG_RING, VEC_COLS:N]
                    pool.tensor_tensor(sig[:, tile % SIG_RING, VEC_COLS:N], u, grown[:, tile % GROWN_RING, :], ALU.mult)\
                        .then_inc(sqp_ready, 1)

            pool.memset(qop[:, :, :], 0.0).then_inc(idle_rows_ready, 1)
            pool.memset(kop[:, :, :], 0.0).then_inc(idle_rows_ready, 1)
            pool.wait_ge(idle_rows_ready, 2)
            pool.memset(kop[MROW:MROW + 2, :, :], 1.0).then_inc(idle_rows_ready, 1)
            pool.wait_ge(idle_rows_ready, 3)
            copy_shape(0, 0)
            pool.wait_ge(head_copied, 1)
            grow(0, 0, 0)
            stages(pool, stage)


def take_stats(dve, tile_of, stats, mv, stats_ready, mv_ready, before, passed):
    for t in range(TB):
        dve.bn_stats(stats[:, t, :], tile_of(t)).then_inc(stats_ready, 1)
    dve.wait_ge(stats_ready, before + TB)
    alone(dve, passed)
    for t in range(TB):
        dve.bn_aggr(mv[:, t, :], stats[:, t, :]).then_inc(mv_ready, 1)


def take_rstd(act, w, mv, lnv, rstd, mv_ready, ln_ready, rstd_ready, turn):
    act.wait_ge(mv_ready, turn * TB + TB)
    act.activation(lnv[:, :], mv[:, :, 1], ACT.Ln, bias=w["eps"][:, 0:1]).then_inc(ln_ready, 1)
    act.wait_ge(ln_ready, turn + 1)
    act.activation(rstd[:, :], lnv[:, :], ACT.Exp, scale=-0.5).then_inc(rstd_ready, 1)


def four(rows):
    return rows[:, :].unsqueeze(1).to_broadcast([P, 4, rows.shape[-1]])


def mix_experts(nc, w):
    with ExitStack() as ctx:
        def sb(name, shape, dt=F32):
            return ctx.enter_context(nc.sbuf_tensor(name, shape, dt))

        def sem(name):
            return ctx.enter_context(nc.semaphore(name))

        f = sb("f_tile", [P, TB, H, DH])
        turned_sb = sb("turned_sb", [P, 2, N])
        y = sb("y", [P, TB, D])
        yn = sb("y_normed", [P, TB, D])
        z = sb("z", [P, TB, D])
        stats = sb("stats_m", [P, 2, TB, 6])
        mv = sb("mv_m", [P, 2, TB, 2])
        lnv = sb("lnv_m", [P, 2, TB])
        rstd = sb("rstd_m", [P, 2, TB])
        lg = sb("gate_logits", [P, TB, E])
        top = sb("gate_max", [P, TB])
        prob = sb("gate_prob", [P, TB, E])
        total = sb("gate_sum", [P, 2, TB])
        inv = sb("gate_inverse", [P, 2, TB])
        kept = sb("gate_kept", [P, TB, E])
        guard = sb("gate_guard", [P, TB])
        weight = sb("gate_weight", [P, TB, E])
        weight_t = sb("gate_weight_t", [E, N])
        ps_t = ctx.enter_context(nc.psum_tensor("ps_mt", [P, 2, HALF], F32))
        ps_y = ctx.enter_context(nc.psum_tensor("ps_my", [P, 2, HALF], F32))
        ps_e = ctx.enter_context(nc.psum_tensor("ps_me", [P, 2, 2, HALF], F32))

        f_copied = sem("f_copied")
        turned, turned_read = sem("m_turned"), sem("m_turned_read")
        y_ready, y_biased = sem("y_ready"), sem("y_biased")
        stats_ready, mv_ready = [sem(f"m_stats{i}") for i in range(2)], [sem(f"m_mv{i}") for i in range(2)]
        ln_ready, rstd_ready = [sem(f"m_ln{i}") for i in range(2)], [sem(f"m_rstd{i}") for i in range(2)]
        yn_ready, x_biased, x_ready, z_ready = sem("yn_ready"), sem("x_biased"), sem("m_x_ready"), sem("m_z_ready")
        gate_ready, gate_step, exp_ready = sem("gate_ready"), sem("gate_step"), sem("gate_exp")
        bias_ready, e_ready, e_step = sem("expert_bias_ready"), sem("e_ready"), sem("e_step")
        GATE = 11
        E_STEPS = TB * E + 2
        block = ctx.enter_context(nc.Block())

        def xt(b, t):
            return w["x"][:, bass.ds(b * TB + t, 1), :].rearrange("p o d -> p (o d)")

        @block.scalar
        def _(act):
            act.preload_act_table_set("natural_log_exp_and_others")
            with act.Fori(0, B) as b:
                act.wait_ge(turned, b * 3 * TB)
                act.activation(f[:, :, :, :].rearrange("p t h d -> p h t d"), w["f"][:, bass.ds(b * H, H), :, :], ACT.Copy).then_inc(f_copied, 1)
                for use in range(2):
                    if use == 1:
                        take_rstd(act, w, mv[:, 0], lnv[:, 0], rstd[:, 0], mv_ready[0], ln_ready[0], rstd_ready[0], b)
                        take_rstd(act, w, mv[:, 1], lnv[:, 1], rstd[:, 1], mv_ready[1], ln_ready[1], rstd_ready[1], b)
                    for g in range(2):
                        act.wait_ge(turned, b * 3 * TB + (use * TB + 4 * (g + 1)))
                        act.wait_ge(y_ready if use == 0 else e_ready, b * (TB if use == 0 else 2 * TB))
                        act.activation(turned_sb[:, use, g * HALF:(g + 1) * HALF], ps_t[:, g, :], ACT.Copy)\
                           .then_inc(turned_read, 1)
                act.wait_ge(gate_step, b * GATE + 3)
                act.activation(prob[:, :, :], lg[:, :, :], ACT.Exp).then_inc(exp_ready, 1)
                act.wait_ge(bias_ready, b * TB)
                for g in range(2):
                    act.wait_ge(turned, b * 3 * TB + (2 * TB + 4 * (g + 1)))
                    act.activation(weight_t[:, g * HALF:(g + 1) * HALF], ps_t[0:E, g, :], ACT.Copy)\
                       .then_inc(turned_read, 1)

        @block.tensor
        def _(pe):
            with pe.Fori(0, B) as b:
                pe.wait_ge(f_copied, b + 1)
                pe.wait_ge(turned_read, b * 6)
                for t in range(TB):
                    pe.transpose(ps_t[:, t // 4, (t % 4) * P:(t % 4 + 1) * P], f[:, t].rearrange("p h d -> p (h d)"),
                                 w["ident"][:, :]).then_inc(turned, 1)
                pe.wait_ge(turned_read, b * 6 + 2)
                pe.wait_ge(e_step, b * E_STEPS)
                for t in range(TB):
                    pe.matmul(ps_y[:, t // 4, (t % 4) * P:(t % 4 + 1) * P], turned_sb[:, 0, t * P:(t + 1) * P],
                              w["wt"][:, 3, :], start=True, stop=True).then_inc(y_ready, 1)
                for t in range(TB):
                    pe.wait_ge(z_ready, b * TB + (t + 1))
                    pe.transpose(ps_t[:, t // 4, (t % 4) * P:(t % 4 + 1) * P], z[:, t, :], w["ident"][:, :])\
                      .then_inc(turned, 1)
                pe.wait_ge(turned_read, b * 6 + 4)
                pe.wait_ge(y_biased, b * 2 + 2)
                for t in range(TB):
                    pe.matmul(ps_y[:, 0, t * E:(t + 1) * E], turned_sb[:, 1, t * P:(t + 1) * P], w["gate"][:, :],
                              start=True, stop=True).then_inc(gate_ready, 1)

                def experts(pair):
                    for half in range(2):
                        pe.wait_ge(e_step, b * E_STEPS + max(0, 2 * E * (pair - 1) + E * (half + 1)))
                        for t in (2 * pair, 2 * pair + 1):
                            pe.matmul(ps_e[:, t % 2, half, :], turned_sb[:, 1, t * P:(t + 1) * P],
                                      w["experts"][:, 4 * half:4 * half + 4, :], start=True, stop=True).then_inc(e_ready, 1)

                experts(0)
                pe.wait_ge(gate_step, b * GATE + GATE)
                for t in range(TB):
                    pe.transpose(ps_t[0:E, t // 4, (t % 4) * P:(t % 4 + 1) * P], weight[:, t, :], w["ident"][:, :])\
                      .then_inc(turned, 1)
                pe.wait_ge(turned_read, b * 6 + 6)
                for t in range(TB):
                    pe.matmul(ps_y[:, t // 4, (t % 4) * P:(t % 4 + 1) * P], weight_t[:, t * P:(t + 1) * P],
                              w["expert_b"][:, :], start=True, stop=True).then_inc(bias_ready, 1)
                for pair in range(1, TB // 2):
                    experts(pair)

        @block.gpsimd
        def _(pool):
            with pool.Fori(0, B) as b:
                for g in range(2):
                    xs = w["x"][:, bass.ds(b * TB + 4 * g, 4), :]
                    pool.tensor_tensor(xs, xs, four(w["ln_b"]), ALU.add).then_inc(x_biased, 1)

        @block.vector
        def _(dve):
            with dve.Fori(0, B) as b:
                dve.wait_ge(yn_ready, b * (TB + 1))
                for g in range(2):
                    dve.wait_ge(y_ready, b * TB + 4 * (g + 1))
                    dve.tensor_tensor(y[:, 4 * g:4 * g + 4, :], ps_y[:, g, :].rearrange("p (t d) -> p t d", t=4),
                                      four(w["bo"]), ALU.add).then_inc(y_biased, 1)
                dve.wait_ge(y_biased, b * 2 + 2)
                take_stats(dve, lambda t: y[:, t, :], stats[:, 0], mv[:, 0], stats_ready[0], mv_ready[0], b * TB, w["dve_passed"])
                dve.wait_ge(mv_ready[0], b * TB + TB)
                dve.wait_ge(rstd_ready[0], b + 1)
                for t in range(TB):
                    dve.tensor_scalar(yn[:, t, :], y[:, t, :], mv[:, 0, t, 0:1], rstd[:, 0, t:t + 1],
                                      ALU.subtract, ALU.mult).then_inc(yn_ready, 1)
                dve.wait_ge(yn_ready, b * (TB + 1) + TB)
                for g in range(2):
                    ins = dve.tensor_tensor(yn[:, 4 * g:4 * g + 4, :], yn[:, 4 * g:4 * g + 4, :], four(w["ln_w"]), ALU.mult)
                ins.then_inc(yn_ready, 1)
                dve.wait_ge(yn_ready, b * (TB + 1) + (TB + 1))
                dve.wait_ge(x_biased, b * 2 + 2)
                xs = w["x"][:, bass.ds(b * TB, TB), :].rearrange("p t d -> p (t d)")
                dve.tensor_tensor(xs, xs, yn[:, :, :].rearrange("p t d -> p (t d)"), ALU.add).then_inc(x_ready, 1)
                dve.wait_ge(x_ready, b + 1)
                alone(dve, w["dve_passed"])
                take_stats(dve, lambda t: xt(b, t), stats[:, 1], mv[:, 1], stats_ready[1], mv_ready[1], b * TB, w["dve_passed"])
                dve.wait_ge(mv_ready[1], b * TB + TB)
                dve.wait_ge(rstd_ready[1], b + 1)
                for t in range(TB):
                    dve.tensor_scalar(z[:, t, :], xt(b, t), mv[:, 1, t, 0:1], rstd[:, 1, t:t + 1],
                                      ALU.subtract, ALU.mult).then_inc(z_ready, 1)
                step = [0]

                def then(ins):
                    ins.then_inc(gate_step, 1)
                    step[0] += 1
                    dve.wait_ge(gate_step, b * GATE + step[0])

                def each(v):
                    return v.unsqueeze(2).to_broadcast([P, TB, E])

                dve.wait_ge(gate_ready, b * TB + TB)
                then(dve.tensor_tensor(lg[:, :, :], ps_y[:, 0, 0:TB * E].rearrange("p (t e) -> p t e", t=TB),
                                       w["gate_b"][:, :].unsqueeze(1).to_broadcast([P, TB, E]), ALU.add))
                then(dve.tensor_reduce(top[:, :], lg[:, :, :], AX.X, ALU.max))
                then(dve.tensor_tensor(lg[:, :, :], lg[:, :, :], each(top[:, :]), ALU.subtract))
                dve.wait_ge(exp_ready, b + 1)
                then(dve.tensor_reduce(total[:, 0, :], prob[:, :, :], AX.X, ALU.add))
                then(dve.reciprocal(inv[:, 0, :], total[:, 0, :]))
                then(dve.tensor_tensor(prob[:, :, :], prob[:, :, :], each(inv[:, 0, :]), ALU.mult))
                then(dve.scalar_tensor_tensor(out=kept[:, :, :], in0=prob[:, :, :], scalar=THRESHOLD, in1=prob[:, :, :],
                                              op0=ALU.is_ge, op1=ALU.mult))
                then(dve.tensor_reduce(total[:, 1, :], kept[:, :, :], AX.X, ALU.add))
                then(dve.scalar_tensor_tensor(out=guard[:, :], in0=total[:, 1, :], scalar=0.0, in1=total[:, 1, :],
                                              op0=ALU.is_equal, op1=ALU.add))
                then(dve.reciprocal(inv[:, 1, :], guard[:, :]))
                then(dve.tensor_tensor(weight[:, :, :], kept[:, :, :], each(inv[:, 1, :]), ALU.mult))
                assert step[0] == GATE
                done = 0
                for pair in range(TB // 2):
                    for e in range(E):
                        for t in (2 * pair, 2 * pair + 1):
                            if e > 0:
                                dve.wait_ge(e_step, b * E_STEPS + (done - 1))
                            if e % 4 == 0:
                                dve.wait_ge(e_ready, b * 2 * TB + (4 * pair + 2 * (e // 4) + t % 2 + 1))
                            dve.scalar_tensor_tensor(out=xt(b, t), in0=ps_e[:, t % 2, e // 4, (e % 4) * D:(e % 4 + 1) * D],
                                                     scalar=weight[:, t, e:e + 1], in1=xt(b, t),
                                                     op0=ALU.mult, op1=ALU.add).then_inc(e_step, 1)
                            done += 1
                dve.wait_ge(e_step, b * E_STEPS + done)
                for g in range(2):
                    dve.wait_ge(bias_ready, b * TB + 4 * (g + 1))
                    xs = w["x"][:, bass.ds(b * TB + 4 * g, 4), :]
                    dve.tensor_tensor(xs, xs, ps_y[:, g, :].rearrange("p (t d) -> p t d", t=4), ALU.add)\
                       .then_inc(e_step, 1)


def attend_causal(nc, w):
    with ExitStack() as ctx:
        def sb(name, shape, dt=F32):
            return ctx.enter_context(nc.sbuf_tensor(name, shape, dt))

        def ps(name, shape, dt=F32):
            return ctx.enter_context(nc.psum_tensor(name, shape, dt))

        def sem(name):
            return ctx.enter_context(nc.semaphore(name))

        stats, mv = sb("stats_c", [P, TB, 6]), sb("mv_c", [P, TB, 2])
        lnv, rstd = sb("lnv_c", [P, TB]), sb("rstd_c", [P, TB])
        z = sb("z_c", [P, TB, D])
        zt = sb("z_turned", [P, N])
        qk = sb("qk_c", [DA, 2, N])
        v = sb("v_c", [P, TB, DA])
        top, shift = sb("top_c", [P, TB]), sb("shift_c", [P, TB])
        prob = sb("prob_c", [P, 2, N])
        total, inv = sb("total_c", [P, TB]), sb("inverse_c", [P, TB])
        prob_t = sb("prob_t", [P, 2, N])
        mixed = sb("mixed", [P, 2, DA])
        mixed_t = sb("mixed_t", [DA, 2, P])
        ps_s = ps("ps_cs", [P, 2, 2, HALF])
        ps_t = ps("ps_ct", [P, 2, HALF])
        ps_o = ps("ps_co", [P, HALF])
        ps_x = ps("ps_cx", [P, HALF])

        stats_ready, mv_ready, ln_ready, rstd_ready = sem("c_stats"), sem("c_mv"), sem("c_ln"), sem("c_rstd")
        z_ready, turned, zt_ready = sem("c_z"), sem("c_turned"), sem("c_zt")
        proj_ready, qk_ready, v_ready, v_done = sem("c_proj"), sem("c_qk"), sem("c_v"), sem("c_v_done")
        s_ready, masked, max_step = sem("c_scores"), sem("c_masked"), sem("c_max")
        exp_ready, p_turned, p_copied = sem("c_exp"), sem("c_p_turned"), sem("c_p_copied")
        o_ready, inv_ready, mixed_ready = sem("c_out"), sem("c_inverse"), sem("c_mixed")
        m_turned, m_copied, add_ready, x_done = sem("c_m_turned"), sem("c_m_copied"), sem("c_add"), sem("c_x_done")
        x_biased = sem("c_x_biased")
        block = ctx.enter_context(nc.Block())

        def xt(b, t):
            return w["x"][:, bass.ds(b * TB + t, 1), :].rearrange("p o d -> p (o d)")

        @block.vector
        def _(dve):
            with dve.Fori(0, B) as b:
                take_stats(dve, lambda t: xt(b, t), stats, mv, stats_ready, mv_ready, b * TB, w["dve_passed"])
                dve.wait_ge(mv_ready, b * TB + TB)
                dve.wait_ge(rstd_ready, b + 1)
                for t in range(TB):
                    dve.tensor_scalar(z[:, t, :], xt(b, t), mv[:, t, 0:1], rstd[:, t:t + 1],
                                      ALU.subtract, ALU.mult).then_inc(z_ready, 1)
                dve.wait_ge(v_ready, b * TB + TB)
                dve.tensor_tensor(v[:, :, :], ps_x[:, :].rearrange("p (t d) -> p t d", t=TB),
                                  w["bv1"][:, :].unsqueeze(1).to_broadcast([P, TB, DA]), ALU.add).then_inc(v_done, 1)

                def weigh(i):
                    dve.wait_ge(exp_ready, b * TB + (i + 1))
                    dve.reciprocal(inv[:, i:i + 1], total[:, i:i + 1]).then_inc(inv_ready, 1)
                    dve.wait_ge(inv_ready, b * TB + (i + 1))
                    dve.wait_ge(o_ready, b * TB + (i + 1))
                    dve.tensor_scalar(mixed[:, i % 2, :], ps_o[:, 0:DA], inv[:, i:i + 1], None, ALU.mult)\
                       .then_inc(mixed_ready, 1)

                def add(i):
                    dve.wait_ge(x_biased, b * 2 + (1 if i < 4 else 2))
                    dve.wait_ge(add_ready, b * TB + (i + 1))
                    dve.tensor_tensor(xt(b, i), xt(b, i), ps_x[:, 0:D], ALU.add).then_inc(x_done, 1)

                def turned_half(i, g):
                    n = min(4, i + 1 - 4 * g)
                    dve.wait_ge(p_turned, b * 12 + (sum(1 + (k >= 4) for k in range(i)) + (g + 1)))
                    dve.tensor_copy(prob_t[:, i % 2, g * HALF:g * HALF + n * P], ps_t[:, g, 0:n * P]).then_inc(p_copied, 1)

                for i in range(TB):
                    dve.wait_ge(s_ready, b * TB + (i + 1))
                    diagonal = ps_s[:, i % 2, i // 4, (i % 4) * P:(i % 4 + 1) * P]
                    dve.tensor_tensor(diagonal, diagonal, w["causal"][:, :], ALU.add).then_inc(masked, 1)
                    dve.wait_ge(masked, b * TB + (i + 1))
                    dve.tensor_reduce(top[:, i:i + 1],
                                      ps_s[:, i % 2, :, :].rearrange("p f k -> p (f k)")[:, 0:(i + 1) * P],
                                      AX.X, ALU.max).then_inc(max_step, 1)
                    dve.wait_ge(max_step, b * 2 * TB + (2 * i + 1))
                    dve.tensor_scalar(shift[:, i:i + 1], top[:, i:i + 1], -float(DA) ** -0.5, None, ALU.mult)\
                       .then_inc(max_step, 1)
                    if i >= 1:
                        for g in range(1 + (i - 1) // 4):
                            turned_half(i - 1, g)
                    if i >= 2:
                        weigh(i - 2)
                    if i >= 3:
                        add(i - 3)
                for g in range(2):
                    turned_half(TB - 1, g)
                for i in (TB - 2, TB - 1):
                    weigh(i)
                    add(i - 1)
                add(TB - 1)
                dve.wait_ge(x_done, b * TB + TB)

        @block.scalar
        def _(act):
            act.preload_act_table_set("natural_log_exp_and_others")
            with act.Fori(0, B) as b:
                take_rstd(act, w, mv, lnv, rstd, mv_ready, ln_ready, rstd_ready, b)
                for g in range(2):
                    act.wait_ge(turned, b * TB + 4 * (g + 1))
                    act.activation(zt[:, g * HALF:(g + 1) * HALF], ps_t[:, g, :], ACT.Copy).then_inc(zt_ready, 1)
                for s in range(2):
                    for g in range(2):
                        act.wait_ge(proj_ready, b * 4 + (2 * s + g + 1))
                        act.activation(qk[:, s, g * HALF:(g + 1) * HALF], ps_s[0:DA, s, g, :], ACT.Identity,
                                       bias=w["b1"][:, s:s + 1]).then_inc(qk_ready, 1)

                def mixed_half(i):
                    act.wait_ge(m_turned, b * TB + (i + 1))
                    act.activation(mixed_t[:, i % 2, :], ps_x[0:DA, P:2 * P], ACT.Copy).then_inc(m_copied, 1)

                for i in range(TB):
                    act.wait_ge(max_step, b * 2 * TB + (2 * i + 2))
                    act.activation(prob[:, i % 2, 0:(i + 1) * P],
                                   ps_s[:, i % 2, :, :].rearrange("p f k -> p (f k)")[:, 0:(i + 1) * P], ACT.Exp,
                                   bias=shift[:, i:i + 1], scale=float(DA) ** -0.5, accum_out=total[:, i:i + 1])\
                       .then_inc(exp_ready, 1)
                    if i >= 2:
                        mixed_half(i - 2)
                mixed_half(TB - 2)
                mixed_half(TB - 1)

        @block.gpsimd
        def _(pool):
            with pool.Fori(0, B) as b:
                pool.wait_ge(z_ready, b * TB + TB)
                for g in range(2):
                    xs = w["x"][:, bass.ds(b * TB + 4 * g, 4), :]
                    pool.tensor_tensor(xs, xs, four(w["bo1"]), ALU.add).then_inc(x_biased, 1)

        @block.tensor
        def _(pe):
            with pe.Fori(0, B) as b:
                for t in range(TB):
                    pe.wait_ge(z_ready, b * TB + (t + 1))
                    if t == 0:
                        pe.wait_ge(p_copied, b * 12)
                    pe.transpose(ps_t[:, t // 4, (t % 4) * P:(t % 4 + 1) * P], z[:, t, :], w["ident"][:, :])\
                      .then_inc(turned, 1)
                pe.wait_ge(zt_ready, b * 2 + 2)
                pe.wait_ge(exp_ready, b * TB)
                for s in range(2):
                    for g in range(2):
                        pe.matmul(ps_s[0:DA, s, g, :], w["qkv1"][:, s, :], zt[:, g * HALF:(g + 1) * HALF],
                                  start=True, stop=True).then_inc(proj_ready, 1)
                pe.wait_ge(x_done, b * TB)
                for t in range(TB):
                    pe.matmul(ps_x[:, t * DA:(t + 1) * DA], zt[:, t * P:(t + 1) * P], w["qkv1"][:, 2, :],
                              start=True, stop=True).then_inc(v_ready, 1)

                def scores(i):
                    if i == 0:
                        pe.wait_ge(qk_ready, b * 4 + 4)
                    else:
                        pe.wait_ge(exp_ready, b * TB + (i - 1))
                    for g in range(1 + i // 4):
                        n = min(4, i + 1 - 4 * g) * P
                        mm = pe.matmul(ps_s[:, i % 2, g, 0:n], qk[:, 0, i * P:(i + 1) * P],
                                       qk[:, 1, g * HALF:g * HALF + n], start=True, stop=True)
                    mm.then_inc(s_ready, 1)

                def turn_weights(i):
                    pe.wait_ge(exp_ready, b * TB + (i + 1))
                    for g in range(1 + i // 4):
                        pe.wait_ge(p_copied, b * 12 + sum(1 + (k >= 4) for k in range(i)))
                        for k in range(4 * g, min(4 * g + 4, i + 1)):
                            mm = pe.transpose(ps_t[:, g, (k % 4) * P:(k % 4 + 1) * P], prob[:, i % 2, k * P:(k + 1) * P],
                                              w["ident"][:, :])
                        mm.then_inc(p_turned, 1)

                def weigh(i):
                    pe.wait_ge(p_copied, b * 12 + sum(1 + (k >= 4) for k in range(i + 1)))
                    if i == 0:
                        pe.wait_ge(v_done, b + 1)
                    pe.wait_ge(mixed_ready, b * TB + i)
                    for k in range(i + 1):
                        mm = pe.matmul(ps_o[:, 0:DA], prob_t[:, i % 2, k * P:(k + 1) * P], v[:, k, :],
                                       start=(k == 0), stop=(k == i))
                    mm.then_inc(o_ready, 1)

                def turn_mixed(i):
                    pe.wait_ge(mixed_ready, b * TB + (i + 1))
                    pe.wait_ge(x_done, b * TB + i)
                    alone(pe, w["pe_passed"])
                    pe.transpose(ps_x[0:DA, P:2 * P], mixed[:, i % 2, :], w["ident"][:, :]).then_inc(m_turned, 1)

                def project(i):
                    pe.wait_ge(m_copied, b * TB + (i + 1))
                    pe.matmul(ps_x[:, 0:D], mixed_t[:, i % 2, :], w["wo1"][:, :], start=True, stop=True)\
                      .then_inc(add_ready, 1)

                scores(0)
                for i in range(TB):
                    if i + 1 < TB:
                        scores(i + 1)
                    turn_weights(i)
                    if i >= 2:
                        turn_mixed(i - 2)
                    if i >= 1:
                        weigh(i - 1)
                    if i >= 2:
                        project(i - 2)
                turn_mixed(TB - 2)
                weigh(TB - 1)
                project(TB - 2)
                turn_mixed(TB - 1)
                project(TB - 1)


def descend_tree(nc, w, out):
    with ExitStack() as ctx:
        def sb(name, shape, dt=F32):
            return ctx.enter_context(nc.sbuf_tensor(name, shape, dt))

        def ps(name, shape, dt=F32):
            return ctx.enter_context(nc.psum_tensor(name, shape, dt))

        def sem(name):
            return ctx.enter_context(nc.semaphore(name))

        stats, mv = sb("stats_d", [P, TB, 6]), sb("mv_d", [P, TB, 2])
        lnv, rstd = sb("lnv_d", [P, TB]), sb("rstd_d", [P, TB])
        z = sb("z_d", [P, TB, D])
        zt = sb("zt_d", [P, N])
        right = sb("right", [P, TB, LEAVES])
        reach = [sb(f"reach{i}", [P, TB, LEAVES]) for i in range(2)]
        reach_t = sb("reach_t", [P, TB, 2, P])
        ps_t = ps("ps_dt", [P, 2, HALF])
        ps_g = ps("ps_dg", [P, 4, HALF])
        ps_x = ps("ps_dx", [P, 2, HALF])
        stats_ready, mv_ready, ln_ready, rstd_ready = sem("d_stats"), sem("d_mv"), sem("d_ln"), sem("d_rstd")
        z_ready, turned, zt_ready = sem("d_z"), sem("d_turned"), sem("d_zt")
        logit_ready, right_ready, level = sem("d_logit"), sem("d_right"), sem("d_level")
        leaf_turned, leaf_copied = sem("d_leaf_turned"), sem("d_leaf_copied")
        add_ready, x_biased, x_done, stored = sem("d_add"), sem("d_x_biased"), sem("d_x_done"), sem("d_stored")
        block = ctx.enter_context(nc.Block())

        def xt(b, t):
            return w["x"][:, bass.ds(b * TB + t, 1), :].rearrange("p o d -> p (o d)")

        LEVELS = 2 * DEPTH

        @block.vector
        def _(dve):
            with dve.Fori(0, B) as b:
                take_stats(dve, lambda t: xt(b, t), stats, mv, stats_ready, mv_ready, b * TB, w["dve_passed"])
                dve.wait_ge(mv_ready, b * TB + TB)
                dve.wait_ge(rstd_ready, b + 1)
                for t in range(TB):
                    dve.tensor_scalar(z[:, t, :], xt(b, t), mv[:, t, 0:1], rstd[:, t:t + 1],
                                      ALU.subtract, ALU.mult).then_inc(z_ready, 1)
                dve.wait_ge(right_ready, b * 4 + 4)
                dve.wait_ge(leaf_turned, b * 4)
                for d in range(DEPTH):
                    n = 2 ** d
                    new = reach[d % 2][:, :, 0:2 * n].rearrange("p t (n s) -> p t n s", s=2)
                    g = right[:, :, n - 1:2 * n - 1]
                    if d == 0:
                        dve.tensor_copy(new[:, :, :, 1], g).then_inc(level, 1)
                        dve.tensor_scalar(new[:, :, :, 0], g, -1.0, 1.0, ALU.mult, ALU.add).then_inc(level, 1)
                    else:
                        old = reach[(d - 1) % 2][:, :, 0:n]
                        dve.wait_ge(level, b * LEVELS + 2 * d)
                        dve.tensor_tensor(new[:, :, :, 1], old, g, ALU.mult).then_inc(level, 1)
                        dve.wait_ge(level, b * LEVELS + (2 * d + 1))
                        dve.tensor_tensor(new[:, :, :, 0], old, new[:, :, :, 1], ALU.subtract).then_inc(level, 1)
                for g in range(2):
                    dve.wait_ge(x_biased, b * 2 + (g + 1))
                    dve.wait_ge(add_ready, b * TB + 4 * (g + 1))
                    xs = w["x"][:, bass.ds(b * TB + 4 * g, 4), :]
                    dve.tensor_tensor(xs, xs, ps_x[:, g, :].rearrange("p (t d) -> p t d", t=4), ALU.add)\
                       .then_inc(x_done, 1)

        @block.scalar
        def _(act):
            with act.Fori(0, B) as b:
                take_rstd(act, w, mv, lnv, rstd, mv_ready, ln_ready, rstd_ready, b)
                for g in range(2):
                    act.wait_ge(turned, b * TB + 4 * (g + 1))
                    act.activation(zt[:, g * HALF:(g + 1) * HALF], ps_t[:, g, :], ACT.Copy).then_inc(zt_ready, 1)
                act.wait_ge(level, b * LEVELS)
                for g in range(4):
                    act.wait_ge(logit_ready, b * TB + 2 * (g + 1))
                    act.activation(right[:, 2 * g:2 * g + 2, 0:NODES],
                                   ps_g[:, g, :].rearrange("p (t n) -> p t n", t=2)[:, :, 0:NODES], ACT.Sigmoid)\
                       .then_inc(right_ready, 1)
                for g in range(4):
                    act.wait_ge(leaf_turned, b * 4 + (g + 1))
                    act.activation(reach_t[:, 2 * g:2 * g + 2, :, :].rearrange("p t i d -> p (t i d)"), ps_g[:, g, :],
                                   ACT.Copy).then_inc(leaf_copied, 1)

        @block.gpsimd
        def _(pool):
            with pool.Fori(0, B) as b:
                pool.wait_ge(z_ready, b * TB + TB)
                for g in range(2):
                    xs = w["x"][:, bass.ds(b * TB + 4 * g, 4), :]
                    pool.tensor_tensor(xs, xs, four(w["bout"]), ALU.add).then_inc(x_biased, 1)

        @block.tensor
        def _(pe):
            with pe.Fori(0, B) as b:
                for t in range(TB):
                    pe.wait_ge(z_ready, b * TB + (t + 1))
                    pe.transpose(ps_t[:, t // 4, (t % 4) * P:(t % 4 + 1) * P], z[:, t, :], w["ident"][:, :])\
                      .then_inc(turned, 1)
                pe.wait_ge(zt_ready, b * 2 + 2)
                pe.wait_ge(leaf_copied, b * 4)
                for t in range(TB):
                    at = (t % 2) * LEAVES
                    pe.matmul(ps_g[:, t // 2, at:at + NODES], zt[:, t * P:(t + 1) * P], w["router"][:, :],
                              start=True, stop=True).then_inc(logit_ready, 1)
                pe.wait_ge(level, b * LEVELS + LEVELS)
                leaves = reach[(DEPTH - 1) % 2]
                for g in range(4):
                    for t in range(2 * g, 2 * g + 2):
                        for i in range(2):
                            at = (t % 2) * LEAVES + i * P
                            mm = pe.transpose(ps_g[:, g, at:at + P], leaves[:, t, i * P:(i + 1) * P], w["ident"][:, :])
                    mm.then_inc(leaf_turned, 1)
                pe.wait_ge(x_done, b * 2)
                for t in range(TB):
                    pe.wait_ge(leaf_copied, b * 4 + (t // 2 + 1))
                    for i in range(2):
                        mm = pe.matmul(ps_x[:, t // 4, (t % 4) * P:(t % 4 + 1) * P], reach_t[:, t, i, :],
                                       w["leaf"][:, i, :], start=(i == 0), stop=(i == 1))
                    mm.then_inc(add_ready, 1)

        @block.sync
        def _(sp):
            with sp.Fori(0, B) as b:
                sp.wait_ge(x_done, b * 2 + 2)
                sp.dma_start(out[bass.ds(b, 1)].rearrange("o (t p) d -> p (o t) d", p=P),
                             w["x"][:, bass.ds(b * TB, TB), :]).then_inc(stored, 16)
            sp.wait_ge(stored, 16 * B)


_INS = ["L0_attn_x"] + [f"L0_attn_{n}" for n in ("Wq", "bq", "Wk", "bk", "Wv", "bv", "Wo", "bo", "beta", "t", "ln_w", "ln_b")]\
    + [f"L0_ffn_{n}" for n in ("gate_w", "gate_b", "expert_w", "expert_b")]\
    + [f"L1_attn_{n}" for n in ("wq", "bq", "wk", "bk", "wv", "bv", "wo", "bo")]\
    + [f"L1_ffn_{n}" for n in ("Wq", "routers", "leaf_keys", "leaf_values", "Wout_w", "Wout_b")]


def kernel(**inputs):
    import numpy as np
    import concourse.bacc as bacc
    from concourse.bass_utils import run_bass_kernel_spmd

    nc = bacc.Bacc("TRN2", target_bir_lowering=False, num_devices=1)
    arrays, drams = {}, {}
    for name in _INS:
        x = np.ascontiguousarray(inputs[name])
        arrays[f"in_{name}"] = x
        drams[name] = nc.dram_tensor(f"in_{name}", x.shape, mybir.dt.from_np(x.dtype), kind="ExternalInput").ap()
    out = nc.dram_tensor("out", (B, N, D), F32, kind="ExternalOutput").ap()
    build(nc, drams, out)
    result = run_bass_kernel_spmd(nc, [arrays], core_ids=[0])
    return result.results[0]["out"]
```

```python
from contextlib import ExitStack

import concourse.bass as bass
from concourse import mybir

F32 = mybir.dt.float32
BF16 = mybir.dt.bfloat16
I32 = mybir.dt.int32
ALU = mybir.AluOpType
ACT = mybir.ActivationFunctionType
AX = mybir.AxisListType

P = 128
B, N, D = 4, 1024, 128
TB = N // P
NT = B * TB
H, DH = 16, 8
NH = B * H
HALF = 512
EPS = 1e-5
SIGN_OFF = 0x7FFFFFFF

E = 8
THRESHOLD = 0.1
DA = 64
DEPTH = 8
LEAVES = 2 ** DEPTH
NODES = LEAVES - 1
MASKED = -100000000000.0

PARTS = 3
TERMS = PARTS * PARTS * DH
MROW = 96
SIGMA_ROWS = 96
SLOTS = 3
TAU_SHIFT = 4
TAU_RING = 6
MAG_RING = 4
VEC_COLS = 176
GROWN_RING = 3
CHUNK = 2
SIG_RING = 12
CHUNK_LAG = 5
PV_LAG = 7
MT_STEP, FT_STEP = 1, 3
SUMS_STEP = 7
LOOPS = (NH - 1) // SLOTS - 1
COLS = DH + 1
PAIRS = [(kind, half) for kind in range(2) for half in range(2)]


def build(nc, a, out):
    with ExitStack() as ctx:
        def sb(name, shape, dt=F32):
            return ctx.enter_context(nc.sbuf_tensor(name, shape, dt))

        def dram(name, shape, dt):
            return nc.dram_tensor(name, shape, dt, kind="Internal").ap()

        w = {}
        w["ident"] = sb("ident", [P, P])
        w["x"] = sb("x_res", [P, NT, D])
        w["wt"] = sb("wt", [P, 4, D])
        w["bq"] = sb("bq_col", [P, 1])
        w["bk"] = sb("bk_col", [P, 1])
        w["bv"] = sb("bv_rows", [P, D])
        w["eps"] = sb("eps", [P, 1])
        w["shape"] = sb("kernel_shape", [P, NH, 2])
        w["v"] = sb("v_heads", [P, NH, TB, COLS])
        w["f"] = sb("f_heads", [P, NH, TB, DH])
        w["bo"] = sb("bo_rows", [P, D])
        w["ln_w"] = sb("ln_w_rows", [P, D])
        w["ln_b"] = sb("ln_b_rows", [P, D])
        w["gate"] = sb("gate", [P, E])
        w["gate_b"] = sb("gate_b_rows", [P, E])
        w["experts"] = sb("experts", [P, E, D])
        w["expert_b"] = sb("expert_b", [E, D])
        w["qkv1"] = sb("qkv1", [P, 3, DA])
        w["b1"] = sb("b1_cols", [DA, 2])
        w["bv1"] = sb("bv1_rows", [P, DA])
        w["wo1"] = sb("wo1", [DA, D])
        w["bo1"] = sb("bo1_rows", [P, D])
        w["causal"] = sb("causal", [P, P])
        w["router"] = sb("router", [P, NODES])
        w["leaf"] = sb("leaf", [P, 2, D])
        w["bout"] = sb("bout_rows", [P, D])
        w["q_parts"] = dram("q_parts", [NH, PARTS, DH, N], BF16)
        w["k_parts"] = dram("k_parts", [NH, PARTS, DH, N], BF16)

        for engine in ("dve", "pool", "sp", "pe", "act"):
            w[f"{engine}_passed"] = ctx.enter_context(nc.semaphore(f"{engine}_passed"))

        w["qop"] = sb("q_operand", [P, SLOTS, N], BF16)
        w["kop"] = sb("k_operand", [P, SLOTS, N], BF16)
        w["ops_loaded"] = [ctx.enter_context(nc.semaphore(f"ops_loaded{slot}")) for slot in range(SLOTS)]
        w["later_loaded"] = ctx.enter_context(nc.semaphore("later_loaded"))
        w["tree_raw"] = sb("tree_raw", [P, 6, D])

        load_weights(nc, a, w)
        project_heads(nc, a, w)
        attend_heads(nc, a, w)
        mix_experts(nc, w)
        attend_causal(nc, w)
        descend_tree(nc, w, out)


def alone(eng, passed):
    eng.sem_inc(passed, 1)


def known(value):
    return isinstance(value, int)


def wait(eng, signal, value):
    if not known(value) or value > 0:
        eng.wait_ge(signal, value)


def rounds(eng, parts):
    leads = [lead for lead, _ in parts]
    first, last = -max(leads), B - 1 - min(leads)
    for r in range(first, -min(leads)):
        for lead, part in parts:
            if r + lead >= 0:
                part(r + lead)
    with eng.Fori(-min(leads), B - max(leads)) as r:
        for lead, part in parts:
            part(r + lead if lead else r)
    for r in range(B - max(leads), last + 1):
        for lead, part in parts:
            if r + lead < B:
                part(r + lead)


def load_weights(nc, a, w):
    with ExitStack() as ctx:
        raw = ctx.enter_context(nc.sbuf_tensor("raw_w", [P, 4, D], F32))
        bt = ctx.enter_context(nc.sbuf_tensor("beta_t", [P, 4, H], F32))
        turned = ctx.enter_context(nc.psum_tensor("turned_w", [P, 4, D], F32))
        loaded = ctx.enter_context(nc.semaphore("loaded"))
        ident_ready = ctx.enter_context(nc.semaphore("ident_ready"))
        turned_ready = ctx.enter_context(nc.semaphore("turned_ready"))
        shape_step = ctx.enter_context(nc.semaphore("shape_step"))
        const_ready = ctx.enter_context(nc.semaphore("const_ready"))
        rows_set = ctx.enter_context(nc.semaphore("rows_set"))
        n_loads = 9 + B
        block = ctx.enter_context(nc.Block())

        @block.sync
        def _(sp):
            for i, name in enumerate(("Wq", "Wk", "Wv", "Wo")):
                sp.dma_start(raw[:, i, :], a[f"L0_attn_{name}"]).then_inc(loaded, 16)
            for key in ("bq", "bk"):
                sp.dma_start(w[key][:, :], a[f"L0_attn_{key}"].rearrange("(p o) -> p o", o=1)).then_inc(loaded, 16)
            sp.dma_start(w["bv"][:, :], a["L0_attn_bv"].partition_broadcast(P)).then_inc(loaded, 16)
            sp.dma_start(bt[:, 0, :], a["L0_attn_beta"].partition_broadcast(P)).then_inc(loaded, 16)
            sp.dma_start(bt[:, 1, :], a["L0_attn_t"].partition_broadcast(P)).then_inc(loaded, 16)
            for b in range(B):
                sp.dma_start(w["x"][:, b * TB:(b + 1) * TB, :],
                             a["L0_attn_x"][b].rearrange("(t p) d -> p t d", p=P)).then_inc(loaded, 16)

        @block.gpsimd
        def _(pool):
            pool.memset(w["ident"][:, :], 0.0).then_inc(const_ready, 1)
            pool.wait_ge(const_ready, 1)
            pool.affine_select(out=w["ident"][:, :], in_=w["ident"][:, :], compare_op=ALU.not_equal, fill=1.0,
                               base=0, pattern=[[-1, P]], channel_multiplier=1).then_inc(ident_ready, 1)
            pool.memset(w["eps"][:, :], EPS)
            pool.memset(w["causal"][:, :], 0.0).then_inc(const_ready, 1)
            pool.wait_ge(const_ready, 2)
            pool.affine_select(out=w["causal"][:, :], in_=w["causal"][:, :], compare_op=ALU.is_ge,
                               fill=MASKED * float(DA) ** 0.5, base=0, pattern=[[-1, P]], channel_multiplier=1)\
                .then_inc(const_ready, 1)
            pool.memset(w["v"][:, :, :, DH:COLS], 2.0)

        @block.tensor
        def _(pe):
            pe.wait_ge(ident_ready, 1)
            pe.wait_ge(loaded, 16 * n_loads)
            for i in range(4):
                pe.transpose(turned[:, i, :], raw[:, i, :], w["ident"][:, :]).then_inc(turned_ready, 1)

        @block.vector
        def _(dve):
            dve.memset(w["qop"][64:P, :, :], 0.0)
            dve.memset(w["kop"][64:P, :, :], 0.0).then_inc(rows_set, 1)
            dve.wait_ge(rows_set, 1)
            dve.memset(w["kop"][MROW:MROW + 2, :, :], 1.0)
            dve.wait_ge(loaded, 16 * n_loads)
            dve.tensor_scalar(bt[:, 0, :], bt[:, 0, :], float(DH) ** 0.5, None, ALU.mult).then_inc(shape_step, 1)
            dve.wait_ge(shape_step, 1)
            dve.tensor_tensor(bt[:, 1, :], bt[:, 0, :], bt[:, 1, :], ALU.mult).then_inc(shape_step, 1)
            dve.wait_ge(shape_step, 2)
            dve.tensor_tensor(bt[:, 2, :], bt[:, 0, :], bt[:, 0, :], ALU.mult).then_inc(shape_step, 1)
            dve.tensor_tensor(bt[:, 3, :], bt[:, 1, :], bt[:, 1, :], ALU.mult).then_inc(shape_step, 1)
            dve.wait_ge(shape_step, 4)
            for b in range(B):
                dve.tensor_scalar(w["shape"][:, b * H:(b + 1) * H, 0], bt[:, 0, :], 2.0, None, ALU.mult)
                dve.tensor_tensor(w["shape"][:, b * H:(b + 1) * H, 1], bt[:, 2, :], bt[:, 3, :], ALU.add)
            dve.wait_ge(turned_ready, 4)
            dve.tensor_copy(w["wt"][:, :, :], turned[:, :, :])


LATER = 22


def load_later(sp, a, w):
    tree = w["tree_raw"]

    def rows_of(name):
        return a[name].partition_broadcast(P)

    def column(name):
        return a[name].rearrange("(p o) -> p o", o=1)

    routers, leaves = a["L1_ffn_routers"], a["L1_ffn_leaf_values"]
    for dst, src in (
        (tree[:, 0, :], routers[0:P, :]), (tree[0:NODES - P, 1, :], routers[P:NODES, :]),
        (tree[:, 2, :], leaves[0:P, :]), (tree[:, 3, :], leaves[P:LEAVES, :]),
        (tree[:, 4, :], a["L1_ffn_Wout_w"]), (tree[:, 5, :], a["L1_ffn_Wq"]),
        (w["bo"][:, :], rows_of("L0_attn_bo")), (w["ln_w"][:, :], rows_of("L0_attn_ln_w")),
        (w["ln_b"][:, :], rows_of("L0_attn_ln_b")), (w["gate"][:, :], a["L0_ffn_gate_w"]),
        (w["gate_b"][:, :], rows_of("L0_ffn_gate_b")),
        (w["experts"][:, :, :], a["L0_ffn_expert_w"].rearrange("e i o -> i e o")),
        (w["expert_b"][:, :], a["L0_ffn_expert_b"]),
        (w["qkv1"][:, 0, :], a["L1_attn_wq"]), (w["qkv1"][:, 1, :], a["L1_attn_wk"]),
        (w["qkv1"][:, 2, :], a["L1_attn_wv"]),
        (w["b1"][:, 0:1], column("L1_attn_bq")), (w["b1"][:, 1:2], column("L1_attn_bk")),
        (w["bv1"][:, :], rows_of("L1_attn_bv")), (w["wo1"][:, :], a["L1_attn_wo"]),
        (w["bo1"][:, :], rows_of("L1_attn_bo")), (w["bout"][:, :], rows_of("L1_ffn_Wout_b")),
    ):
        sp.dma_start(dst, src).then_inc(w["later_loaded"], 16)


def load_operands(sp, w, n, slot):
    qop, kop, done = w["qop"], w["kop"], w["ops_loaded"][slot]
    for i in range(PARTS):
        sp.dma_start(qop[i * PARTS * DH:(i + 1) * PARTS * DH, slot, :],
                     w["q_parts"][bass.ds(n, 1), i].to_broadcast([PARTS, DH, N])).then_inc(done, 16)
    sp.dma_start(kop[0:TERMS, slot, :],
                 w["k_parts"][bass.ds(n, 1)].rearrange("o j d t -> (o j d) t").unsqueeze(0)
                 .to_broadcast([PARTS, PARTS * DH, N])).then_inc(done, 16)


def project_heads(nc, a, w):
    with ExitStack() as ctx:
        def sb(name, shape, dt=F32):
            return ctx.enter_context(nc.sbuf_tensor(name, shape, dt))

        def sem(name):
            return ctx.enter_context(nc.semaphore(name))

        stats = sb("stats", [P, TB, 6])
        mv = sb("mean_var", [P, TB, 2])
        rstd = sb("rstd", [P, TB])
        lnv = sb("ln_var", [P, TB])
        shift = sb("shift", [P, TB])
        h = sb("h", [P, TB, D])
        ht = sb("h_turned", [P, N])
        qk = sb("qk", [P, 2, N])
        rest = sb("rest", [P, 2, N])
        parts = sb("parts", [P, 2, PARTS, N], BF16)
        pt = ctx.enter_context(nc.psum_tensor("ps_turn", [P, 2, HALF], F32))
        pq = ctx.enter_context(nc.psum_tensor("ps_qk", [P, 2, 2, HALF], F32))
        pv = ctx.enter_context(nc.psum_tensor("ps_v", [P, 2, HALF], F32))
        tree = w["tree_raw"]
        tree_t = sb("tree_t", [P, 5, D])
        tree_turned, tree_ready, made_ready = sem("tree_turned"), sem("tree_ready"), sem("made_ready")
        stats_ready = sem("stats_ready")
        mv_ready = sem("mv_ready")
        ln_ready = sem("ln_ready")
        rstd_ready = sem("rstd_ready")
        h_ready = sem("h_ready")
        shift_ready = sem("shift_ready")
        turned = sem("turned")
        ht_ready = sem("ht_ready")
        proj_ready = sem("proj_ready")
        qk_ready = sem("qk_ready")
        split_step = sem("split_step")
        third_ready = [sem(f"third_ready{s}") for s in range(2)]
        v_ready = sem("v_ready")
        v_done = sem("v_done")
        stored = sem("stored")
        x_done = sem("x_done")
        n_stores = 2 * PARTS

        def third_part(eng, s):
            eng.tensor_tensor(parts[:, s, 2, :], rest[:, s, :], parts[:, s, 1, :], ALU.subtract)\
               .then_inc(third_ready[s], 1)

        block = ctx.enter_context(nc.Block())

        @block.vector
        def _(dve):
            def normalise(b):
                for t in range(TB):
                    dve.bn_stats(stats[:, t, :], w["x"][:, bass.ds(b * TB + t, 1), :].rearrange("p o d -> p (o d)"))\
                       .then_inc(stats_ready, 1)
                wait(dve, ln_ready, b)
                wait(dve, h_ready, b * TB)
                wait(dve, stats_ready, b * TB + TB)
                alone(dve, w["dve_passed"])
                for t in range(TB):
                    dve.bn_aggr(mv[:, t, :], stats[:, t, :]).then_inc(mv_ready, 1)
                wait(dve, mv_ready, b * TB + TB)
                take_shift(dve, mv, rstd, shift, rstd_ready, shift_ready, b)

            def split(b):
                for g in range(2):
                    wait(dve, v_ready, b * TB + (g + 1) * 4)
                    dst = w["v"][:, bass.ds(b * H, H), 4 * g:4 * g + 4, 0:DH].rearrange("p h t d -> p t h d")
                    dve.tensor_tensor(dst, pv[:, g, :].rearrange("p (t h d) -> p t h d", t=4, h=H),
                                      w["bv"][:, :].rearrange("p (h d) -> p h d", h=H).unsqueeze(1)
                                      .to_broadcast([P, 4, H, DH]), ALU.add).then_inc(v_done, 1)
                wait(dve, stored, b * (16 * n_stores))
                for s in range(2):
                    wait(dve, qk_ready, b * 4 + (2 * s + 2))
                    dve.tensor_copy(parts[:, s, 0, :], qk[:, s, :]).then_inc(split_step, 1)
                    wait(dve, split_step, b * 6 + (3 * s + 1))
                    dve.tensor_tensor(rest[:, s, :], qk[:, s, :], parts[:, s, 0, :], ALU.subtract).then_inc(split_step, 1)
                    wait(dve, split_step, b * 6 + (3 * s + 2))
                    dve.tensor_copy(parts[:, s, 1, :], rest[:, s, :]).then_inc(split_step, 1)
                    if s == 1:
                        dve.wait_ge(split_step, b * 6 + 6)
                        third_part(dve, s)

            rounds(dve, [(1, normalise), (0, split)])

        @block.scalar
        def _(act):
            act.preload_act_table_set("natural_log_exp_and_others")
            with act.Fori(0, B) as b:
                act.wait_ge(mv_ready, b * TB + TB)
                act.activation(lnv[:, :], mv[:, :, 1], ACT.Ln, bias=w["eps"][:, 0:1]).then_inc(ln_ready, 1)
                act.wait_ge(ln_ready, b + 1)
                act.wait_ge(h_ready, b * TB)
                act.activation(rstd[:, :], lnv[:, :], ACT.Exp, scale=-0.5).then_inc(rstd_ready, 1)
                act.wait_ge(turned, b * TB)
                act.wait_ge(x_done, b)
                normal_tiles(act, w, h, lambda t: w["x"][:, bass.ds(b * TB + t, 1), :].rearrange("p o d -> p (o d)"),
                             rstd, shift, shift_ready, h_ready, b)
                act.wait_ge(proj_ready, b * 4)
                act.wait_ge(v_ready, b * TB)
                for g in range(2):
                    act.wait_ge(turned, b * TB + 4 * (g + 1))
                    act.activation(ht[:, g * HALF:(g + 1) * HALF], pt[:, g, :], ACT.Copy).then_inc(ht_ready, 1)
                act.wait_ge(split_step, b * 6)
                for s in range(2):
                    for g in range(2):
                        act.wait_ge(proj_ready, b * 4 + (2 * s + g + 1))
                        act.activation(qk[:, s, g * HALF:(g + 1) * HALF], pq[:, s, g, :], ACT.Identity,
                                       bias=w["bq" if s == 0 else "bk"][:, 0:1]).then_inc(qk_ready, 1)
            act.wait_ge(tree_turned, 5)
            act.activation(tree_t[:, 0:2, :].rearrange("p i d -> p (i d)")[:, 0:NODES],
                           pt[:, 0, 0:NODES], ACT.Copy).then_inc(tree_ready, 1)
            act.activation(tree_t[:, 2:4, :].rearrange("p i d -> p (i d)"), pt[:, 0, 2 * D:4 * D], ACT.Copy)\
               .then_inc(tree_ready, 1)
            act.activation(tree_t[:, 4, :], pt[:, 1, 0:D], ACT.Copy).then_inc(tree_ready, 1)
            act.wait_ge(made_ready, 3)
            act.activation(w["router"][:, :], pq[:, 0, 0, 0:NODES], ACT.Copy)
            act.activation(w["leaf"][:, :, :].rearrange("p i d -> p (i d)"), pq[:, 0, 1, 0:2 * D], ACT.Copy)

        @block.tensor
        def _(pe):
            with pe.Fori(0, B) as b:
                pe.wait_ge(ht_ready, b * 2)
                for t in range(TB):
                    pe.wait_ge(h_ready, b * TB + (t + 1))
                    pe.transpose(pt[:, t // 4, (t % 4) * P:(t % 4 + 1) * P], h[:, t, :], w["ident"][:, :])\
                      .then_inc(turned, 1)
                pe.wait_ge(ht_ready, b * 2 + 2)
                pe.wait_ge(qk_ready, b * 4)
                for s in range(2):
                    for g in range(2):
                        pe.matmul(pq[:, s, g, :], w["wt"][:, s, :], ht[:, g * HALF:(g + 1) * HALF],
                                  start=True, stop=True).then_inc(proj_ready, 1)
                pe.wait_ge(v_done, b * 2)
                for t in range(TB):
                    pe.matmul(pv[:, t // 4, (t % 4) * P:(t % 4 + 1) * P], ht[:, t * P:(t + 1) * P], w["wt"][:, 2, :],
                              start=True, stop=True).then_inc(v_ready, 1)
            pe.wait_ge(w["later_loaded"], 16 * LATER)
            for i in range(5):
                rows = NODES - P if i == 1 else P
                pe.transpose(pt[:, i // 4, (i % 4) * D:(i % 4) * D + rows], tree[0:rows, i, :],
                             w["ident"][0:rows, 0:rows]).then_inc(tree_turned, 1)
            pe.wait_ge(tree_ready, 3)
            pe.wait_ge(qk_ready, 4 * B)
            pe.matmul(pq[:, 0, 0, 0:NODES], tree[:, 5, :],
                      tree_t[:, 0:2, :].rearrange("p i d -> p (i d)")[:, 0:NODES], start=True, stop=True)\
              .then_inc(made_ready, 1)
            for i in range(2):
                pe.matmul(pq[:, 0, 1, i * D:(i + 1) * D], tree_t[:, 2 + i, :], tree_t[:, 4, :], start=True, stop=True)\
                  .then_inc(made_ready, 1)

        @block.gpsimd
        def _(pool):
            with pool.Fori(0, B) as b:
                pool.wait_ge(h_ready, b * TB + TB)
                xs = w["x"][:, bass.ds(b * TB, TB), :].rearrange("p t d -> p (t d)")
                pool.tensor_tensor(xs, xs, h[:, :, :].rearrange("p t d -> p (t d)"), ALU.add).then_inc(x_done, 1)
                pool.wait_ge(split_step, b * 6 + 3)
                third_part(pool, 0)

        @block.sync
        def _(sp):
            def store(b):
                for s, scratch in enumerate((w["q_parts"], w["k_parts"])):
                    sp.wait_ge(third_ready[s], b + 1)
                    for i in range(PARTS):
                        sp.dma_start(scratch[bass.ds(b * H, H), i], parts[:, s, i, :]).then_inc(stored, 16)

            load_later(sp, a, w)
            store(0)
            sp.wait_ge(stored, 16 * n_stores)
            for n in range(SLOTS):
                load_operands(sp, w, n, n)
            with sp.Fori(1, B) as b:
                store(b)
            sp.wait_ge(stored, 16 * n_stores * B)


def attend_heads(nc, a, w):
    with ExitStack() as ctx:
        def sb(name, shape, dt=F32):
            return ctx.enter_context(nc.sbuf_tensor(name, shape, dt))

        def ps(name, shape, dt=F32):
            return ctx.enter_context(nc.psum_tensor(name, shape, dt))

        def sem(name):
            return ctx.enter_context(nc.semaphore(name))

        qop, kop, ops_loaded = w["qop"], w["kop"], w["ops_loaded"]
        vop = sb("v_operand", [P, SLOTS, TB, COLS])
        shape = sb("shape_operand", [P, SLOTS, 2])
        tau = sb("tau_weights", [P, TAU_RING, N])
        mag = sb("magnitudes", [P, MAG_RING, N])
        run = sb("running_max", [P, SLOTS, N])
        grown = sb("grown", [P, GROWN_RING, N - VEC_COLS])
        sig = sb("sigma_weights", [P, SIG_RING, N])
        rowmax = sb("row_max", [P, TB])
        mrow = sb("max_rows", [TB, 2, P], BF16)
        sums = sb("sums", [P, HALF])
        rden = sb("rden", [P, 4, 4])
        quotient = sb("quotient", [P, 4, 2, DH])

        ps_tau = ps("ps_tau", [P, 2, 2, HALF])
        ps_sig = ps("ps_sig", [P, 2, HALF])
        ps_misc = ps("ps_misc", [P, HALF])
        ps_acc = ps("ps_acc", [P, HALF])

        head_copied = sem("head_copied")
        tau_ready, tau_done = sem("tau_scores_ready"), sem("tau_weights_ready")
        sig_ready, mag_ready, run_ready = sem("sig_scores_ready"), sem("magnitudes_ready"), sem("running_max_ready")
        grown_ready = sem("grown_ready")
        sqv_ready, sqp_ready = sem("vector_squares_ready"), sem("pool_squares_ready")
        ln_done, sig_done = sem("logs_ready"), sem("sigma_weights_ready")
        misc_ready, misc_done = sem("misc_ready"), sem("misc_read")
        mrow_ready, mrow_loaded = sem("mrow_ready"), sem("mrow_loaded")
        pv_done, sums_ready = sem("pv_done"), sem("sums_ready")
        acc_set, norm_step = sem("acc_set"), sem("norm_step")

        LOADED = 16 * (PARTS + 1)

        def misc_before(s):
            return 0 if isinstance(s, int) and s <= 1 else s * 4 - 5

        def stages(eng, stage):
            for s in range(SLOTS):
                stage(s, s, 0)
            with eng.Fori(0, LOOPS) as i:
                for k in range(SLOTS, 2 * SLOTS):
                    stage(i * SLOTS + k, k % SLOTS, i + k // SLOTS)
            for s in range((LOOPS + 1) * SLOTS, NH + 2):
                stage(s, s % SLOTS, s // SLOTS)

        def at(s, low, high):
            return not known(s) or low <= s <= high

        def tau_tile(s, slot, j):
            back = 1 if j >= TAU_SHIFT else 2
            if not at(s, back, NH - 1 + back):
                return None
            tile = (j - TAU_SHIFT) % TB
            return s - back, (slot - back) % SLOTS, tile, s * TB + (tile - back * TB)

        block = ctx.enter_context(nc.Block())

        @block.sync
        def _(sp):
            def rows(n, slot, misc_uses):
                wait(sp, mrow_ready, n + 1)
                sp.dma_start(qop[MROW:MROW + 1, slot, :], mrow[:, 0, :]).then_inc(mrow_loaded, 16)
                wait(sp, misc_done, misc_uses)
                sp.dma_start(qop[MROW + 1:MROW + 2, slot, :], mrow[:, 1, :]).then_inc(mrow_loaded, 16)

            def stage(s, slot, turn):
                if at(s, 1, NH):
                    rows(s - 1, (slot - 1) % SLOTS, misc_before(s) + 3)
                if at(s, 2, NH - 2):
                    wait(sp, tau_ready, s * TB - TB)
                    alone(sp, w["sp_passed"])
                    load_operands(sp, w, s + 1, (slot + 1) % SLOTS)

            stages(sp, stage)

        @block.tensor
        def _(pe):
            def turn_running(slot, half, before):
                wait(pe, misc_done, before)
                for t in range(4):
                    q = half * HALF + t * P
                    mm = pe.transpose(ps_misc[:, t * P:(t + 1) * P], run[:, slot, q:q + P], w["ident"][:, :])
                mm.then_inc(misc_ready, 1)

            def turn_maxima(before):
                pe.wait_ge(misc_done, before)
                pe.transpose(ps_misc[0:TB, 0:P], rowmax[:, :], w["ident"][:, :]).then_inc(misc_ready, 1)

            def turn_sums(v, before):
                pe.wait_ge(sums_ready, v + 1)
                pe.wait_ge(misc_done, before)
                for t in range(4):
                    mm = pe.transpose(ps_misc[:, t * P:(t + 1) * P], sums[:, t * P:(t + 1) * P], w["ident"][:, :])
                mm.then_inc(misc_ready, 1)

            def weigh(v, slot, j):
                if j == 0:
                    wait(pe, sums_ready, v)
                    if at(v, 0, NH - 1):
                        pe.wait_ge(head_copied, v * 2 + 2)
                kinds = []
                if at(v, 1, NH):
                    pe.wait_ge(tau_done, v * TB + (j - TB + 1))
                    kinds.append(0)
                if at(v, 0, NH - 1):
                    pe.wait_ge(sig_done, v * (TB // CHUNK) + (j // CHUNK + 1))
                    kinds.append(1)
                for q, (kind, half) in enumerate(PAIRS):
                    if kind in kinds:
                        tile = slot * TB + j
                        weights = tau[:, (tile - TB) % TAU_RING] if kind == 0 else sig[:, tile % SIG_RING]
                        mm = pe.matmul(ps_acc[32 * q:32 * q + COLS, :], vop[:, (slot - 1 + kind) % SLOTS, j, :],
                                       weights[:, half * HALF:(half + 1) * HALF],
                                       start=(j == 0), stop=(j == TB - 1))
                mm.then_inc(pv_done, 1)

            def stage(s, slot, turn):
                before = misc_before(s)
                for j in range(TB):
                    keys = slice(j * P, (j + 1) * P)

                    def sigma_scores(half):
                        wait(pe, run_ready, s * (2 * TB) + (2 * j - 1 + half))
                        pe.matmul(ps_sig[:, half, :], kop[0:SIGMA_ROWS, slot, keys],
                                  qop[0:SIGMA_ROWS, slot, half * HALF:(half + 1) * HALF],
                                  start=True, stop=True).then_inc(sig_ready, 1)

                    if at(s, 0, NH - 1):
                        if j == 0:
                            pe.wait_ge(ops_loaded[slot], turn * LOADED + LOADED)
                        sigma_scores(0)
                    elif j == 0 and at(s, NH, NH):
                        pe.wait_ge(run_ready, 2 * TB * NH)
                    if j == 0 and at(s, 1, NH):
                        turn_running((slot - 1) % SLOTS, 0, before)
                    if tile := tau_tile(s, slot, j):
                        head, head_slot, of, g = tile
                        if of == 0:
                            pe.wait_ge(mrow_loaded, head * 32 + 32)
                        wait(pe, tau_done, g - 1)
                        for half in range(2):
                            mm = pe.matmul(ps_tau[:, of % 2, half, :], kop[:, head_slot, of * P:(of + 1) * P],
                                           qop[:, head_slot, half * HALF:(half + 1) * HALF], start=True, stop=True)
                        mm.then_inc(tau_ready, 1)
                    if at(s, 0, NH - 1):
                        sigma_scores(1)
                    if j < PV_LAG:
                        if at(s, 1, NH + 1):
                            weigh(s - 1, (slot - 1) % SLOTS, j - PV_LAG + TB)
                    elif at(s, 0, NH):
                        weigh(s, slot, j - PV_LAG)
                    if at(s, 1, NH):
                        if j == 0:
                            turn_running((slot - 1) % SLOTS, 1, before + 1)
                        if j == MT_STEP:
                            turn_maxima(before + 2)
                    if j == FT_STEP and at(s, 2, NH + 1):
                        turn_sums(s - 2, before + (3 if at(s, 0, NH) else 0))

            stages(pe, stage)
            turn_sums(NH, misc_before(NH + 1) + 1)

        @block.vector
        def _(dve):
            def half_maxima(half, before):
                dve.wait_ge(misc_ready, before + 1)
                dve.tensor_reduce(rowmax[:, 4 * half:4 * half + 4],
                                  ps_misc[:, :].rearrange("p (t k) -> p t k", t=4), AX.X, ALU.max).then_inc(misc_done, 1)

            def second_part(n):
                dve.wait_ge(mrow_ready, n + 1)
                dve.scalar_tensor_tensor(out=mrow[:, 1, :], in0=ps_misc[0:TB, 0:P], scalar=-1.0, in1=mrow[:, 0, :],
                                         op0=ALU.mult, op1=ALU.subtract).then_inc(misc_done, 1)

            turned = ps_misc[:, :].rearrange("p (t g r) -> p t g r", t=4, g=4)

            def result(n):
                return w["f"][:, bass.ds(n, 1), :, :].rearrange("p o (f t) d -> p t (o f) d", f=2)

            def over(g):
                return rden[:, :, g:g + 2].unsqueeze(3).to_broadcast([P, 4, 2, DH])

            def invert(v, before):
                dve.wait_ge(misc_ready, before + 1)
                wait(dve, norm_step, v * 2)
                dve.reciprocal(rden[:, :, :], turned[:, :, :, DH]).then_inc(norm_step, 1)

            def divide(v):
                dve.wait_ge(norm_step, v * 2 + 1)
                if at(v, 0, NH - 1):
                    dve.tensor_tensor(result(v), turned[:, :, 2:4, 0:DH], over(2), ALU.mult)
                dve.tensor_tensor(quotient[:, :, :, :], turned[:, :, 0:2, 0:DH] if at(v, 1, NH)
                                  else turned[:, :, 2:4, 0:DH], over(0) if at(v, 1, NH) else over(2),
                                  ALU.mult).then_inc(misc_done, 1)

            def complete(v, before):
                dve.wait_ge(misc_done, before + 1)
                if at(v, 1, NH):
                    dve.tensor_tensor(result(v - 1), result(v - 1), quotient[:, :, :, :], ALU.add).then_inc(norm_step, 1)
                else:
                    dve.tensor_copy(result(v), quotient[:, :, :, :]).then_inc(norm_step, 1)

            def stage(s, slot, turn):
                before = misc_before(s)
                if at(s, 0, NH - 1):
                    dve.wait_ge(head_copied, s * 2 + 1)
                for j in range(TB):
                    tile = slot * TB + j

                    def magnitude(half):
                        dve.wait_ge(sig_ready, s * (2 * TB) + (2 * j + half + 1))
                        if half == 0:
                            wait(dve, sqv_ready, s * TB + (j - MAG_RING + 1))
                            wait(dve, sqp_ready, s * TB + (j - MAG_RING + 1))
                        cols = slice(half * HALF, (half + 1) * HALF)
                        dve.tensor_scalar(mag[:, tile % MAG_RING, cols].bitcast(I32),
                                          ps_sig[:, half, :].bitcast(I32), SIGN_OFF, None, ALU.bitwise_and)\
                           .then_inc(mag_ready, 1)
                        if j == 0:
                            dve.tensor_copy(run[:, slot, cols], ps_sig[:, half, :]).then_inc(run_ready, 1)
                        else:
                            dve.wait_ge(run_ready, s * (2 * TB) + (2 * j - 1 + half))
                            dve.tensor_tensor(run[:, slot, cols], ps_sig[:, half, :], run[:, slot, cols], ALU.max)\
                               .then_inc(run_ready, 1)

                    if at(s, 0, NH - 1):
                        magnitude(0)
                    if j == 0 and at(s, 1, NH):
                        half_maxima(0, before)
                    sums_use = before + (3 if at(s, 0, NH) else 0)
                    if j == FT_STEP + 1 and at(s, 2, NH + 1):
                        invert(s - 2, sums_use)
                    if j == FT_STEP + 2 and at(s, 2, NH + 1):
                        complete(s - 2, sums_use)
                    if at(s, 0, NH - 1):
                        magnitude(1)
                    if at(s, 1, NH):
                        if j == 0:
                            half_maxima(1, before + 1)
                        if j == MT_STEP + 1:
                            second_part(s - 1)
                    if j == FT_STEP + 1 and at(s, 2, NH + 1):
                        divide(s - 2)
                    if at(s, 0, NH - 1):
                        dve.wait_ge(mag_ready, s * (2 * TB) + (2 * j + 1))
                        wait(dve, pv_done, s * TB + (j - SIG_RING + 1))
                        u = mag[:, tile % MAG_RING, 0:VEC_COLS]
                        dve.scalar_tensor_tensor(out=sig[:, tile % SIG_RING, 0:VEC_COLS], in0=u,
                                                 scalar=shape[:, slot, 0:1], in1=u, op0=ALU.add, op1=ALU.mult)\
                           .then_inc(sqv_ready, 1)

            dve.memset(ps_acc[:, :], 0.0).then_inc(acc_set, 1)
            stages(dve, stage)
            invert(NH, misc_before(NH + 1) + 1)
            divide(NH)
            complete(NH, misc_before(NH + 1) + 1)

        @block.scalar
        def _(act):
            def chunk(n, slot, c):
                first = (slot * TB + c * CHUNK) % SIG_RING
                tile = sig[:, first:first + CHUNK, :]
                act.wait_ge(sqv_ready, n * TB + (c * CHUNK + CHUNK))
                act.wait_ge(sqp_ready, n * TB + (c * CHUNK + CHUNK))
                act.activation(tile, tile, ACT.Ln, bias=shape[:, slot, 1:2]).then_inc(ln_done, 1)
                act.wait_ge(ln_done, n * (TB // CHUNK) + (c + 1))
                act.activation(tile, tile, ACT.Exp, scale=-1.0).then_inc(sig_done, 1)

            def first_part(n, before):
                act.wait_ge(misc_ready, before + 1)
                wait(act, mrow_loaded, n * 32)
                act.activation(mrow[:, 0, :], ps_misc[0:TB, 0:P], ACT.Copy, scale=-1.0).then_inc(mrow_ready, 1)

            def take_sums(v):
                act.wait_ge(pv_done, v * TB + TB)
                act.activation(sums[:, :], ps_acc[:, :], ACT.Copy).then_inc(sums_ready, 1)

            def stage(s, slot, turn):
                for j in range(TB):
                    if j == MT_STEP + 1 and at(s, 1, NH):
                        first_part(s - 1, misc_before(s) + 2)
                    if j == SUMS_STEP and at(s, 1, NH + 1):
                        wait(act, misc_done, misc_before(s) if at(s, 2, NH + 1) else 0)
                        take_sums(s - 1)
                    if tile := tau_tile(s, slot, j):
                        head, head_slot, of, g = tile
                        act.wait_ge(tau_ready, g + 1)
                        wait(act, pv_done, g + (TB - TAU_RING + 1))
                        act.activation(tau[:, (head_slot * TB + of) % TAU_RING, :],
                                       ps_tau[:, of % 2, :, :].rearrange("p h q -> p (h q)"),
                                       ACT.Exp, scale=float(DH) ** -0.5).then_inc(tau_done, 1)
                    if j % CHUNK == 1:
                        c = (j - CHUNK_LAG) // CHUNK
                        if c >= 0:
                            if at(s, 0, NH - 1):
                                chunk(s, slot, c)
                        elif at(s, 1, NH):
                            chunk(s - 1, (slot - 1) % SLOTS, c + TB // CHUNK)

            act.preload_act_table_set("natural_log_exp_and_others")
            act.wait_ge(acc_set, 1)
            stages(act, stage)

        @block.gpsimd
        def _(pool):
            def copy_shape(n, slot):
                pool.tensor_copy(shape[:, slot, :], w["shape"][:, bass.ds(n, 1), :].rearrange("p o c -> p (o c)"))\
                    .then_inc(head_copied, 1)

            def grow(s, slot, j):
                pool.wait_ge(mag_ready, s * (2 * TB) + (2 * j + 2))
                wait(pool, sqp_ready, s * TB + (j - GROWN_RING + 1))
                alone(pool, w["pool_passed"])
                tile = slot * TB + j
                u = mag[:, tile % MAG_RING, VEC_COLS:N]
                pool.tensor_scalar(grown[:, tile % GROWN_RING, :], u, 1.0, shape[:, slot, 0:1], ALU.mult, ALU.add)\
                    .then_inc(grown_ready, 1)

            def stage(s, slot, turn):
                if not at(s, 0, NH - 1):
                    return
                for j in range(TB):
                    tile = slot * TB + j
                    if j == 2:
                        if at(s, 2, NH):
                            wait(pool, pv_done, s * TB - TB)
                            alone(pool, w["pool_passed"])
                        pool.tensor_copy(vop[:, slot, :, :], w["v"][:, bass.ds(s, 1), :, :]
                                         .rearrange("p o t c -> p (o t) c")).then_inc(head_copied, 1)
                        if at(s, 0, NH - 2):
                            copy_shape(s + 1, (slot + 1) % SLOTS)
                    if j + 1 < TB:
                        grow(s, slot, j + 1)
                    elif at(s, 0, NH - 2):
                        pool.wait_ge(head_copied, s * 2 + 3)
                        grow(s + 1, (slot + 1) % SLOTS, 0)
                    wait(pool, pv_done, s * TB + (j - SIG_RING + 1))
                    pool.wait_ge(grown_ready, s * TB + (j + 1))
                    u = mag[:, tile % MAG_RING, VEC_COLS:N]
                    pool.tensor_tensor(sig[:, tile % SIG_RING, VEC_COLS:N], u, grown[:, tile % GROWN_RING, :], ALU.mult)\
                        .then_inc(sqp_ready, 1)

            copy_shape(0, 0)
            pool.wait_ge(head_copied, 1)
            grow(0, 0, 0)
            stages(pool, stage)


def take_stats(dve, tile_of, stats, mv, stats_ready, mv_ready, before, passed):
    for t in range(TB):
        dve.bn_stats(stats[:, t, :], tile_of(t)).then_inc(stats_ready, 1)
    dve.wait_ge(stats_ready, before + TB)
    alone(dve, passed)
    for t in range(TB):
        dve.bn_aggr(mv[:, t, :], stats[:, t, :]).then_inc(mv_ready, 1)


def take_rstd(act, w, mv, lnv, rstd, mv_ready, ln_ready, rstd_ready, turn):
    act.wait_ge(mv_ready, turn * TB + TB)
    act.activation(lnv[:, :], mv[:, :, 1], ACT.Ln, bias=w["eps"][:, 0:1]).then_inc(ln_ready, 1)
    act.wait_ge(ln_ready, turn + 1)
    act.activation(rstd[:, :], lnv[:, :], ACT.Exp, scale=-0.5).then_inc(rstd_ready, 1)


def take_shift(dve, mv, rstd, shift, rstd_ready, shift_ready, turn):
    dve.wait_ge(rstd_ready, turn + 1)
    dve.scalar_tensor_tensor(out=shift[:, :], in0=mv[:, :, 0], scalar=-1.0, in1=rstd[:, :],
                             op0=ALU.mult, op1=ALU.mult).then_inc(shift_ready, 1)


def normal_tiles(act, w, out, tile_of, rstd, shift, shift_ready, done, turn):
    act.wait_ge(shift_ready, turn + 1)
    alone(act, w["act_passed"])
    for t in range(TB):
        act.activation(out[:, t, :], tile_of(t), ACT.Identity, bias=shift[:, t:t + 1],
                       scale=rstd[:, t:t + 1]).then_inc(done, 1)


def four(rows):
    return rows[:, :].unsqueeze(1).to_broadcast([P, 4, rows.shape[-1]])


def mix_experts(nc, w):
    with ExitStack() as ctx:
        def sb(name, shape, dt=F32):
            return ctx.enter_context(nc.sbuf_tensor(name, shape, dt))

        def sem(name):
            return ctx.enter_context(nc.semaphore(name))

        f = sb("f_tile", [P, TB, H, DH])
        turned_sb = sb("turned_sb", [P, 2, N])
        y = sb("y", [P, TB, D])
        yn = sb("y_normed", [P, TB, D])
        z = sb("z", [P, TB, D])
        stats = sb("stats_m", [P, 2, TB, 6])
        mv = sb("mv_m", [P, 2, TB, 2])
        lnv = sb("lnv_m", [P, 2, TB])
        rstd = sb("rstd_m", [P, 2, TB])
        lg = sb("gate_logits", [P, TB, E])
        top = sb("gate_max", [P, TB])
        prob = sb("gate_prob", [P, TB, E])
        total = sb("gate_sum", [P, 2, TB])
        inv = sb("gate_inverse", [P, 2, TB])
        kept = sb("gate_kept", [P, TB, E])
        guard = sb("gate_guard", [P, TB])
        weight = sb("gate_weight", [P, TB, E])
        weight_t = sb("gate_weight_t", [E, N])
        ps_t = ctx.enter_context(nc.psum_tensor("ps_mt", [P, 2, HALF], F32))
        ps_y = ctx.enter_context(nc.psum_tensor("ps_my", [P, 2, HALF], F32))
        ps_e = ctx.enter_context(nc.psum_tensor("ps_me", [P, 2, 2, HALF], F32))

        f_copied = sem("f_copied")
        turned, turned_read = sem("m_turned"), sem("m_turned_read")
        y_ready, y_biased = sem("y_ready"), sem("y_biased")
        stats_ready, mv_ready = [sem(f"m_stats{i}") for i in range(2)], [sem(f"m_mv{i}") for i in range(2)]
        ln_ready, rstd_ready = [sem(f"m_ln{i}") for i in range(2)], [sem(f"m_rstd{i}") for i in range(2)]
        yn_ready, x_step, x_ready, z_ready = sem("yn_ready"), sem("x_step"), sem("m_x_ready"), sem("m_z_ready")
        gate_ready, gate_step, exp_ready = sem("gate_ready"), sem("gate_step"), sem("gate_exp")
        bias_ready, bias_added = sem("expert_bias_ready"), sem("expert_bias_added")
        e_ready, e_step = sem("e_ready"), sem("e_step")
        GATE = 11
        block = ctx.enter_context(nc.Block())

        def xt(b, t):
            return w["x"][:, bass.ds(b * TB + t, 1), :].rearrange("p o d -> p (o d)")

        @block.scalar
        def _(act):
            def take_weights(b):
                wait(act, bias_ready, b * TB)
                for g in range(2):
                    act.wait_ge(turned, b * 3 * TB + (2 * TB + 4 * (g + 1)))
                    act.activation(weight_t[:, g * HALF:(g + 1) * HALF], ps_t[0:E, g, :], ACT.Copy)\
                       .then_inc(turned_read, 1)

            def take_turned(b, use, read, before):
                for g in range(2):
                    act.wait_ge(turned, b * 3 * TB + (use * TB + 4 * (g + 1)))
                    wait(act, read, before)
                    act.activation(turned_sb[:, use, g * HALF:(g + 1) * HALF], ps_t[:, g, :], ACT.Copy)\
                       .then_inc(turned_read, 1)

            def normal_and_gate(b):
                wait(act, turned, b * 3 * TB)
                alone(act, w["act_passed"])
                act.activation(f[:, :, :, :].rearrange("p t h d -> p h t d"), w["f"][:, bass.ds(b * H, H), :, :],
                               ACT.Copy).then_inc(f_copied, 1)
                take_turned(b, 0, y_ready, b * TB)
                take_rstd(act, w, mv[:, 0], lnv[:, 0], rstd[:, 0], mv_ready[0], ln_ready[0], rstd_ready[0], b)
                take_rstd(act, w, mv[:, 1], lnv[:, 1], rstd[:, 1], mv_ready[1], ln_ready[1], rstd_ready[1], b)
                take_turned(b, 1, e_ready, b * 2 * TB)
                act.wait_ge(gate_step, b * GATE + 3)
                act.activation(prob[:, :, :], lg[:, :, :], ACT.Exp).then_inc(exp_ready, 1)

            act.preload_act_table_set("natural_log_exp_and_others")
            rounds(act, [(0, take_weights), (1, normal_and_gate)])

        @block.tensor
        def _(pe):
            def project(b):
                pe.wait_ge(f_copied, b + 1)
                wait(pe, turned_read, b * 6)
                for t in range(TB):
                    pe.transpose(ps_t[:, t // 4, (t % 4) * P:(t % 4 + 1) * P], f[:, t].rearrange("p h d -> p (h d)"),
                                 w["ident"][:, :]).then_inc(turned, 1)
                wait(pe, bias_added, b * 2)
                for t in range(TB):
                    if t % 4 == 0:
                        pe.wait_ge(turned_read, b * 6 + (1 + t // 4))
                    pe.matmul(ps_y[:, t // 4, (t % 4) * P:(t % 4 + 1) * P], turned_sb[:, 0, t * P:(t + 1) * P],
                              w["wt"][:, 3, :], start=True, stop=True).then_inc(y_ready, 1)

            def gate(b):
                for t in range(TB):
                    pe.wait_ge(z_ready, b * TB + (t + 1))
                    pe.transpose(ps_t[:, t // 4, (t % 4) * P:(t % 4 + 1) * P], z[:, t, :], w["ident"][:, :])\
                      .then_inc(turned, 1)
                pe.wait_ge(y_biased, b * 2 + 2)
                for t in range(TB):
                    if t % 4 == 0:
                        pe.wait_ge(turned_read, b * 6 + (3 + t // 4))
                    pe.matmul(ps_y[:, 0, t * E:(t + 1) * E], turned_sb[:, 1, t * P:(t + 1) * P], w["gate"][:, :],
                              start=True, stop=True).then_inc(gate_ready, 1)

            def experts(pair):
                def part(b):
                    for half in range(2):
                        wait(pe, e_step, b * TB * E + max(0, 2 * E * (pair - 1) + E * (half + 1)))
                        for t in (2 * pair, 2 * pair + 1):
                            pe.matmul(ps_e[:, t % 2, half, :], turned_sb[:, 1, t * P:(t + 1) * P],
                                      w["experts"][:, 4 * half:4 * half + 4, :], start=True, stop=True).then_inc(e_ready, 1)
                return part

            def biases(b):
                pe.wait_ge(gate_step, b * GATE + GATE)
                for t in range(TB):
                    pe.transpose(ps_t[0:E, t // 4, (t % 4) * P:(t % 4 + 1) * P], weight[:, t, :], w["ident"][:, :])\
                      .then_inc(turned, 1)
                for t in range(TB):
                    if t % 4 == 0:
                        pe.wait_ge(turned_read, b * 6 + (5 + t // 4))
                    pe.matmul(ps_y[:, t // 4, (t % 4) * P:(t % 4 + 1) * P], weight_t[:, t * P:(t + 1) * P],
                              w["expert_b"][:, :], start=True, stop=True).then_inc(bias_ready, 1)

            rounds(pe, [(0, experts(0)), (0, biases), (0, experts(1)), (1, project), (0, experts(2)),
                        (0, experts(3)), (1, gate)])

        @block.gpsimd
        def _(pool):
            def each(rows):
                return rows[:, :].unsqueeze(1).to_broadcast([P, TB, D])

            with pool.Fori(0, B) as b:
                xs = w["x"][:, bass.ds(b * TB, TB), :]
                pool.wait_ge(x_ready, b)
                alone(pool, w["pool_passed"])
                pool.tensor_tensor(xs, xs, each(w["ln_b"]), ALU.add).then_inc(x_step, 1)
                pool.wait_ge(yn_ready, b * TB + TB)
                alone(pool, w["pool_passed"])
                pool.wait_ge(x_step, b * 2 + 1)
                pool.tensor_tensor(yn[:, :, :], yn[:, :, :], each(w["ln_w"]), ALU.mult).then_inc(x_step, 1)
                pool.wait_ge(x_step, b * 2 + 2)
                alone(pool, w["pool_passed"])
                pool.tensor_tensor(xs, xs, yn[:, :, :], ALU.add).then_inc(x_ready, 1)

        @block.vector
        def _(dve):
            def project(b):
                wait(dve, yn_ready, b * TB)
                for g in range(2):
                    dve.wait_ge(y_ready, b * TB + 4 * (g + 1))
                    dve.tensor_tensor(y[:, 4 * g:4 * g + 4, :], ps_y[:, g, :].rearrange("p (t d) -> p t d", t=4),
                                      four(w["bo"]), ALU.add).then_inc(y_biased, 1)
                dve.wait_ge(y_biased, b * 2 + 2)
                take_stats(dve, lambda t: y[:, t, :], stats[:, 0], mv[:, 0], stats_ready[0], mv_ready[0], b * TB,
                           w["dve_passed"])
                dve.wait_ge(mv_ready[0], b * TB + TB)
                dve.wait_ge(rstd_ready[0], b + 1)
                wait(dve, x_ready, b)
                for t in range(TB):
                    dve.tensor_scalar(yn[:, t, :], y[:, t, :], mv[:, 0, t, 0:1], rstd[:, 0, t:t + 1],
                                      ALU.subtract, ALU.mult).then_inc(yn_ready, 1)

            def normalise(b):
                dve.wait_ge(x_ready, b + 1)
                alone(dve, w["dve_passed"])
                take_stats(dve, lambda t: xt(b, t), stats[:, 1], mv[:, 1], stats_ready[1], mv_ready[1], b * TB,
                           w["dve_passed"])
                dve.wait_ge(mv_ready[1], b * TB + TB)
                dve.wait_ge(rstd_ready[1], b + 1)
                for t in range(TB):
                    dve.tensor_scalar(z[:, t, :], xt(b, t), mv[:, 1, t, 0:1], rstd[:, 1, t:t + 1],
                                      ALU.subtract, ALU.mult).then_inc(z_ready, 1)

            def gate(b):
                step = [0]

                def then(ins):
                    ins.then_inc(gate_step, 1)
                    step[0] += 1
                    dve.wait_ge(gate_step, b * GATE + step[0])

                def each(v):
                    return v.unsqueeze(2).to_broadcast([P, TB, E])

                dve.wait_ge(gate_ready, b * TB + TB)
                then(dve.tensor_tensor(lg[:, :, :], ps_y[:, 0, 0:TB * E].rearrange("p (t e) -> p t e", t=TB),
                                       w["gate_b"][:, :].unsqueeze(1).to_broadcast([P, TB, E]), ALU.add))
                then(dve.tensor_reduce(top[:, :], lg[:, :, :], AX.X, ALU.max))
                then(dve.tensor_tensor(lg[:, :, :], lg[:, :, :], each(top[:, :]), ALU.subtract))
                dve.wait_ge(exp_ready, b + 1)
                then(dve.tensor_reduce(total[:, 0, :], prob[:, :, :], AX.X, ALU.add))
                then(dve.reciprocal(inv[:, 0, :], total[:, 0, :]))
                then(dve.tensor_tensor(prob[:, :, :], prob[:, :, :], each(inv[:, 0, :]), ALU.mult))
                then(dve.scalar_tensor_tensor(out=kept[:, :, :], in0=prob[:, :, :], scalar=THRESHOLD, in1=prob[:, :, :],
                                              op0=ALU.is_ge, op1=ALU.mult))
                then(dve.tensor_reduce(total[:, 1, :], kept[:, :, :], AX.X, ALU.add))
                then(dve.scalar_tensor_tensor(out=guard[:, :], in0=total[:, 1, :], scalar=0.0, in1=total[:, 1, :],
                                              op0=ALU.is_equal, op1=ALU.add))
                then(dve.reciprocal(inv[:, 1, :], guard[:, :]))
                then(dve.tensor_tensor(weight[:, :, :], kept[:, :, :], each(inv[:, 1, :]), ALU.mult))
                assert step[0] == GATE

            def experts(pair):
                def part(b):
                    done = 2 * E * pair
                    if pair == 1:
                        dve.wait_ge(bias_added, b * 2 + 2)
                    for e in range(E):
                        for t in (2 * pair, 2 * pair + 1):
                            if e > 0:
                                dve.wait_ge(e_step, b * TB * E + (done - 1))
                            if e % 4 == 0:
                                dve.wait_ge(e_ready, b * 2 * TB + (4 * pair + 2 * (e // 4) + t % 2 + 1))
                            dve.scalar_tensor_tensor(out=xt(b, t), in0=ps_e[:, t % 2, e // 4, (e % 4) * D:(e % 4 + 1) * D],
                                                     scalar=weight[:, t, e:e + 1], in1=xt(b, t),
                                                     op0=ALU.mult, op1=ALU.add).then_inc(e_step, 1)
                            done += 1
                return part

            def biases(b):
                dve.wait_ge(e_step, b * TB * E + 2 * E)
                for g in range(2):
                    dve.wait_ge(bias_ready, b * TB + 4 * (g + 1))
                    xs = w["x"][:, bass.ds(b * TB + 4 * g, 4), :]
                    dve.tensor_tensor(xs, xs, ps_y[:, g, :].rearrange("p (t d) -> p t d", t=4), ALU.add)\
                       .then_inc(bias_added, 1)

            rounds(dve, [(0, experts(0)), (0, biases), (0, experts(1)), (1, project), (0, experts(2)),
                         (1, normalise), (0, experts(3)), (1, gate)])


def attend_causal(nc, w):
    with ExitStack() as ctx:
        def sb(name, shape, dt=F32):
            return ctx.enter_context(nc.sbuf_tensor(name, shape, dt))

        def ps(name, shape, dt=F32):
            return ctx.enter_context(nc.psum_tensor(name, shape, dt))

        def sem(name):
            return ctx.enter_context(nc.semaphore(name))

        stats, mv = sb("stats_c", [P, TB, 6]), sb("mv_c", [P, TB, 2])
        lnv, rstd = sb("lnv_c", [P, TB]), sb("rstd_c", [P, TB])
        z = sb("z_c", [P, TB, D])
        zt = sb("z_turned", [P, N])
        qk = sb("qk_c", [DA, 2, N])
        v = sb("v_c", [P, TB, DA])
        top, shift = sb("top_c", [P, TB]), sb("shift_c", [P, TB])
        prob = sb("prob_c", [P, 2, N])
        total, inv = sb("total_c", [P, TB]), sb("inverse_c", [P, TB])
        prob_t = sb("prob_t", [P, 2, N])
        mixed = sb("mixed", [P, 2, DA])
        mixed_t = sb("mixed_t", [DA, 2, P])
        ps_s = ps("ps_cs", [P, 2, 2, HALF])
        ps_t = ps("ps_ct", [P, 2, HALF])
        ps_o = ps("ps_co", [P, HALF])
        ps_x = ps("ps_cx", [P, HALF])

        stats_ready, mv_ready, ln_ready, rstd_ready = sem("c_stats"), sem("c_mv"), sem("c_ln"), sem("c_rstd")
        z_ready, turned, zt_ready = sem("c_z"), sem("c_turned"), sem("c_zt")
        proj_ready, qk_ready, v_ready, v_done = sem("c_proj"), sem("c_qk"), sem("c_v"), sem("c_v_done")
        s_ready, masked, max_step = sem("c_scores"), sem("c_masked"), sem("c_max")
        exp_ready, p_turned, p_copied = sem("c_exp"), sem("c_p_turned"), sem("c_p_copied")
        o_ready, inv_ready, mixed_ready = sem("c_out"), sem("c_inverse"), sem("c_mixed")
        m_turned, m_copied, add_ready, x_done = sem("c_m_turned"), sem("c_m_copied"), sem("c_add"), sem("c_x_done")
        x_biased = sem("c_x_biased")
        EARLY = 6
        block = ctx.enter_context(nc.Block())

        def xt(b, t):
            return w["x"][:, bass.ds(b * TB + t, 1), :].rearrange("p o d -> p (o d)")

        @block.vector
        def _(dve):
            def normalise(b):
                take_stats(dve, lambda t: xt(b, t), stats, mv, stats_ready, mv_ready, b * TB, w["dve_passed"])
                dve.wait_ge(mv_ready, b * TB + TB)
                dve.wait_ge(rstd_ready, b + 1)
                wait(dve, turned, b * TB)
                for t in range(TB):
                    dve.tensor_scalar(z[:, t, :], xt(b, t), mv[:, t, 0:1], rstd[:, t:t + 1],
                                      ALU.subtract, ALU.mult).then_inc(z_ready, 1)

            def weigh(b, i):
                dve.wait_ge(exp_ready, b * TB + (i + 1))
                dve.reciprocal(inv[:, i:i + 1], total[:, i:i + 1]).then_inc(inv_ready, 1)
                dve.wait_ge(inv_ready, b * TB + (i + 1))
                dve.wait_ge(o_ready, b * TB + (i + 1))
                dve.tensor_scalar(mixed[:, i % 2, :], ps_o[:, 0:DA], inv[:, i:i + 1], None, ALU.mult)\
                   .then_inc(mixed_ready, 1)

            def add(b, i):
                dve.wait_ge(x_biased, b * 2 + (1 if i < 4 else 2))
                dve.wait_ge(add_ready, b * TB + (i + 1))
                dve.tensor_tensor(xt(b, i), xt(b, i), ps_x[:, 0:D], ALU.add).then_inc(x_done, 1)

            def turned_half(b, i, g):
                n = min(4, i + 1 - 4 * g)
                dve.wait_ge(p_turned, b * 12 + (sum(1 + (k >= 4) for k in range(i)) + (g + 1)))
                dve.tensor_copy(prob_t[:, i % 2, g * HALF:g * HALF + n * P], ps_t[:, g, 0:n * P]).then_inc(p_copied, 1)

            def steps(b, tiles):
                for i in tiles:
                    dve.wait_ge(s_ready, b * TB + (i + 1))
                    diagonal = ps_s[:, i % 2, i // 4, (i % 4) * P:(i % 4 + 1) * P]
                    dve.tensor_tensor(diagonal, diagonal, w["causal"][:, :], ALU.add).then_inc(masked, 1)
                    dve.wait_ge(masked, b * TB + (i + 1))
                    dve.tensor_reduce(top[:, i:i + 1],
                                      ps_s[:, i % 2, :, :].rearrange("p f k -> p (f k)")[:, 0:(i + 1) * P],
                                      AX.X, ALU.max).then_inc(max_step, 1)
                    dve.wait_ge(max_step, b * 2 * TB + (2 * i + 1))
                    dve.tensor_scalar(shift[:, i:i + 1], top[:, i:i + 1], -float(DA) ** -0.5, None, ALU.mult)\
                       .then_inc(max_step, 1)
                    if i >= 1:
                        for g in range(1 + (i - 1) // 4):
                            turned_half(b, i - 1, g)
                    if i >= 2:
                        weigh(b, i - 2)
                    if i >= 3:
                        add(b, i - 3)

            def begin(b):
                dve.wait_ge(v_ready, b * TB + TB)
                dve.tensor_tensor(v[:, :, :], ps_x[:, :].rearrange("p (t d) -> p t d", t=TB),
                                  w["bv1"][:, :].unsqueeze(1).to_broadcast([P, TB, DA]), ALU.add).then_inc(v_done, 1)
                steps(b, range(EARLY))

            def end(b):
                steps(b, range(EARLY, TB))
                for g in range(2):
                    turned_half(b, TB - 1, g)
                for i in (TB - 2, TB - 1):
                    weigh(b, i)
                    add(b, i - 1)
                add(b, TB - 1)
                dve.wait_ge(x_done, b * TB + TB)

            rounds(dve, [(0, begin), (1, normalise), (0, end)])

        @block.scalar
        def _(act):
            def mixed_half(b, i):
                act.wait_ge(m_turned, b * TB + (i + 1))
                act.activation(mixed_t[:, i % 2, :], ps_x[0:DA, P:2 * P], ACT.Copy).then_inc(m_copied, 1)

            def steps(b, tiles):
                for i in tiles:
                    act.wait_ge(max_step, b * 2 * TB + (2 * i + 2))
                    act.activation(prob[:, i % 2, 0:(i + 1) * P],
                                   ps_s[:, i % 2, :, :].rearrange("p f k -> p (f k)")[:, 0:(i + 1) * P], ACT.Exp,
                                   bias=shift[:, i:i + 1], scale=float(DA) ** -0.5, accum_out=total[:, i:i + 1])\
                       .then_inc(exp_ready, 1)
                    if i >= 2:
                        mixed_half(b, i - 2)

            def take_qk(b, g):
                for s in range(2):
                    act.wait_ge(proj_ready, b * 4 + (2 * g + s + 1))
                    act.activation(qk[:, s, g * HALF:(g + 1) * HALF], ps_s[0:DA, s, g, :], ACT.Identity,
                                   bias=w["b1"][:, s:s + 1]).then_inc(qk_ready, 1)

            def begin(b):
                for g in range(2):
                    act.wait_ge(turned, b * TB + 4 * (g + 1))
                    act.activation(zt[:, g * HALF:(g + 1) * HALF], ps_t[:, g, :], ACT.Copy).then_inc(zt_ready, 1)
                take_qk(b, 0)
                steps(b, range(1))
                take_qk(b, 1)
                steps(b, range(1, EARLY))

            def rstd_of(b):
                take_rstd(act, w, mv, lnv, rstd, mv_ready, ln_ready, rstd_ready, b)

            def end(b):
                steps(b, range(EARLY, TB))
                mixed_half(b, TB - 2)
                mixed_half(b, TB - 1)

            act.preload_act_table_set("natural_log_exp_and_others")
            rounds(act, [(0, begin), (1, rstd_of), (0, end)])

        @block.gpsimd
        def _(pool):
            with pool.Fori(0, B) as b:
                pool.wait_ge(z_ready, b * TB + TB)
                for g in range(2):
                    xs = w["x"][:, bass.ds(b * TB + 4 * g, 4), :]
                    pool.tensor_tensor(xs, xs, four(w["bo1"]), ALU.add).then_inc(x_biased, 1)

        @block.tensor
        def _(pe):
            with pe.Fori(0, B) as b:
                for t in range(TB):
                    pe.wait_ge(z_ready, b * TB + (t + 1))
                    if t == 0:
                        pe.wait_ge(p_copied, b * 12)
                    pe.transpose(ps_t[:, t // 4, (t % 4) * P:(t % 4 + 1) * P], z[:, t, :], w["ident"][:, :])\
                      .then_inc(turned, 1)

                def project_qk(g):
                    pe.wait_ge(zt_ready, b * 2 + (g + 1))
                    for s in range(2):
                        pe.matmul(ps_s[0:DA, s, g, :], w["qkv1"][:, s, :], zt[:, g * HALF:(g + 1) * HALF],
                                  start=True, stop=True).then_inc(proj_ready, 1)

                pe.wait_ge(exp_ready, b * TB)
                project_qk(0)
                pe.wait_ge(zt_ready, b * 2 + 2)
                pe.wait_ge(x_done, b * TB)
                for t in range(TB):
                    pe.matmul(ps_x[:, t * DA:(t + 1) * DA], zt[:, t * P:(t + 1) * P], w["qkv1"][:, 2, :],
                              start=True, stop=True).then_inc(v_ready, 1)

                def scores(i):
                    if i == 0:
                        pe.wait_ge(qk_ready, b * 4 + 2)
                    else:
                        if i == 4:
                            pe.wait_ge(qk_ready, b * 4 + 4)
                        pe.wait_ge(exp_ready, b * TB + (i - 1))
                    for g in range(1 + i // 4):
                        n = min(4, i + 1 - 4 * g) * P
                        mm = pe.matmul(ps_s[:, i % 2, g, 0:n], qk[:, 0, i * P:(i + 1) * P],
                                       qk[:, 1, g * HALF:g * HALF + n], start=True, stop=True)
                    mm.then_inc(s_ready, 1)

                def turn_weights(i):
                    pe.wait_ge(exp_ready, b * TB + (i + 1))
                    for g in range(1 + i // 4):
                        pe.wait_ge(p_copied, b * 12 + sum(1 + (k >= 4) for k in range(i)))
                        for k in range(4 * g, min(4 * g + 4, i + 1)):
                            mm = pe.transpose(ps_t[:, g, (k % 4) * P:(k % 4 + 1) * P], prob[:, i % 2, k * P:(k + 1) * P],
                                              w["ident"][:, :])
                        mm.then_inc(p_turned, 1)

                def weigh(i):
                    pe.wait_ge(p_copied, b * 12 + sum(1 + (k >= 4) for k in range(i + 1)))
                    if i == 0:
                        pe.wait_ge(v_done, b + 1)
                    pe.wait_ge(mixed_ready, b * TB + i)
                    for k in range(i + 1):
                        mm = pe.matmul(ps_o[:, 0:DA], prob_t[:, i % 2, k * P:(k + 1) * P], v[:, k, :],
                                       start=(k == 0), stop=(k == i))
                    mm.then_inc(o_ready, 1)

                def turn_mixed(i):
                    pe.wait_ge(mixed_ready, b * TB + (i + 1))
                    pe.wait_ge(x_done, b * TB + i)
                    alone(pe, w["pe_passed"])
                    pe.transpose(ps_x[0:DA, P:2 * P], mixed[:, i % 2, :], w["ident"][:, :]).then_inc(m_turned, 1)

                def project(i):
                    pe.wait_ge(m_copied, b * TB + (i + 1))
                    pe.matmul(ps_x[:, 0:D], mixed_t[:, i % 2, :], w["wo1"][:, :], start=True, stop=True)\
                      .then_inc(add_ready, 1)

                scores(0)
                project_qk(1)
                for i in range(TB):
                    if i + 1 < TB:
                        scores(i + 1)
                    turn_weights(i)
                    if i >= 2:
                        turn_mixed(i - 2)
                    if i >= 1:
                        weigh(i - 1)
                    if i >= 2:
                        project(i - 2)
                turn_mixed(TB - 2)
                weigh(TB - 1)
                project(TB - 2)
                turn_mixed(TB - 1)
                project(TB - 1)


def descend_tree(nc, w, out):
    with ExitStack() as ctx:
        def sb(name, shape, dt=F32):
            return ctx.enter_context(nc.sbuf_tensor(name, shape, dt))

        def ps(name, shape, dt=F32):
            return ctx.enter_context(nc.psum_tensor(name, shape, dt))

        def sem(name):
            return ctx.enter_context(nc.semaphore(name))

        stats, mv = sb("stats_d", [P, TB, 6]), sb("mv_d", [P, TB, 2])
        lnv, rstd = sb("lnv_d", [P, TB]), sb("rstd_d", [P, TB])
        z = sb("z_d", [P, TB, D])
        zt = sb("zt_d", [P, N])
        right = sb("right", [P, B, TB, LEAVES])
        reach = [sb(f"reach{i}", [P, TB, LEAVES]) for i in range(2)]
        reach_t = sb("reach_t", [P, TB, 2, P])
        ps_t = ps("ps_dt", [P, 2, HALF])
        ps_g = ps("ps_dg", [P, 2, HALF])
        ps_l = ps("ps_dl", [P, 2, HALF])
        ps_x = ps("ps_dx", [P, 2, HALF])
        stats_ready, mv_ready, ln_ready, rstd_ready = sem("d_stats"), sem("d_mv"), sem("d_ln"), sem("d_rstd")
        z_ready, turned, zt_ready = sem("d_z"), sem("d_turned"), sem("d_zt")
        logit_ready, right_ready, level = sem("d_logit"), sem("d_right"), sem("d_level")
        leaf_turned, leaf_copied = sem("d_leaf_turned"), sem("d_leaf_copied")
        add_ready, x_biased, x_done, stored = sem("d_add"), sem("d_x_biased"), sem("d_x_done"), sem("d_stored")
        block = ctx.enter_context(nc.Block())

        def xt(b, t):
            return w["x"][:, bass.ds(b * TB + t, 1), :].rearrange("p o d -> p (o d)")

        LEVELS = 2 * DEPTH

        @block.vector
        def _(dve):
            def normalise(b):
                take_stats(dve, lambda t: xt(b, t), stats, mv, stats_ready, mv_ready, b * TB, w["dve_passed"])
                dve.wait_ge(mv_ready, b * TB + TB)
                dve.wait_ge(rstd_ready, b + 1)
                wait(dve, turned, b * TB)
                for t in range(TB):
                    dve.tensor_scalar(z[:, t, :], xt(b, t), mv[:, t, 0:1], rstd[:, t:t + 1],
                                      ALU.subtract, ALU.mult).then_inc(z_ready, 1)

            def descend(b):
                dve.wait_ge(right_ready, b * 4 + 4)
                wait(dve, leaf_turned, b * 4)
                for d in range(DEPTH):
                    n = 2 ** d
                    new = reach[d % 2][:, :, 0:2 * n].rearrange("p t (n s) -> p t n s", s=2)
                    g = right[:, bass.ds(b, 1), :, n - 1:2 * n - 1].rearrange("p o t n -> p (o t) n")
                    if d == 0:
                        dve.tensor_copy(new[:, :, :, 1], g).then_inc(level, 1)
                        dve.tensor_scalar(new[:, :, :, 0], g, -1.0, 1.0, ALU.mult, ALU.add).then_inc(level, 1)
                    else:
                        old = reach[(d - 1) % 2][:, :, 0:n]
                        dve.wait_ge(level, b * LEVELS + 2 * d)
                        dve.tensor_tensor(new[:, :, :, 1], old, g, ALU.mult).then_inc(level, 1)
                        dve.wait_ge(level, b * LEVELS + (2 * d + 1))
                        dve.tensor_tensor(new[:, :, :, 0], old, new[:, :, :, 1], ALU.subtract).then_inc(level, 1)

            def add(b):
                for g in range(2):
                    dve.wait_ge(x_biased, b * 2 + (g + 1))
                    dve.wait_ge(add_ready, b * TB + 4 * (g + 1))
                    xs = w["x"][:, bass.ds(b * TB + 4 * g, 4), :]
                    dve.tensor_tensor(xs, xs, ps_x[:, g, :].rearrange("p (t d) -> p t d", t=4), ALU.add)\
                       .then_inc(x_done, 1)

            rounds(dve, [(1, normalise), (0, descend), (-1, add)])

        @block.scalar
        def _(act):
            def branch(b):
                take_rstd(act, w, mv, lnv, rstd, mv_ready, ln_ready, rstd_ready, b)
                for g in range(2):
                    act.wait_ge(turned, b * TB + 4 * (g + 1))
                    act.activation(zt[:, g * HALF:(g + 1) * HALF], ps_t[:, g, :], ACT.Copy).then_inc(zt_ready, 1)
                for g in range(4):
                    act.wait_ge(logit_ready, b * TB + 2 * (g + 1))
                    alone(act, w["act_passed"])
                    act.activation(right[:, bass.ds(b, 1), 2 * g:2 * g + 2, 0:NODES].rearrange("p o t n -> p (o t) n"),
                                   ps_g[:, g % 2, :].rearrange("p (t n) -> p t n", t=2)[:, :, 0:NODES], ACT.Sigmoid)\
                       .then_inc(right_ready, 1)

            def take_leaves(b):
                for g in range(4):
                    act.wait_ge(leaf_turned, b * 4 + (g + 1))
                    act.activation(reach_t[:, 2 * g:2 * g + 2, :, :].rearrange("p t i d -> p (t i d)"),
                                   ps_l[:, g % 2, :], ACT.Copy).then_inc(leaf_copied, 1)

            rounds(act, [(1, branch), (0, take_leaves)])

        @block.gpsimd
        def _(pool):
            with pool.Fori(0, B) as b:
                pool.wait_ge(z_ready, b * TB + TB)
                for g in range(2):
                    xs = w["x"][:, bass.ds(b * TB + 4 * g, 4), :]
                    pool.tensor_tensor(xs, xs, four(w["bout"]), ALU.add).then_inc(x_biased, 1)

        @block.tensor
        def _(pe):
            def logits(b):
                wait(pe, zt_ready, b * 2)
                for t in range(TB):
                    pe.wait_ge(z_ready, b * TB + (t + 1))
                    pe.transpose(ps_t[:, t // 4, (t % 4) * P:(t % 4 + 1) * P], z[:, t, :], w["ident"][:, :])\
                      .then_inc(turned, 1)
                for t in range(TB):
                    if t % 4 == 0:
                        pe.wait_ge(zt_ready, b * 2 + (1 + t // 4))
                    if t % 2 == 0:
                        wait(pe, right_ready, b * 4 + max(t // 2 - 1, 0))
                    at = (t % 2) * LEAVES
                    pe.matmul(ps_g[:, t // 2 % 2, at:at + NODES], zt[:, t * P:(t + 1) * P], w["router"][:, :],
                              start=True, stop=True).then_inc(logit_ready, 1)

            def leaves(b):
                pe.wait_ge(level, b * LEVELS + LEVELS)
                last = reach[(DEPTH - 1) % 2]
                for g in range(4):
                    wait(pe, leaf_copied, b * 4 + max(g - 1, 0))
                    for t in range(2 * g, 2 * g + 2):
                        for i in range(2):
                            at = (t % 2) * LEAVES + i * P
                            mm = pe.transpose(ps_l[:, g % 2, at:at + P], last[:, t, i * P:(i + 1) * P], w["ident"][:, :])
                    mm.then_inc(leaf_turned, 1)
                wait(pe, x_done, b * 2)
                for t in range(TB):
                    pe.wait_ge(leaf_copied, b * 4 + (t // 2 + 1))
                    for i in range(2):
                        mm = pe.matmul(ps_x[:, t // 4, (t % 4) * P:(t % 4 + 1) * P], reach_t[:, t, i, :],
                                       w["leaf"][:, i, :], start=(i == 0), stop=(i == 1))
                    mm.then_inc(add_ready, 1)

            rounds(pe, [(1, logits), (0, leaves)])

        @block.sync
        def _(sp):
            with sp.Fori(0, B) as b:
                sp.wait_ge(x_done, b * 2 + 2)
                sp.dma_start(out[bass.ds(b, 1)].rearrange("o (t p) d -> p (o t) d", p=P),
                             w["x"][:, bass.ds(b * TB, TB), :]).then_inc(stored, 16)
            sp.wait_ge(stored, 16 * B)


_INS = ["L0_attn_x"] + [f"L0_attn_{n}" for n in ("Wq", "bq", "Wk", "bk", "Wv", "bv", "Wo", "bo", "beta", "t", "ln_w", "ln_b")]\
    + [f"L0_ffn_{n}" for n in ("gate_w", "gate_b", "expert_w", "expert_b")]\
    + [f"L1_attn_{n}" for n in ("wq", "bq", "wk", "bk", "wv", "bv", "wo", "bo")]\
    + [f"L1_ffn_{n}" for n in ("Wq", "routers", "leaf_keys", "leaf_values", "Wout_w", "Wout_b")]


def kernel(**inputs):
    import numpy as np
    import concourse.bacc as bacc
    from concourse.bass_utils import run_bass_kernel_spmd

    nc = bacc.Bacc("TRN2", target_bir_lowering=False, num_devices=1)
    arrays, drams = {}, {}
    for name in _INS:
        x = np.ascontiguousarray(inputs[name])
        arrays[f"in_{name}"] = x
        drams[name] = nc.dram_tensor(f"in_{name}", x.shape, mybir.dt.from_np(x.dtype), kind="ExternalInput").ap()
    out = nc.dram_tensor("out", (B, N, D), F32, kind="ExternalOutput").ap()
    build(nc, drams, out)
    result = run_bass_kernel_spmd(nc, [arrays], core_ids=[0])
    return result.results[0]["out"]
```
